# Optimizing a Trainium2 kernel written in Bass

```python
import numpy as np
import jax
import jax.numpy as jnp

def _softmax(x, axis=-1):
    return jax.nn.softmax(x, axis=axis)

def _gelu(x):
    return jax.nn.gelu(x, approximate=True)

def _silu(x):
    return jax.nn.silu(x)

def _sigmoid(x):
    return jax.nn.sigmoid(x)

def _layernorm(x, axis=-1, eps=1e-05):
    m = jnp.mean(x, axis=axis, keepdims=True)
    v = jnp.var(x, axis=axis, keepdims=True)
    return (x - m) / jnp.sqrt(v + eps)

def _scatter_add(tgt, idx, src, axis=0):
    return tgt.at[idx].add(src)

def _segment_sum(src, seg, n):
    return jax.ops.segment_sum(src, seg, n)
kernel_name = 'mk_flamingo_gated_d1_seqx_r4_473252'

def setup_inputs(seed: int=0):
    np.random.seed(seed)
    _w = jnp.asarray

    def _rec_inputs():
        import jax
        import jax.numpy as jnp
        _rk = jax.random.key(seed)
        x = -0.0002928 + 1 * jax.random.normal(jax.random.fold_in(_rk, 1), (32, 128, 256), jnp.float32)
        _lenS = 128 - jax.random.randint(jax.random.fold_in(_rk, 7), (32,), 0, max(1, 128 // 4) + 1, jnp.int32)
        _lenS2 = 128 - jax.random.randint(jax.random.fold_in(_rk, 8), (32,), 0, max(1, 128 // 4) + 1, jnp.int32)
        _ctx_1024P = jax.random.normal(jax.random.fold_in(_rk, 11), (32, 16, 256), jnp.float32)
        _ctx_1024c = jax.random.dirichlet(jax.random.fold_in(_rk, 511), 0.3 * jnp.ones((16,), jnp.float32), (32, 128))
        _ctx_1024t = jnp.einsum('bsk,bkd->bsd', _ctx_1024c, _ctx_1024P)
        _ctx_1024t = _ctx_1024t * jax.lax.rsqrt(jnp.mean(jnp.square(_ctx_1024t)) + 1e-12) * 0.953939
        ctx_1024 = -1.39393e-06 + 0.999914 * (_ctx_1024t + 0.3 * jax.random.normal(jax.random.fold_in(_rk, 611), (32, 128, 256), jnp.float32))
        fside_1x16xSxS2_0 = 7.48737e-06 + 1.00011 * jax.random.normal(jax.random.fold_in(_rk, 13), (1, 16, 128, 128), jnp.float32)
        _validS = jnp.arange(128)[None, :] < _lenS[:, None]
        _validS2 = jnp.arange(128)[None, :] < _lenS2[:, None]
        _causal = jnp.tril(jnp.ones((128, 128), dtype=bool))
        mask_BxS2_bk0 = jnp.logical_not(jnp.broadcast_to(_validS2[:, :], (32, 128)))
        _g = jax.random.normal(jax.random.fold_in(_rk, 9001), (2, 1), jnp.float32)
        _g = jnp.sign(_g) * jnp.maximum(jnp.abs(_g), 1.0) + (_g == 0) * 1.0
        g_xattn = _g[0]
        g_ffn = _g[1]
        return (x, ctx_1024, fside_1x16xSxS2_0, mask_BxS2_bk0, g_xattn, g_ffn)
    x, ctx_1024, fside_1x16xSxS2_0, mask_BxS2_bk0, g_xattn, g_ffn = _rec_inputs()

    def _L0_xattn_setup():
        import jax, jax.numpy as jnp
        import numpy as np
        B, S, H, NH = (2, 512, 256, 16)
        HD = H // NH

        def _shape(x):
            b, s, _ = x.shape
            return x.reshape(b, s, NH, HD).transpose(0, 2, 1, 3)
        key = jax.random.key(seed)
        ks = jax.random.split(key, 12)
        query = jax.random.normal(ks[0], (B, S, H), dtype=jnp.float32)
        key_t = jax.random.normal(ks[1], (B, S, H), dtype=jnp.float32)
        value = jax.random.normal(ks[2], (B, S, H), dtype=jnp.float32)
        kpm = jax.random.randint(ks[3], (B, S), 0, 2).astype(bool)
        kpm = kpm.at[:, 0].set(False)
        bias = jax.random.normal(ks[4], (1, NH, S, S), dtype=jnp.float32)
        init = 0.02
        q_w = jax.random.normal(ks[5], (H, H), dtype=jnp.float32) * init
        k_w = jax.random.normal(ks[6], (H, H), dtype=jnp.float32) * init
        v_w = jax.random.normal(ks[7], (H, H), dtype=jnp.float32) * init
        o_w = jax.random.normal(ks[8], (H, H), dtype=jnp.float32) * init
        q_b = jnp.zeros((H,), jnp.float32)
        k_b = jnp.zeros((H,), jnp.float32)
        v_b = jnp.zeros((H,), jnp.float32)
        o_b = jnp.zeros((H,), jnp.float32)
        return {'query': query, 'key': key_t, 'value': value, 'key_padding_mask': kpm, 'bias': bias, 'q_w': q_w, 'q_b': q_b, 'k_w': k_w, 'k_b': k_b, 'v_w': v_w, 'v_b': v_b, 'o_w': o_w, 'o_b': o_b}
    _L0_xattn_all = _L0_xattn_setup()
    _L0_xattn_in = {k: v for k, v in _L0_xattn_all.items() if k in ('q_w', 'q_b', 'k_w', 'k_b', 'v_w', 'v_b', 'o_w', 'o_b')}
    del _L0_xattn_all

    def _L0_ffn_setup():
        import jax, jax.numpy as jnp
        import numpy as np
        B, S, DIM = (2, 512, 256)
        HID = 512
        E, NSH, TOPK = (8, 2, 2)

        def _ffn(x, w1, w2, w3):
            return jax.nn.silu(x @ w1.T) * (x @ w3.T) @ w2.T
        key = jax.random.key(seed)
        ks = jax.random.split(key, 8)
        sc = 0.02
        return {'x': jax.random.normal(ks[0], (B, S, DIM), jnp.float32), 'router_w': jax.random.normal(ks[1], (E, DIM), jnp.float32) * sc, 'expert_bias': jnp.zeros((E,), jnp.float32), 'w1': jax.random.normal(ks[2], (E, HID, DIM), jnp.float32) * sc, 'w3': jax.random.normal(ks[3], (E, HID, DIM), jnp.float32) * sc, 'w2': jax.random.normal(ks[4], (E, DIM, HID), jnp.float32) * sc, 'sw1': jax.random.normal(ks[5], (NSH, HID, DIM), jnp.float32) * sc, 'sw3': jax.random.normal(ks[6], (NSH, HID, DIM), jnp.float32) * sc, 'sw2': jax.random.normal(ks[7], (NSH, DIM, HID), jnp.float32) * sc}
    _L0_ffn_all = _L0_ffn_setup()
    _L0_ffn_in = {k: v for k, v in _L0_ffn_all.items() if k in ('router_w', 'expert_bias', 'w1', 'w3', 'w2', 'sw1', 'sw3', 'sw2')}
    del _L0_ffn_all
    return {'x': x, 'ctx_1024': ctx_1024, 'fside_1x16xSxS2_0': fside_1x16xSxS2_0, 'mask_BxS2_bk0': mask_BxS2_bk0, 'g_xattn': g_xattn, 'g_ffn': g_ffn, 'L0_xattn_q_w': _L0_xattn_in['q_w'], 'L0_xattn_q_b': _L0_xattn_in['q_b'], 'L0_xattn_k_w': _L0_xattn_in['k_w'], 'L0_xattn_k_b': _L0_xattn_in['k_b'], 'L0_xattn_v_w': _L0_xattn_in['v_w'], 'L0_xattn_v_b': _L0_xattn_in['v_b'], 'L0_xattn_o_w': _L0_xattn_in['o_w'], 'L0_xattn_o_b': _L0_xattn_in['o_b'], 'L0_ffn_router_w': _L0_ffn_in['router_w'], 'L0_ffn_expert_bias': _L0_ffn_in['expert_bias'], 'L0_ffn_w1': _L0_ffn_in['w1'], 'L0_ffn_w3': _L0_ffn_in['w3'], 'L0_ffn_w2': _L0_ffn_in['w2'], 'L0_ffn_sw1': _L0_ffn_in['sw1'], 'L0_ffn_sw3': _L0_ffn_in['sw3'], 'L0_ffn_sw2': _L0_ffn_in['sw2']}

def reference(x, ctx_1024, fside_1x16xSxS2_0, mask_BxS2_bk0, g_xattn, g_ffn, L0_xattn_q_w, L0_xattn_q_b, L0_xattn_k_w, L0_xattn_k_b, L0_xattn_v_w, L0_xattn_v_b, L0_xattn_o_w, L0_xattn_o_b, L0_ffn_router_w, L0_ffn_expert_bias, L0_ffn_w1, L0_ffn_w3, L0_ffn_w2, L0_ffn_sw1, L0_ffn_sw3, L0_ffn_sw2):
    import jax
    import jax.numpy as jnp

    def _L0_xattn_ref(query, key, value, key_padding_mask, bias, q_w, q_b, k_w, k_b, v_w, v_b, o_w, o_b):
        import jax, jax.numpy as jnp
        import numpy as np
        B, S, H, NH = (2, 512, 256, 16)
        HD = H // NH

        def _shape(x):
            b, s, _ = x.shape
            return x.reshape(b, s, NH, HD).transpose(0, 2, 1, 3)
        scale = HD ** (-0.5)
        q = _shape(query @ q_w.T + q_b)
        k = _shape(key @ k_w.T + k_b)
        v = _shape(value @ v_w.T + v_b)
        attn = jnp.einsum('bhqd,bhkd->bhqk', q, k) * scale + bias
        mask = key_padding_mask[:, None, None, :]
        attn = jnp.where(mask, -jnp.inf, attn)
        probs = jax.nn.softmax(attn, axis=-1)
        probs = jnp.where(mask, 0.0, probs)
        denom = jnp.maximum(probs.sum(axis=-1, keepdims=True), 1e-06)
        probs = probs / denom
        ctx = jnp.einsum('bhqk,bhkd->bhqd', probs, v)
        ctx = ctx.transpose(0, 2, 1, 3).reshape(query.shape[0], query.shape[1], H)
        return ctx @ o_w.T + o_b

    def _L0_ffn_ref(x, router_w, expert_bias, w1, w3, w2, sw1, sw3, sw2):
        import jax, jax.numpy as jnp
        import numpy as np
        B, S, DIM = (2, 512, 256)
        HID = 512
        E, NSH, TOPK = (8, 2, 2)

        def _ffn(x, w1, w2, w3):
            return jax.nn.silu(x @ w1.T) * (x @ w3.T) @ w2.T
        bs, sl, d = x.shape
        xf = x.reshape(-1, d)
        shared = jnp.zeros_like(xf)
        for i in range(sw1.shape[0]):
            shared = shared + _ffn(xf, sw1[i], sw2[i], sw3[i])
        logits = xf @ router_w.T + expert_bias
        rw, sel = jax.lax.top_k(logits, TOPK)
        rw = jax.nn.softmax(rw.astype(jnp.float32), axis=-1).astype(x.dtype)
        onehot = jax.nn.one_hot(sel, E, dtype=x.dtype)
        combine = jnp.einsum('tk,tke->te', rw, onehot)

        def body(acc, ew):
            e1, e3, e2, cw = ew
            acc = acc + cw[:, None] * _ffn(xf, e1, e2, e3)
            return (acc, None)
        out, _ = jax.lax.scan(body, jnp.zeros_like(xf), (w1, w3, w2, combine.T))
        out = out + shared
        return out.reshape(bs, sl, -1)
    x = x + jnp.tanh(g_xattn[0]) * _L0_xattn_ref(_layernorm(x, axis=-1), ctx_1024, ctx_1024, mask_BxS2_bk0, fside_1x16xSxS2_0, L0_xattn_q_w, L0_xattn_q_b, L0_xattn_k_w, L0_xattn_k_b, L0_xattn_v_w, L0_xattn_v_b, L0_xattn_o_w, L0_xattn_o_b)
    x = x + jnp.tanh(g_ffn[0]) * _L0_ffn_ref(_layernorm(x, axis=-1), L0_ffn_router_w, L0_ffn_expert_bias, L0_ffn_w1, L0_ffn_w3, L0_ffn_w2, L0_ffn_sw1, L0_ffn_sw3, L0_ffn_sw2)
    return x

_drawn_inputs = setup_inputs


def setup_inputs(seed=0):
    import zlib

    import numpy as np

    out = dict(_drawn_inputs(seed))
    spreads = {'L0_xattn_q_b': (0.0, 0.8),
     'L0_xattn_k_b': (0.0, 0.8),
     'L0_xattn_v_b': (0.0, 0.342),
     'L0_xattn_o_b': (0.0, 0.1),
     'L0_ffn_expert_bias': (0.0, 0.8)}
    factors = {'fside_1x16xSxS2_0': 7.041,
     'L0_xattn_q_w': 8.0,
     'L0_xattn_k_w': 8.0,
     'L0_ffn_router_w': 4.153,
     'L0_ffn_w1': 3.57,
     'L0_ffn_w3': 3.528,
     'L0_ffn_w2': 3.531}
    for name, (base, spread) in spreads.items():
        noise = np.random.default_rng([zlib.crc32(name.encode()), seed]).standard_normal(out[name].shape)
        drawn = base * np.exp(spread * noise) if base else spread * noise
        out[name] = jnp.asarray(drawn.astype(out[name].dtype))
    for name, factor in factors.items():
        out[name] = (out[name] * factor).astype(out[name].dtype)
    return out
```

```python
from contextlib import ExitStack

import concourse.bass as bass
from concourse import mybir

ALU = mybir.AluOpType
ACT = mybir.ActivationFunctionType
AX = mybir.AxisListType
F32 = mybir.dt.float32
F16 = mybir.dt.float16
BF16 = mybir.dt.bfloat16
I32 = mybir.dt.int32
U8 = mybir.dt.uint8

P = 128
B, S, D = 32, 128, 256
NH, HD = 16, 16
E, NSH, HID = 8, 2, 512
C = D // P
KC = HID // P
NPAIR = B // 2
QUAD = 4
NQ = NH // QUAD
SLOT_TILES = 72
HALF = B // 2
CHUNK = 1024
NCHUNK = 3 * (NSH + E)
PRE_CHUNKS = 0
ATT_CHUNKS = NPAIR
EPS = 1e-5
FRONT = 6
ZERO_ROWS = 8
ZERO_DMAS = SLOT_TILES // ZERO_ROWS
CONSTS = 9
PICK_STEP, EXP_STEP, RANK_STEP, ROUTE_STEPS = 14, 15, 43, 54
MASK_Q, MASK_K = 60000.0, -60000.0
MAX_CLAMP = 60000.0
ROW_MASK, ROW_MAX = 64, 96


def build(nc, x, ctxT, bias_q, bias_t, mask, maskT, g_att, g_ffn, attw, qkb, vb, ob,
          rw, eb, wall, out):
    es = ExitStack()
    with es:
        def sb(name, shape, dt):
            return es.enter_context(nc.sbuf_tensor(name, shape, dt))

        def sem(name):
            return es.enter_context(nc.semaphore(name))

        xs = sb("xs", [P, B, D], F32)
        stage = sb("stage", [P, 2, CHUNK], F32)
        ident = sb("ident", [P, P], F32)
        ident16 = sb("ident16", [P, P], F16)
        stats = sb("stats", [P, 2, 6], F32)
        mv = sb("mv", [P, 2, 2], F32)
        mean = sb("mean", [P, B], F32)
        rstd = sb("rstd", [P, B], F32)
        var_eps = sb("var_eps", [P, B], F32)
        std = sb("std", [P, B], F32)
        gates = sb("gates", [P, 2], F32)
        graw = sb("graw", [P, 2], F32)
        rw_f = sb("rw_f", [P, C, E], F32)
        rwh = sb("rwh", [P, C, E], F16)
        rwl = sb("rwl", [P, C, E], F16)
        ebr = sb("ebr", [P, E], F32)

        WBYTES = NCHUNK * CHUNK * 4
        ATT_AT = (PRE_CHUNKS + ATT_CHUNKS) * CHUNK * 4
        ARENA = 162 * 1024
        arena = sb("arena", [P, ARENA // 2], F16)
        cursor = [0]

        def carve(shape, dt, size):
            n = size
            for k in shape:
                n *= k
            a = arena[:, cursor[0] // 2:(cursor[0] + n) // 2]
            cursor[0] += -(-n // 32) * 32
            assert cursor[0] <= ARENA, cursor[0]
            if dt != F16:
                a = a.bitcast(dt)
            if len(shape) > 1:
                names = "abcd"[:len(shape)]
                a = a.rearrange(f"p ({' '.join(names)}) -> p {' '.join(names)}",
                                **{m: k for m, k in zip(names, shape)})
            return a

        wparts = arena[:, 0:WBYTES // 2]

        cursor[0] = ATT_AT
        bq = carve([NH, S], F16, 2)
        bth = carve([NH, S], F16, 2)
        btl = carve([NH, S], F16, 2)
        QS = [carve([NH, 2 * S], F16, 2) for _ in range(2)]
        KS = [carve([NH, 2 * S], F16, 2) for _ in range(2)]
        prob_all = carve([4 * QUAD, S], F32, 4)
        prob = [prob_all[:, QUAD * k:QUAD * k + QUAD, :] for k in range(4)]
        prob_lo = [carve([QUAD, S], F16, 2) for _ in range(4)]
        xn = carve([2, D], F32, 4)
        xnh = carve([C, 2, S], F16, 2)
        xnl = carve([C, 2, S], F16, 2)
        cf = [carve([C, 2, S], F32, 4) for _ in range(2)]
        ch = carve([C, 2, S], F16, 2)
        cl = carve([C, 2, S], F16, 2)
        qp = carve([2, C, 2 * S], F16, 2)
        kp = carve([2, C, 2 * S], F16, 2)
        v32 = carve([2, D], F32, 4)
        vh = [carve([2, NH, HD + 1], F16, 2) for _ in range(2)]
        vl = [carve([2, NH, HD + 1], F16, 2) for _ in range(2)]
        mx = carve([2, NH], F32, 4)
        mclamp = carve([2, NH], F32, 4)
        mrow = carve([2, S], F16, 2)
        den = carve([2, NH], F32, 4)
        rden = carve([2, NH], F32, 4)
        on = carve([2, D], F32, 4)
        onh = carve([2 * C, S], F16, 2)
        onl = carve([2 * C, S], F16, 2)
        awh = carve([4, C, D], F16, 2)
        awl = carve([4, C, D], F16, 2)
        qkbias = carve([4], F32, 4)
        vbr = carve([D], F32, 4)
        obr = carve([D], F32, 4)
        nmask = carve([B], F32, 4)
        mraw = carve([B], U8, 1)
        mrow_raw = carve([S], U8, 1)
        mrow16 = carve([S], F16, 2)

        cursor[0] = WBYTES
        rows = [carve([D], F32, 4) for _ in range(2)]
        xh = [carve([C, P], F16, 2) for _ in range(2)]
        xl = [carve([C, P], F16, 2) for _ in range(2)]
        sil = [carve([HID], F32, 4) for _ in range(2)]
        hid = [carve([HID], F32, 4) for _ in range(2)]
        hlo = [carve([HID], F16, 2) for _ in range(2)]
        ysb = [carve([D], F32, 4) for _ in range(2)]
        srow = [carve([D], F32, 4) for _ in range(2)]
        yg = [carve([2, D], F32, 4) for _ in range(2)]
        rt = carve([12, B, E], F32, 4)
        pick = carve([B, E], F16, 2)
        tri = carve([P], F16, 2)
        ones = carve([P], F16, 2)
        iota_e = carve([E], F32, 4)
        iota_t = carve([SLOT_TILES], F32, 4)
        sm = carve([12, B], F32, 4)
        cnt = carve([8, E], F32, 4)
        cnt_i = carve([E], I32, 4)
        slots = carve([2, B], I32, 4)
        slot_idx = [carve([2], I32, 4) for _ in range(2)]
        te_f = carve([SLOT_TILES, E], F32, 4)
        te_s = carve([SLOT_TILES], F32, 4)
        te = carve([SLOT_TILES], I32, 4)

        pb = [es.enter_context(nc.psum_tensor(f"bank{i}", [P, 512], F32)) for i in range(8)]
        psT, psQ, psK, psC = pb[0], pb[1], pb[2], pb[3]
        psR = pb[6]

        q_scr = nc.dram_tensor("q_scr", (2, 2, D, 2 * S), F16).ap()
        k_scr = nc.dram_tensor("k_scr", (2, 2, D, 2 * S), F16).ap()
        m_scr = nc.dram_tensor("m_scr", (B, S), F16).ap()
        xslots = nc.dram_tensor("xslots", (SLOT_TILES * P, D), F32).ap()
        yslots = nc.dram_tensor("yslots", (SLOT_TILES * P, D), F32).ap()
        ysv = yslots.rearrange("(t p) d -> t p d", p=P)

        x_in = [sem(f"x_in{q}") for q in range(4)]
        const_in = sem("const_in")
        const_rows = sem("const_rows")
        idents = sem("idents")
        stage_in = [sem("stage_in0"), sem("stage_in1")]
        stage_hi = sem("stage_hi")
        stage_lo = sem("stage_lo")
        setup_dve = sem("setup_dve")
        setup_act = sem("setup_act")
        mask_out = sem("mask_out")
        zero_out = sem("zero_out")
        stats_done = sem("stats_done")
        aggr_done = sem("aggr_done")
        ln_ready = sem("ln_ready")
        std_ready = sem("std_ready")

        ctx_in = [sem("ctx_in0"), sem("ctx_in1")]
        xn_ready = sem("xn_ready")
        xt_mm = sem("xt_mm")
        xh_ready = sem("xh_ready")
        xl_ready = sem("xl_ready")
        ch_ready = sem("ch_ready")
        cl_ready = sem("cl_ready")
        q_mm = sem("q_mm")
        k_mm = sem("k_mm")
        v_mm = sem("v_mm")
        qh_ready = sem("qh_ready")
        ql_ready = sem("ql_ready")
        kh_ready = sem("kh_ready")
        kl_ready = sem("kl_ready")
        v32_ready = sem("v32_ready")
        vh_ready = sem("vh_ready")
        vl_ready = sem("vl_ready")
        vmask_ready = sem("vmask_ready")
        q_out = sem("q_out")
        k_out = sem("k_out")
        qs_in = [sem("qs_in0"), sem("qs_in1")]
        ks_in = [sem("ks_in0"), sem("ks_in1")]
        s_mm = sem("s_mm")
        mx_ready = sem("mx_ready")
        mclamp_ready = sem("mclamp_ready")
        m_mm = sem("m_mm")
        mrow_ready = sem("mrow_ready")
        m_in = [sem("m_in0"), sem("m_in1")]
        st_mm = sem("st_mm")
        prob_ready = sem("prob_ready")
        prob_lo_ready = sem("prob_lo_ready")
        pv_mm = sem("pv_mm")
        den_ready = sem("den_ready")
        rden_ready = sem("rden_ready")
        on_ready = sem("on_ready")
        ot_mm = sem("ot_mm")
        onh_ready = sem("onh_ready")
        onl_ready = sem("onl_ready")
        o_mm = sem("o_mm")
        xb_ready = sem("xb_ready")
        x1_ready = sem("x1_ready")

        block = es.enter_context(nc.Block())

        def words_high(a):
            return a.bitcast(BF16).rearrange("p (n two) -> p n two", two=2)[:, :, 1]

        def flat(a):
            return a.rearrange("p a b -> p (a b)")

        bq_f, bth_f, btl_f = flat(bq), flat(bth), flat(btl)
        awh_f = awh.rearrange("p a b c -> p (a b c)")
        awl_f = awl.rearrange("p a b c -> p (a b c)")

        def front_parts(k):
            if k < 2:
                return awh_f[:, bass.ts(k, CHUNK)], awl_f[:, bass.ts(k, CHUNK)]
            if k < 4:
                return bq_f[:, bass.ts(k - 2, CHUNK)], None
            return bth_f[:, bass.ts(k - 4, CHUNK)], btl_f[:, bass.ts(k - 4, CHUNK)]

        def weight_parts(w):
            return (wparts[:, bass.ds(w * (2 * CHUNK), CHUNK)],
                    wparts[:, bass.ds(w * (2 * CHUNK) + CHUNK, CHUNK)])

        def lows(n):
            return (n if n <= 2 else 2 if n <= 4 else n - 2) if isinstance(n, int) else n - 2

        def act_high(act, k, slot, dst):
            act.wait_ge(stage_in[slot], k)
            nc.scalar.activation(dst, stage[:, slot, :], ACT.Copy).then_inc(stage_hi, 1)

        def pool_low(pool, n, slot, hi, lo):
            pool.wait_ge(stage_hi, n)
            nc.gpsimd.tensor_tensor(lo, stage[:, slot, :], hi, ALU.subtract).then_inc(stage_lo, 1)


        def pair_loop(eng, body):
            body(0, 0, 0)
            body(1, 1, 0)
            with eng.Fori(1, NPAIR // 2 - 1) as k:
                body(2 * k, 0, k)
                body(2 * k + 1, 1, k)
            body(NPAIR - 2, 0, NPAIR // 2 - 1)
            body(NPAIR - 1, 1, NPAIR // 2 - 1)

        def known(i):
            return isinstance(i, int)

        def before(i, n):
            return i >= n if known(i) else True

        def upto(i, n):
            return i <= n if known(i) else True

        R1, RE, R2 = B, B + HALF, B + HALF + SLOT_TILES
        RTOT = R2 + (B - HALF)
        U1, UE, U2 = 0, 2 * HALF, 2 * HALF + SLOT_TILES
        UTOT = U2 + 2 * (B - HALF)

        route_const = sem("route_const")
        rows_made = sem("rows_made")
        rows_in = [sem("rows_in0"), sem("rows_in1")]
        tr_mm = sem("tr_mm")
        th_ready = sem("th_ready")
        tl_ready = sem("tl_ready")
        router_mm = sem("router_mm")
        logit_ready = sem("logit_ready")
        route = sem("route")
        rank_mm = sem("rank_mm")
        exp_ready = sem("exp_ready")
        idx_ready = sem("idx_ready")
        dve_passed = sem("dve_passed")
        pool_passed = sem("pool_passed")
        sp_passed = sem("sp_passed")
        srow_made = sem("srow_made")
        scattered = [sem("scattered0"), sem("scattered1")]
        h1_mm = sem("h1_mm")
        h3_mm = sem("h3_mm")
        sil_ready = sem("sil_ready")
        hid_ready = sem("hid_ready")
        hlo_ready = sem("hlo_ready")
        y_mm = sem("y_mm")
        y_added = sem("y_added")
        y_copied = sem("y_copied")
        y_out = [sem("y_out0"), sem("y_out1")]
        gathered = [sem("gathered0"), sem("gathered1")]
        comb_a = sem("comb_a")
        comb_b = sem("comb_b")
        res_out = sem("res_out")
        mv_ready = sem("mv_ready")
        var_ready = sem("var_ready")
        ln2_std = sem("ln2_std")
        ln2_rstd = sem("ln2_rstd")

        def section(r):
            return "R" if r < R1 else "1" if r < RE else "E" if r < R2 else "2"

        def last_unit(r, sect=None):
            sect = sect or section(r)
            return {"1": 2 * (r - R1) + 1, "E": r - RE + UE, "2": 2 * (r - R2) + 1 + U2}[sect]

        def steps(r, sect):
            if sect == "E":
                return [(r - RE + UE, 1, 1)]
            u = 2 * (r - R1) if sect == "1" else 2 * (r - R2) + U2
            return [(u, 1, 0), (u + 1, 0, 1)]

        def moe_loop(eng, body):
            for a, b, sect, prev, nxt in ((R1, RE, "1", None, "E"), (RE, R2, "E", "1", "2"),
                                          (R2, RTOT, "2", "E", None)):
                n = (b - a) // 2
                body(a, 0, sect, prev, sect, 0)
                body(a + 1, 1, sect, sect, sect, 0)
                with eng.Fori(1, n - 1) as k:
                    body(2 * k + a, 0, sect, sect, sect, k)
                    body(2 * k + (a + 1), 1, sect, sect, sect, k)
                body(b - 2, 0, sect, sect, sect, n - 1)
                body(b - 1, 1, sect, sect, nxt, n - 1)

        @block.sync
        def _(sp):
            def wait_stage_slot(n):
                sp.wait_ge(stage_hi, n - 1)
                sp.sem_inc(sp_passed, 1)
                sp.wait_ge(stage_lo, lows(n - 1))

            def load_stage(slot, src):
                sp.dma_start(stage[:, slot, :], src).then_inc(stage_in[slot], 16)

            xv = x.rearrange("b s d -> s b d")
            sp.dma_start(xs[:, 0:8, :], xv[:, 0:8, :]).then_inc(x_in[0], 16)
            for dst, src in ((graw[:, 0:1], g_att.partition_broadcast(P)), (graw[:, 1:2], g_ffn.partition_broadcast(P)),
                             (qkbias, qkb), (vbr, vb.partition_broadcast(P)), (obr, ob.partition_broadcast(P)),
                             (mraw, maskT), (mrow_raw[0:B, :], mask),
                             (rw_f[:, :, :], rw.rearrange("(c p) e -> p c e", p=P)), (ebr[:, :], eb.partition_broadcast(P))):
                sp.dma_start(dst, src).then_inc(const_in, 16)

            def front_src(k):
                if k < 2:
                    return attw[k]
                return (bias_q if k < 4 else bias_t)[k % 2]

            for k in range(FRONT + PRE_CHUNKS):
                if k >= 2:
                    wait_stage_slot(k)
                load_stage(k % 2, front_src(k) if k < FRONT else wall[k - FRONT])
                if 1 <= k < 4:
                    sp.dma_start(xs[:, 8 * k:8 * k + 8, :], xv[:, 8 * k:8 * k + 8, :]).then_inc(x_in[k], 16)
            sp.wait_ge(setup_dve, 1)
            sp.dma_start(m_scr, mrow16[0:B, :]).then_inc(mask_out, 16)
            sp.wait_ge(mask_out, 16)

            cv = ctxT.rearrange("(c p) t -> p c t", p=P)

            def load_ctx(i, p):
                sp.dma_start(cf[p].rearrange("p c b t -> p c (b t)"),
                             cv[:, :, bass.ds(i * (2 * S), 2 * S)]).then_inc(ctx_in[p], 16)

            def parts_out(i, p):
                for scr, parts, ready, sent in ((q_scr, qp, ql_ready, q_out), (k_scr, kp, kl_ready, k_out)):
                    sp.wait_ge(ready, 2 * i + 2)
                    sp.dma_start(scr[p].rearrange("s (c p) t -> p s c t", p=P), parts).then_inc(sent, 16)

            def stack(i, p):
                if before(i, 2):
                    sp.wait_ge(st_mm, 8 * i - 8)
                for scr, dst, sent, arrived, order in ((q_scr, QS[p], q_out, qs_in[p], (0, 0, 1)),
                                                       (k_scr, KS[p], k_out, ks_in[p], (0, 1, 0))):
                    sp.wait_ge(sent, 16 * i + 16)
                    for j, part in enumerate(order):
                        sp.dma_start(dst[HD * j:HD * j + HD],
                                     scr[p, part].rearrange("(h d) t -> d h t", d=HD)).then_inc(arrived, 16)
                row = m_scr[bass.ds(2 * i, 2), :].rearrange("b t -> (b t)").partition_broadcast(NH)
                sp.dma_start(KS[p][ROW_MASK:ROW_MASK + 1], row.unsqueeze(0)).then_inc(ks_in[p], 16)

            def max_row(i, p, b):
                sp.wait_ge(mrow_ready, 2 * i + b + 1)
                sp.dma_start(QS[p][ROW_MAX:ROW_MAX + 1, :, b * S:b * S + S], mrow[0:NH, b, :]).then_inc(m_in[b], 16)

            load_ctx(0, 0)
            load_ctx(1, 1)
            sp.wait_ge(const_rows, 2)
            parts_out(0, 0)
            stack(0, 0)

            def body(i, p, k):
                if upto(i, NPAIR - 3):
                    sp.wait_ge(ch_ready, i + 1)
                    sp.wait_ge(cl_ready, i + 1)
                    load_ctx(i + 2, p)
                max_row(i, p, 0)
                if upto(i, NPAIR - 2):
                    parts_out(i + 1, 1 - p)
                max_row(i, p, 1)
                if upto(i, NPAIR - 2):
                    stack(i + 1, 1 - p)
                wait_stage_slot(FRONT + PRE_CHUNKS + i)
                load_stage(p, wall[bass.ds(i + PRE_CHUNKS, 1)].rearrange("a p n -> (a p) n"))

            pair_loop(sp, body)

            for w in range(PRE_CHUNKS + ATT_CHUNKS, NCHUNK):
                wait_stage_slot(FRONT + w)
                load_stage(w % 2, wall[w])

            sp.wait_ge(zero_out, 16 * ZERO_DMAS)
            for s in range(2):
                sp.wait_ge(scattered[s], 16 * B)
            xsv = xslots.rearrange("(t p) d -> t p d", p=P)

            def load_rows(t, p):
                sp.wait_ge(tr_mm, t + RE - 1)
                sp.dma_start(rows[p], xsv[bass.ds(t, 1)].rearrange("a p d -> (a p) d")).then_inc(rows_in[p], 16)

            with sp.Fori(0, SLOT_TILES // 2) as k:
                load_rows(2 * k, 0)
                load_rows(2 * k + 1, 1)

            def store_out(n, j):
                sp.wait_ge(comb_b, n + 1)
                sp.dma_start(out[bass.ds(j, 1)].rearrange("a s d -> (a s) d"), xs[:, bass.ds(j, 1), :].rearrange("p a d -> p (a d)")).then_inc(res_out, 16)

            store_out(0, 0)
            with sp.Fori(1, HALF) as k:
                store_out(2 * k - 1, k)
                store_out(2 * k, k + HALF - 1)
            store_out(B - 1, B - 1)
            sp.wait_ge(res_out, 16 * B)

        @block.gpsimd
        def _(pool):
            nc.gpsimd.memset(ident[:, :], 0.0).then_inc(idents, 1)
            nc.gpsimd.memset(ident16[:, :], 0.0).then_inc(idents, 1)
            pool.wait_ge(idents, 2)
            nc.gpsimd.affine_select(out=ident[:, :], in_=ident[:, :], compare_op=ALU.not_equal, fill=1.0,
                                    base=0, pattern=[[-1, P]], channel_multiplier=1).then_inc(idents, 1)
            nc.gpsimd.affine_select(out=ident16[:, :], in_=ident16[:, :], compare_op=ALU.not_equal, fill=1.0,
                                    base=0, pattern=[[-1, P]], channel_multiplier=1).then_inc(idents, 1)
            zsrc = flat(prob_all)
            nc.gpsimd.memset(zsrc, 0.0).then_inc(idents, 1)
            pool.wait_ge(idents, 5)
            zv = xslots.rearrange("(n p r) d -> n p (r d)", p=P, r=ZERO_ROWS)
            for n in range(SLOT_TILES // ZERO_ROWS):
                pool.dma_start(zv[n], zsrc).then_inc(zero_out, 16)
            for t in QS + KS:
                last = nc.gpsimd.memset(flat(t).bitcast(F32), 0.0)
            for t in vl:
                last = nc.gpsimd.memset(t.rearrange("p b h e -> p (b h e)"), 0.0)
            last.then_inc(idents, 1)
            for k in range(FRONT + PRE_CHUNKS):
                hi, lo = front_parts(k) if k < FRONT else weight_parts(k - FRONT)
                if lo is not None:
                    pool_low(pool, k + 1, k % 2, hi, lo)

            def context_low(i, p):
                pool.wait_ge(ch_ready, i + 1)
                if before(i, 1):
                    pool.wait_ge(v_mm, i)
                nc.gpsimd.tensor_tensor(cl.rearrange("p c b t -> p (c b t)"), cf[p].rearrange("p c b t -> p (c b t)"),
                                        ch.rearrange("p c b t -> p (c b t)"), ALU.subtract).then_inc(cl_ready, 1)

            def mask_columns(i, p):
                if before(i, 2):
                    pool.wait_ge(pv_mm, 8 * i - 8)
                for b in range(2):
                    nc.gpsimd.tensor_copy(vh[p][:, b, :, HD], nmask[:, bass.ds(2 * i + b, 1)].to_broadcast([P, NH])).then_inc(vmask_ready, 1)

            def add_output_bias(i):
                pool.wait_ge(xn_ready, 2 * i + 2)
                for b in range(2):
                    xb = xs[:, bass.ds(2 * i + b, 1), :].rearrange("p a d -> p (a d)")
                    nc.gpsimd.tensor_tensor(xb, xb, obr, ALU.add).then_inc(xb_ready, 1)

            pool.wait_ge(setup_dve, 4)
            context_low(0, 0)
            mask_columns(0, 0)

            def body(i, p, k):
                if upto(i, NPAIR - 2):
                    context_low(i + 1, 1 - p)
                add_output_bias(i)
                if upto(i, NPAIR - 2):
                    mask_columns(i + 1, 1 - p)
                hi, lo = weight_parts(i + PRE_CHUNKS)
                pool_low(pool, FRONT + PRE_CHUNKS + i + 1, p, hi, lo)

            pair_loop(pool, body)

            pool.wait_ge(x1_ready, B)
            nc.gpsimd.memset(tri, 1.0).then_inc(route_const, 1)
            nc.gpsimd.memset(ones, 1.0).then_inc(route_const, 1)
            nc.gpsimd.iota(iota_e, [[1, E]], base=0, channel_multiplier=0,
                           allow_small_or_imprecise_dtypes=True).then_inc(route_const, 1)
            nc.gpsimd.iota(iota_t, [[1, SLOT_TILES]], base=0, channel_multiplier=0,
                           allow_small_or_imprecise_dtypes=True).then_inc(route_const, 1)
            pool.wait_ge(route_const, 4)
            nc.gpsimd.affine_select(out=tri, in_=tri, compare_op=ALU.is_gt, fill=0.0, base=0,
                                    pattern=[[1, P]], channel_multiplier=-1).then_inc(route_const, 1)
            first = PRE_CHUNKS + ATT_CHUNKS
            with pool.Fori(0, (NCHUNK - first) // 2) as k:
                for q in range(2):
                    hi, lo = weight_parts(2 * k + (first + q))
                    pool_low(pool, 2 * k + (FRONT + first + q + 1), q, hi, lo)
            pool.wait_ge(route, ROUTE_STEPS)

            def indices(n, j, p, users, used):
                if used is not None:
                    pool.wait_ge(users[p], used)
                nc.gpsimd.tensor_copy(slot_idx[p], slots[:, :, bass.ds(j, 1)].rearrange("p s a -> p (s a)"))\
                    .then_inc(idx_ready, 1)
                pool.wait_ge(idx_ready, n + 1)
                pool.sem_inc(pool_passed, 1)

            def scatter(j, p, used):
                pool.wait_ge(srow_made, j + 1)
                indices(j, j, p, scattered, used)
                for s in range(2):
                    nc.gpsimd.indirect_dma_start(
                        xslots, bass.IndirectOffsetOnAxis(ap=slot_idx[p][:, s:s + 1], axis=0),
                        srow[p], None).then_inc(scattered[p], 16)

            scatter(0, 0, None)
            scatter(1, 1, None)
            with pool.Fori(1, B // 2) as k:
                scatter(2 * k, 0, 32 * k)
                scatter(2 * k + 1, 1, 32 * k)
            for s in range(2):
                pool.wait_ge(y_out[s], 16 * (SLOT_TILES // 2))

            def gather(n, j, p, half):
                if known(half) and half < 1:
                    indices(B + n, j, p, scattered, 16 * B)
                else:
                    pool.wait_ge(comb_b, n - 1)
                    indices(B + n, j, p, gathered, 32 * half)
                for s in range(2):
                    nc.gpsimd.indirect_dma_start(
                        yg[p][:, s, :], None, yslots,
                        bass.IndirectOffsetOnAxis(ap=slot_idx[p][:, s:s + 1], axis=0)).then_inc(gathered[p], 16)

            gather(0, 0, 0, 0)
            gather(1, 1, 1, 0)
            gather(2, HALF, 0, 1)
            with pool.Fori(2, HALF) as k:
                gather(2 * k - 1, k, 1, k - 1)
                gather(2 * k, k + HALF - 1, 0, k)
            gather(B - 1, B - 1, 1, HALF - 1)

        @block.scalar
        def _(act):
            act.wait_ge(const_in, 16 * CONSTS)
            nc.scalar.activation(gates[:, :], graw[:, :], ACT.Tanh).then_inc(setup_act, 1)
            nc.scalar.activation(rwh[:, :, :], rw_f[:, :, :], ACT.Copy).then_inc(setup_act, 1)
            for k in range(FRONT + PRE_CHUNKS):
                hi, lo = front_parts(k) if k < FRONT else weight_parts(k - FRONT)
                if k == 0:
                    act.wait_ge(setup_dve, 6)
                act_high(act, 16 * (k // 2 + 1), k % 2, hi)
            act.wait_ge(mv_ready, 2 * B)
            nc.scalar.activation(std[:, :], var_eps[:, :], ACT.Sqrt).then_inc(std_ready, 1)

            def context_high(i, p, k):
                act.wait_ge(ctx_in[p], 16 * (k + 1))
                if before(i, 1):
                    act.wait_ge(v_mm, i)
                nc.scalar.activation(ch.rearrange("p c b t -> p (c b t)"), cf[p].rearrange("p c b t -> p (c b t)"),
                                     ACT.Copy).then_inc(ch_ready, 1)

            def xn_high(i):
                act.wait_ge(xt_mm, i + 1)
                if before(i, 1):
                    act.wait_ge(q_mm, i)
                nc.scalar.activation(xnh, psT[:, :].rearrange("p (b c t) -> p c b t", b=2, c=C),
                                     ACT.Copy).then_inc(xh_ready, 1)

            def qk_high(i):
                for ps, parts, col, mm, sent, ready in ((psQ, qp, 0, q_mm, q_out, qh_ready),
                                                        (psK, kp, 2, k_mm, k_out, kh_ready)):
                    act.wait_ge(mm, i + 1)
                    if before(i, 1):
                        act.wait_ge(sent, 16 * i)
                    for m in range(C):
                        nc.scalar.activation(parts[:, 0, m, :], ps[:, bass.ts(m, 2 * S)], ACT.Identity,
                                             bias=qkbias[:, col + m:col + m + 1]).then_inc(ready, 1)

            def v_high(i, p):
                act.wait_ge(v32_ready, i + 1)
                if before(i, 2):
                    act.wait_ge(pv_mm, 8 * i - 8)
                for b in range(2):
                    nc.scalar.activation(vh[p][:, b, :, 0:HD], v32[:, b, :].rearrange("p (h e) -> p h e", h=NH),
                                         ACT.Copy, scale=nmask[:, bass.ds(2 * i + b, 1)]).then_inc(vh_ready, 1)

            def max_row(i, b):
                act.wait_ge(m_mm, 2 * i + b + 1)
                if before(i, 1):
                    act.wait_ge(m_in[b], 16 * i)
                nc.scalar.activation(mrow[0:NH, b, :], psC[0:NH, 384:512], ACT.Copy, scale=-1.0).then_inc(mrow_ready, 1)

            def out_high(i):
                act.wait_ge(ot_mm, i + 1)
                if before(i, 1):
                    act.wait_ge(o_mm, i)
                nc.scalar.activation(flat(onh), psT[:, :], ACT.Copy).then_inc(onh_ready, 1)

            act.wait_ge(zero_out, 16 * ZERO_DMAS)
            context_high(0, 0, 0)
            xn_high(0)
            qk_high(0)
            v_high(0, 0)
            context_high(1, 1, 0)

            def body(i, p, k):
                if before(i, 1):
                    out_high(i - 1)
                max_row(i, 0)
                if upto(i, NPAIR - 2):
                    xn_high(i + 1)
                    qk_high(i + 1)
                max_row(i, 1)
                if upto(i, NPAIR - 2):
                    v_high(i + 1, 1 - p)
                for n in range(8):
                    act.wait_ge(st_mm, 8 * i + n + 1)
                    if before(i, 1) or n >= 4:
                        act.wait_ge(pv_mm, 8 * i + n - 3)
                    nc.scalar.activation(flat(prob[n % 4]), pb[6 + n % 2][:, :], ACT.Exp).then_inc(prob_ready, 1)
                if upto(i, NPAIR - 3):
                    context_high(i + 2, p, k + 1)
                act_high(act, 16 * ((FRONT + PRE_CHUNKS) // 2 + k + 1), p, weight_parts(i + PRE_CHUNKS)[0])

            pair_loop(act, body)
            out_high(NPAIR - 1)
            act.wait_ge(x1_ready, B)


            def split_high(r, p, sect=None):
                act.wait_ge(tr_mm, r + 1)
                if not (known(r) and r < 2):
                    if (sect or section(r - 2)) == "R":
                        act.wait_ge(router_mm, r - 1)
                    else:
                        act.wait_ge(h3_mm, last_unit(r - 2, sect) + 1)
                nc.scalar.activation(flat(xh[p]), pb[7 * p][:, 0:D], ACT.Copy).then_inc(th_ready, 1)

            def router_std(r):
                act.wait_ge(var_ready, r + 1)
                nc.scalar.activation(std[:, bass.ds(r, 1)], var_eps[:, bass.ds(r, 1)], ACT.Sqrt).then_inc(ln2_std, 1)

            router_std(0)
            for r in range(2):
                router_std(r + 1)
                split_high(r, r % 2)
            first = PRE_CHUNKS + ATT_CHUNKS
            turns = (NCHUNK - first) // 2
            assert first % 2 == 0 and 2 + 4 * turns <= B - 1
            with act.Fori(0, turns) as k:
                for q in range(4):
                    router_std(4 * k + q + 3)
                    split_high(4 * k + q + 2, q % 2, "R")
                    if q % 2:
                        act_high(act, 16 * ((FRONT + first) // 2 + 1) + 16 * k, q // 2,
                                 weight_parts(2 * k + first + q // 2)[0])
            for r in range(2 + 4 * turns, B):
                if r < B - 1:
                    router_std(r + 1)
                split_high(r, r % 2)
            act.wait_ge(route, EXP_STEP)
            nc.scalar.activation(sm[:, 5, :], sm[:, 4, :], ACT.Exp).then_inc(exp_ready, 1)
            split_high(R1, 0)

            def copy_y(t, p, k):
                act.wait_ge(y_mm, t + UE + 1)
                if not (known(k) and k < 1):
                    act.wait_ge(y_out[p], 16 * k)
                nc.scalar.activation(ysb[p], pb[1 + 5 * p][:, 0:D], ACT.Copy).then_inc(y_copied, 1)
                act.wait_ge(y_copied, t + 1)
                act.dma_start(ysv[bass.ds(t, 1)].rearrange("a p d -> (a p) d"), ysb[p]).then_inc(y_out[p], 16)

            def body(r, p, sect, prev, nxt, k):
                for u, first_unit, last in steps(r, sect):
                    q = p if sect == "E" else 1 - first_unit
                    act.wait_ge(h1_mm, u + 1)
                    if not (known(u) and u < 2):
                        act.wait_ge(hid_ready, u - 1)
                    nc.scalar.activation(sil[q], pb[2 + 2 * q][:, :], ACT.Silu).then_inc(sil_ready, 1)
                    if last and nxt is not None:
                        split_high(r + 1, 1 - p, None if known(r) else sect)
                    if first_unit and prev == "E":
                        copy_y(r - 1 - RE, 1 - p, (r - 1 - RE) // 2 if known(r) else k if p else k - 1)

            moe_loop(act, body)

        @block.tensor
        def _(pe):
            mm = nc.tensor.matmul

            def transpose_xn(i):
                pe.wait_ge(xn_ready, 2 * i + 2)
                if before(i, 1):
                    pe.wait_ge(xl_ready, i)
                if before(i, 2):
                    pe.wait_ge(onl_ready, i - 1)
                for b in range(2):
                    for c in range(C):
                        k = b * C + c
                        last = nc.tensor.transpose(psT[:, bass.ts(k, P)], xn[:, b, bass.ts(c, P)], ident[:, :])
                last.then_inc(xt_mm, 1)

            def project_qk(ps, j, act_h, act_l, done):
                for m in range(C):
                    for c in range(C):
                        for w, a in ((awh, act_h), (awh, act_l), (awl, act_h)):
                            last = mm(ps[:, bass.ts(m, 2 * S)], w[:, j, c, bass.ts(m, P)],
                                      a[:, c].rearrange("p b t -> p (b t)"),
                                      start=(c == 0 and w is awh and a is act_h),
                                      stop=(c == C - 1 and w is awl))
                last.then_inc(done, 1)

            def project(i):
                pe.wait_ge(xl_ready, i + 1)
                if before(i, 1):
                    pe.wait_ge(v32_ready, i)
                project_qk(psQ, 0, xnh, xnl, q_mm)
                pe.wait_ge(cl_ready, i + 1)
                if before(i, 3):
                    pe.wait_ge(x1_ready, 2 * i - 4)
                project_qk(psK, 1, ch, cl, k_mm)
                pe.wait_ge(ql_ready, 2 * i + 2)
                for b in range(2):
                    for c in range(C):
                        for a, w in ((ch, awh), (cl, awh), (ch, awl)):
                            last = mm(psQ[:, bass.ts(b, D)], a[:, c, b, :], w[:, 2, c, :],
                                      start=(c == 0 and a is ch and w is awh),
                                      stop=(c == C - 1 and w is awl))
                last.then_inc(v_mm, 1)

            def scores(i, p, b, half):
                for k in range(NQ):
                    n = 4 * b + k
                    bank = pb[4 + n % 2]
                    if n == 0:
                        pe.wait_ge(qs_in[p], 48 * (half + 1))
                        pe.wait_ge(ks_in[p], 64 * (half + 1))
                    if before(i, 1) or n >= 2:
                        pe.wait_ge(mx_ready, 8 * i + n - 1)
                    mm(bank[:, :], ident16[:, :], bq_f[:, bass.ts(k, 512)], start=True, stop=False,
                   skip_group_check=True)
                    for h in range(QUAD):
                        last = mm(bank[:, bass.ts(h, S)], QS[p][0:ROW_MAX, QUAD * k + h, bass.ts(b, S)],
                                  KS[p][0:ROW_MAX, QUAD * k + h, bass.ts(b, S)], start=False, stop=True,
                                  skip_group_check=True)
                    last.then_inc(s_mm, 1)

            def transpose_max(i, b):
                pe.wait_ge(mclamp_ready, 2 * i + b + 1)
                if b == 0 and before(i, 1):
                    pe.wait_ge(on_ready, 2 * i)
                if before(i, 1) or b:
                    pe.wait_ge(mrow_ready, 2 * i + b)
                nc.tensor.transpose(psC[0:NH, 384:512], mclamp[:, b, :], ident[:, :]).then_inc(m_mm, 1)

            def scores_t(i, p, n):
                b, k = n // 4, n % 4
                bank = pb[6 + n % 2]
                if k == 0:
                    pe.wait_ge(m_in[b], 16 * i + 16)
                if before(i, 1) or n >= 2:
                    pe.wait_ge(prob_ready, 8 * i + n - 1)
                mm(bank[:, :], ident16[:, :], bth_f[:, bass.ts(k, 512)], start=True, stop=False,
                   skip_group_check=True)
                mm(bank[:, :], ident16[:, :], btl_f[:, bass.ts(k, 512)], start=False, stop=False,
                   skip_group_check=True)
                for h in range(QUAD):
                    last = mm(bank[:, bass.ts(h, S)], KS[p][0:ROW_MAX + 1, QUAD * k + h, bass.ts(b, S)],
                              QS[p][0:ROW_MAX + 1, QUAD * k + h, bass.ts(b, S)], start=False, stop=True,
                              skip_group_check=True)
                last.then_inc(st_mm, 1)

            def values(i, p, n):
                b, k = n // 4, n % 4
                if n == 0:
                    pe.wait_ge(vl_ready, 2 * i + 2)
                    pe.wait_ge(vmask_ready, 2 * i + 2)
                    pe.wait_ge(mrow_ready, 2 * i + 2)
                if k == 0 and (before(i, 1) or b):
                    pe.wait_ge(on_ready, 2 * i + b)
                pe.wait_ge(prob_lo_ready, 8 * i + n + 1)
                hi = words_high(flat(prob[n % 4]))
                for h in range(QUAD):
                    hh = QUAD * k + h
                    o = psC[:, hh * (HD + 1):(hh + 1) * (HD + 1)]
                    mm(o, hi[:, bass.ts(h, S)], vh[p][:, b, hh, :], start=True, stop=False)
                    mm(o, hi[:, bass.ts(h, S)], vl[p][:, b, hh, :], start=False, stop=False)
                    last = mm(o, prob_lo[n % 4][:, h, :], vh[p][:, b, hh, :], start=False, stop=True)
                last.then_inc(pv_mm, 1)

            def transpose_out(i):
                pe.wait_ge(on_ready, 2 * i + 2)
                pe.wait_ge(xl_ready, min(i + 2, NPAIR) if known(i) else i + 2)
                for k in range(2 * C):
                    last = nc.tensor.transpose(psT[:, bass.ts(k, P)], on.rearrange("p b d -> p (b d)")[:, bass.ts(k, P)],
                                               ident[:, :])
                last.then_inc(ot_mm, 1)

            def project_out(i):
                pe.wait_ge(onl_ready, i + 1)
                pe.wait_ge(kl_ready, min(2 * i + 6, 2 * NPAIR) if known(i) else 2 * i + 6)
                for b in range(2):
                    for c in range(C):
                        for a, w in ((onh, awh), (onl, awh), (onh, awl)):
                            last = mm(psK[:, bass.ts(b, D)], a[:, b * C + c, :], w[:, 3, c, :],
                                      start=(c == 0 and a is onh and w is awh),
                                      stop=(c == C - 1 and w is awl))
                last.then_inc(o_mm, 1)

            pe.wait_ge(idents, 4)
            pe.wait_ge(stage_hi, FRONT)
            pe.wait_ge(stage_lo, lows(FRONT))
            transpose_xn(0)
            project(0)

            def body(i, p, k):
                scores(i, p, 0, k)
                if before(i, 1):
                    transpose_out(i - 1)
                scores(i, p, 1, k)
                transpose_max(i, 0)
                if upto(i, NPAIR - 2):
                    transpose_xn(i + 1)
                    project(i + 1)
                transpose_max(i, 1)
                if before(i, 1):
                    project_out(i - 1)
                for n in range(8):
                    scores_t(i, p, n)
                    if n >= 2:
                        values(i, p, n - 2)
                values(i, p, 6)
                values(i, p, 7)

            pair_loop(pe, body)
            transpose_out(NPAIR - 1)
            project_out(NPAIR - 1)
            pe.wait_ge(x1_ready, B)

            def transpose_rows(r, p, sect, half):
                if sect == "E":
                    pe.wait_ge(rows_in[p], 16 * (half + 1))
                else:
                    pe.wait_ge(rows_made, r + 1 if sect != "2" else r + 1 - R2 + RE)
                if not (known(r) and r < 2):
                    pe.wait_ge(tl_ready, r - 1)
                for c in range(C):
                    last = nc.tensor.transpose(pb[7 * p][:, bass.ts(c, P)], rows[p][:, bass.ts(c, P)], ident[:, :])
                last.then_inc(tr_mm, 1)

            def router(r, p):
                pe.wait_ge(tl_ready, r + 1)
                if not (known(r) and r < 2):
                    pe.wait_ge(logit_ready, r - 1)
                for c in range(C):
                    for a, w in ((xh[p], rwh), (xl[p], rwh), (xh[p], rwl)):
                        last = mm(pb[2 + p][:, 0:E], a[:, c, :], w[:, c, :],
                                  start=(c == 0 and a is xh[p] and w is rwh), stop=(c == C - 1 and w is rwl))
                last.then_inc(router_mm, 1)

            transpose_rows(0, 0, "R", 0)
            transpose_rows(1, 1, "R", 0)
            router(0, 0)
            with pe.Fori(1, B // 2) as k:
                transpose_rows(2 * k, 0, "R", k)
                router(2 * k - 1, 1)
                transpose_rows(2 * k + 1, 1, "R", k)
                router(2 * k, 0)
            router(B - 1, 1)
            pe.wait_ge(route, PICK_STEP)
            pe.wait_ge(route_const, 5)
            pe.wait_ge(logit_ready, B)
            mm(psR[:, 0:B * E], tri, flat(pick), start=True, stop=True)
            mm(psR[:, B * E:], ones, flat(pick), start=True, stop=True).then_inc(rank_mm, 1)
            transpose_rows(R1, 0, "1", 0)

            def up(u, q, p, at):
                if not (known(u) and u < 2):
                    pe.wait_ge(hid_ready, u - 1)
                for j, done in ((0, h1_mm), (1, h3_mm)):
                    base = at + j * 2 * CHUNK
                    for m in range(KC):
                        for c in range(C):
                            hi = wparts[:, bass.ds(base + c * HID + m * P, P)]
                            lo = wparts[:, bass.ds(base + CHUNK + c * HID + m * P, P)]
                            o = pb[2 + 2 * q + j][:, bass.ts(m, P)]
                            mm(o, hi, xh[p][:, c, :], start=(c == 0), stop=False)
                            mm(o, hi, xl[p][:, c, :], start=False, stop=False)
                            last = mm(o, lo, xh[p][:, c, :], start=False, stop=(c == C - 1))
                    last.then_inc(done, 1)

            def down(u, q, p, at, first, last_unit):
                pe.wait_ge(hlo_ready, u + 1)
                o = pb[1 + 5 * p][:, 0:D]
                hi = words_high(hid[q])
                base = at + 2 * 2 * CHUNK
                for k in range(KC):
                    w_hi = wparts[:, bass.ds(base + k * D, D)]
                    w_lo = wparts[:, bass.ds(base + CHUNK + k * D, D)]
                    mm(o, hi[:, bass.ts(k, P)], w_hi, start=(first and k == 0), stop=False)
                    mm(o, hi[:, bass.ts(k, P)], w_lo, start=False, stop=False)
                    last = mm(o, hlo[q][:, bass.ts(k, P)], w_hi, start=False, stop=(last_unit and k == KC - 1))
                last.then_inc(y_mm, 1)

            def wait_y_bank(r, sect=None):
                sect = sect or section(r - 2)
                if sect == "R":
                    pe.wait_ge(route, RANK_STEP)
                elif sect == "E":
                    pe.wait_ge(y_copied, r - 1 - RE)
                else:
                    pe.wait_ge(y_added, r - 1 - R1 if sect == "1" else r - 1 - R2 + HALF)

            def expert_at(t):
                return pe.value_load(te[0:1, bass.ds(t, 1)], min_val=3 * NSH * 2 * CHUNK,
                                     max_val=3 * (NSH + E - 1) * 2 * CHUNK)

            shared2 = 3 * 2 * CHUNK

            def body(r, p, sect, prev, nxt, k):
                for j, (u, first, last) in enumerate(steps(r, sect)):
                    q = p if sect == "E" else j
                    at = expert_at(r - RE) if sect == "E" else j * shared2
                    if first:
                        pe.wait_ge(tl_ready, r + 1)
                    if sect == "E":
                        if known(r) and r == RE:
                            pe.wait_ge(stage_hi, FRONT + NCHUNK)
                            pe.wait_ge(stage_lo, lows(FRONT + NCHUNK))
                            pe.wait_ge(route, ROUTE_STEPS)
                            pe.wait_ge(y_added, HALF - 1)
                        if known(r) and r == RE + 1:
                            pe.wait_ge(y_added, HALF)
                    up(u, q, p, at)
                    if last and nxt is not None:
                        transpose_rows(r + 1, 1 - p, nxt, 0 if nxt != sect else k + p)
                    if j == 1:
                        wait_y_bank(r, None if known(r) else sect)
                        down(u - 1, 1 - q, p, 0, True, False)
                    elif prev == "E":
                        at = expert_at(r - 1 - RE)
                        wait_y_bank(r - 1, None if known(r) else sect)
                        down(u - 1, 1 - q, 1 - p, at, True, True)
                    elif prev is not None:
                        down(u - 1, 1 - q, 1 - p, shared2, False, True)

            moe_loop(pe, body)
            down(UTOT - 1, 1, 1, shared2, False, True)

        @block.vector
        def _(dve):
            V = nc.vector
            dve.wait_ge(const_in, 16 * CONSTS)
            dve.wait_ge(idents, 6)
            for p in range(2):
                V.memset(flat(QS[p])[ROW_MASK:ROW_MASK + 1, :], MASK_Q)
                V.memset(flat(KS[p])[ROW_MAX:ROW_MAX + 1, :], 1.0).then_inc(const_rows, 1)
            V.tensor_scalar(mrow16[0:B, :], mrow_raw[0:B, :], MASK_K, None, ALU.mult).then_inc(setup_dve, 1)
            dve.wait_ge(setup_act, 2)
            V.tensor_tensor(rwl[:, :, :], rw_f[:, :, :], rwh[:, :, :], ALU.subtract).then_inc(setup_dve, 1)
            V.tensor_scalar(nmask, mraw, -1.0, 1.0, ALU.mult, ALU.add).then_inc(setup_dve, 1)
            V.tensor_scalar(obr, obr, gates[:, 0:1], None, ALU.mult).then_inc(setup_dve, 1)
            dve.wait_ge(stage_in[0], 16)
            V.tensor_scalar(stage[:, 0, 0:C * D], stage[:, 0, 0:C * D], HD ** -0.5, None, ALU.mult).then_inc(setup_dve, 1)
            V.tensor_scalar(qkbias[:, 0:C], qkbias[:, 0:C], HD ** -0.5, None, ALU.mult).then_inc(setup_dve, 1)

            for q in range(4):
                dve.wait_ge(x_in[q], 16)
                with dve.Fori(8 * q, 8 * q + 8) as j:
                    V.bn_stats(stats[:, 0, :], xs[:, bass.ds(j, 1), :].rearrange("p a d -> p (a d)")).then_inc(stats_done, 1)
                    dve.wait_ge(stats_done, j + 1)
                    dve.sem_inc(dve_passed, 1)
                    V.bn_aggr(mv[:, 0, :], stats[:, 0, :]).then_inc(aggr_done, 1)
                    dve.wait_ge(aggr_done, j + 1)
                    V.tensor_copy(mean[:, bass.ds(j, 1)], mv[:, 0, 0:1]).then_inc(mv_ready, 1)
                    V.tensor_scalar(var_eps[:, bass.ds(j, 1)], mv[:, 0, 1:2], EPS, None, ALU.add).then_inc(mv_ready, 1)
                    dve.wait_ge(mv_ready, 2 * j + 2)
            dve.wait_ge(std_ready, 1)
            V.reciprocal(rstd[:, :], std[:, :]).then_inc(ln_ready, 1)
            dve.wait_ge(ln_ready, 1)

            def normalise(i):
                for b in range(2):
                    j = 2 * i + b
                    if before(i, 1):
                        dve.wait_ge(xt_mm, i)
                    V.tensor_scalar(xn[:, b, :], xs[:, bass.ds(j, 1), :].rearrange("p a d -> p (a d)"),
                                    mean[:, bass.ds(j, 1)], rstd[:, bass.ds(j, 1)],
                                    ALU.subtract, ALU.mult).then_inc(xn_ready, 1)

            def xn_low(i):
                dve.wait_ge(xh_ready, i + 1)
                V.tensor_tensor(xnl, psT[:, :].rearrange("p (b c t) -> p c b t", b=2, c=C), xnh,
                                ALU.subtract).then_inc(xl_ready, 1)

            def qk_low(i):
                for ps, parts, col, high, ready in ((psQ, qp, 0, qh_ready, ql_ready), (psK, kp, 2, kh_ready, kl_ready)):
                    dve.wait_ge(high, 2 * i + 2)
                    for m in range(C):
                        V.scalar_tensor_tensor(out=parts[:, 1, m, :], in0=ps[:, bass.ts(m, 2 * S)],
                                               scalar=qkbias[:, col + m:col + m + 1], in1=parts[:, 0, m, :],
                                               op0=ALU.add, op1=ALU.subtract).then_inc(ready, 1)

            def v_parts(i, p):
                dve.wait_ge(v_mm, i + 1)
                if before(i, 1):
                    dve.wait_ge(vh_ready, 2 * i)
                    dve.wait_ge(vl_ready, 2 * i)
                V.tensor_tensor(v32, psQ[:, :].rearrange("p (b d) -> p b d", b=2),
                                vbr.unsqueeze(1).to_broadcast([P, 2, D]), ALU.add).then_inc(v32_ready, 1)
                dve.wait_ge(v32_ready, i + 1)
                for b in range(2):
                    dve.wait_ge(vh_ready, 2 * i + b + 1)
                    V.scalar_tensor_tensor(out=vl[p][:, b, :, 0:HD], in0=v32[:, b, :].rearrange("p (h e) -> p h e", h=NH),
                                           scalar=nmask[:, bass.ds(2 * i + b, 1)], in1=vh[p][:, b, :, 0:HD],
                                           op0=ALU.mult, op1=ALU.subtract).then_inc(vl_ready, 1)

            def maxima(i, b):
                for k in range(NQ):
                    n = 4 * b + k
                    dve.wait_ge(s_mm, 8 * i + n + 1)
                    V.tensor_reduce(mx[:, b, bass.ts(k, QUAD)], pb[4 + n % 2][:, :].rearrange("p (h t) -> p h t", h=QUAD),
                                    AX.X, ALU.max).then_inc(mx_ready, 1)
                dve.wait_ge(mx_ready, 8 * i + 4 * b + 4)
                if before(i, 1):
                    dve.wait_ge(m_mm, 2 * i + b - 1)
                V.tensor_scalar(mclamp[:, b, :], mx[:, b, :], -MAX_CLAMP, MAX_CLAMP, ALU.max, ALU.min)\
                    .then_inc(mclamp_ready, 1)

            def prob_low(i, n):
                dve.wait_ge(prob_ready, 8 * i + n + 1)
                V.tensor_tensor(flat(prob_lo[n % 4]), flat(prob[n % 4]), words_high(flat(prob[n % 4])),
                                ALU.subtract).then_inc(prob_lo_ready, 1)

            def normalise_heads(i, b):
                dve.wait_ge(pv_mm, 8 * i + 4 * b + 4)
                o = psC[:, 0:NH * (HD + 1)].rearrange("p (h e) -> p h e", h=NH)
                V.tensor_scalar(den[:, b, :], o[:, :, HD], 1e-6, None, ALU.max).then_inc(den_ready, 1)
                dve.wait_ge(den_ready, 2 * i + b + 1)
                V.reciprocal(rden[:, b, :], den[:, b, :]).then_inc(rden_ready, 1)
                dve.wait_ge(rden_ready, 2 * i + b + 1)
                if before(i, 1):
                    dve.wait_ge(ot_mm, i)
                V.tensor_tensor(on[:, b, :].rearrange("p (h e) -> p h e", h=NH), o[:, :, 0:HD],
                                rden[:, b, :].unsqueeze(2).to_broadcast([P, NH, HD]), ALU.mult).then_inc(on_ready, 1)

            def out_low(i):
                dve.wait_ge(onh_ready, i + 1)
                V.tensor_tensor(flat(onl), psT[:, :], flat(onh), ALU.subtract).then_inc(onl_ready, 1)

            def residual(i):
                dve.wait_ge(o_mm, i + 1)
                dve.wait_ge(xb_ready, 2 * i + 2)
                for b in range(2):
                    xb = xs[:, bass.ds(2 * i + b, 1), :].rearrange("p a d -> p (a d)")
                    V.scalar_tensor_tensor(out=xb, in0=psK[:, bass.ts(b, D)], scalar=gates[:, 0:1], in1=xb,
                                           op0=ALU.mult, op1=ALU.add).then_inc(x1_ready, 1)

            normalise(0)
            xn_low(0)
            qk_low(0)
            v_parts(0, 0)
            normalise(1)

            def body(i, p, k):
                maxima(i, 0)
                if before(i, 1):
                    out_low(i - 1)
                maxima(i, 1)
                if upto(i, NPAIR - 2):
                    xn_low(i + 1)
                    qk_low(i + 1)
                    v_parts(i + 1, 1 - p)
                if before(i, 1):
                    residual(i - 1)
                if upto(i, NPAIR - 3):
                    normalise(i + 2)
                for n in range(4):
                    prob_low(i, n)
                prob_low(i, 4)
                normalise_heads(i, 0)
                for n in range(5, 8):
                    prob_low(i, n)
                normalise_heads(i, 1)

            pair_loop(dve, body)
            out_low(NPAIR - 1)
            residual(NPAIR - 1)
            dve.wait_ge(x1_ready, B)

            def row(j):
                return xs[:, bass.ds(j, 1), :].rearrange("p a d -> p (a d)")

            def make_rows(dst, j, made):
                V.tensor_scalar(dst, row(j), mean[:, bass.ds(j, 1)], rstd[:, bass.ds(j, 1)],
                                ALU.subtract, ALU.mult).then_inc(made, 1)

            def ln2_stats(j, p):
                V.bn_stats(stats[:, p, :], row(j)).then_inc(stats_done, 1)
                dve.wait_ge(stats_done, B + j + 1)
                dve.sem_inc(dve_passed, 1)
                V.bn_aggr(mv[:, p, :], stats[:, p, :]).then_inc(aggr_done, 1)
                dve.wait_ge(aggr_done, B + j + 1)
                V.tensor_scalar(var_eps[:, bass.ds(j, 1)], mv[:, p, 1:2], EPS, None, ALU.add).then_inc(var_ready, 1)
                V.tensor_copy(mean[:, bass.ds(j, 1)], mv[:, p, 0:1]).then_inc(mv_ready, 1)

            def ln2_rows(j, p):
                dve.wait_ge(ln2_std, j + 1)
                V.reciprocal(rstd[:, bass.ds(j, 1)], std[:, bass.ds(j, 1)]).then_inc(ln2_rstd, 1)
                dve.wait_ge(ln2_rstd, j + 1)
                dve.wait_ge(mv_ready, 2 * B + j + 1)
                if not (known(j) and j < 2):
                    dve.wait_ge(tr_mm, j - 1)
                make_rows(rows[p], j, rows_made)

            def split_low(r, p):
                dve.wait_ge(th_ready, r + 1)
                V.tensor_tensor(flat(xl[p]), pb[7 * p][:, 0:D], flat(xh[p]), ALU.subtract).then_inc(tl_ready, 1)

            lg = rt[:, 0]

            def logits(r, p):
                dve.wait_ge(router_mm, r + 1)
                V.tensor_tensor(lg[:, bass.ds(r, 1), :].rearrange("p a e -> p (a e)"), pb[2 + p][:, 0:E], ebr[:, :],
                                ALU.add).then_inc(logit_ready, 1)

            def router_tile(r, p, more):
                if more >= 1:
                    ln2_rows(r + 1, 1 - p)
                if more >= 2:
                    ln2_stats(r + 2, p)
                split_low(r, p)
                logits(r, p)

            ln2_stats(0, 0)
            ln2_stats(1, 1)
            ln2_rows(0, 0)
            router_tile(0, 0, 2)
            router_tile(1, 1, 2)
            with dve.Fori(1, B // 2 - 1) as k:
                router_tile(2 * k, 0, 2)
                router_tile(2 * k + 1, 1, 2)
            router_tile(B - 2, 0, 1)
            router_tile(B - 1, 1, 0)
            dve.wait_ge(logit_ready, B)
            dve.wait_ge(route_const, 5)

            step = [0]

            def link(ins):
                step[0] += 1
                ins.then_inc(route, 1)
                dve.wait_ge(route, step[0])
                return step[0]

            ie = iota_e.unsqueeze(1).to_broadcast([P, B, E])

            def over_e(a):
                return a.unsqueeze(2).to_broadcast([P, B, E])

            src = lg
            for k in range(2):
                best, sel = sm[:, 2 * k], sm[:, 2 * k + 1]
                ge, hot = rt[:, 1], rt[:, 2 + k]
                link(V.tensor_reduce(best, src, AX.X, ALU.max))
                link(V.tensor_tensor(ge, src, over_e(best), ALU.is_ge))
                link(V.scalar_tensor_tensor(out=ge, in0=ge, scalar=-float(E), in1=ie, op0=ALU.mult, op1=ALU.add))
                link(V.tensor_reduce(sel, ge, AX.X, ALU.min))
                link(V.tensor_scalar(sel, sel, float(E), None, ALU.add))
                link(V.tensor_tensor(hot, ie, over_e(sel), ALU.is_equal))
                if k == 0:
                    link(V.scalar_tensor_tensor(out=rt[:, 4], in0=hot, scalar=-3.0e38, in1=lg, op0=ALU.mult, op1=ALU.add))
                    src = rt[:, 4]
            assert link(V.tensor_tensor(pick, rt[:, 2], rt[:, 3], ALU.add)) == PICK_STEP
            assert link(V.tensor_tensor(sm[:, 4], sm[:, 2], sm[:, 0], ALU.subtract)) == EXP_STEP
            dve.wait_ge(rank_mm, 1)
            a, bb = rt[:, 5], rt[:, 6]
            tot = rt[:, 7]
            link(V.tensor_copy(flat(tot), psR[:, B * E:]))
            link(V.tensor_copy(flat(a), psR[:, B * E:]))
            sh = 1
            while sh < B:
                V.tensor_copy(bb[:, 0:sh, :], a[:, 0:sh, :]).then_inc(route, 1)
                step[0] += 1
                link(V.tensor_tensor(bb[:, sh:, :], a[:, sh:, :], a[:, 0:B - sh, :], ALU.add))
                a, bb = bb, a
                sh *= 2
            link(V.tensor_scalar(cnt[:, 0], a[:, B - 1, :], float(P - 1), None, ALU.add))
            link(V.tensor_tensor(a, a, tot, ALU.subtract))
            link(V.tensor_copy(cnt_i, cnt[:, 0]))
            link(V.tensor_scalar(cnt_i, cnt_i, 7, None, ALU.logical_shift_right))
            link(V.tensor_copy(cnt[:, 1], cnt_i))
            ca, cb = cnt[:, 1], cnt[:, 2]
            link(V.tensor_copy(cnt[:, 3], cnt[:, 1]))
            ca = cnt[:, 3]
            sh = 1
            while sh < E:
                V.tensor_copy(cb[:, 0:sh], ca[:, 0:sh]).then_inc(route, 1)
                step[0] += 1
                link(V.tensor_tensor(cb[:, sh:], ca[:, sh:], ca[:, 0:E - sh], ALU.add))
                ca, cb = cb, ca
                sh *= 2
            link(V.tensor_tensor(cnt[:, 4], ca, cnt[:, 1], ALU.subtract))
            link(V.tensor_scalar(cnt[:, 5], cnt[:, 4], float(P), None, ALU.mult))
            link(V.tensor_tensor(a, a, cnt[:, 5].unsqueeze(1).to_broadcast([P, B, E]), ALU.add))
            link(V.tensor_tensor(flat(a), flat(a), psR[:, 0:B * E], ALU.add))
            for k in range(2):
                link(V.tensor_tensor(rt[:, 8], rt[:, 2 + k], a, ALU.mult))
                link(V.tensor_reduce(sm[:, 6 + k], rt[:, 8], AX.X, ALU.add))
                link(V.tensor_copy(slots[:, k, :], sm[:, 6 + k]))
            link(V.tensor_tensor(te_f, iota_t.unsqueeze(2).to_broadcast([P, SLOT_TILES, E]),
                                 ca.unsqueeze(1).to_broadcast([P, SLOT_TILES, E]), ALU.is_ge))
            link(V.tensor_reduce(te_s, te_f, AX.X, ALU.add))
            link(V.tensor_scalar(te_s, te_s, float(E - 1), float(NSH), ALU.min, ALU.add))
            link(V.tensor_scalar(te_s, te_s, float(3 * 2 * CHUNK), None, ALU.mult))
            assert link(V.tensor_copy(te, te_s)) == ROUTE_STEPS
            dve.wait_ge(exp_ready, 1)
            link(V.tensor_scalar(sm[:, 8], sm[:, 5], 1.0, None, ALU.add))
            link(V.reciprocal(sm[:, 9], sm[:, 8]))
            link(V.tensor_scalar(sm[:, 10], sm[:, 9], gates[:, 1:2], None, ALU.mult))
            link(V.tensor_tensor(sm[:, 11], sm[:, 10], sm[:, 5], ALU.mult))

            def shared_rows(r, p, j):
                dve.wait_ge(tr_mm, r - 1)
                make_rows(rows[p], j, rows_made)

            def scatter_rows(j, p, half):
                if not (known(half) and half < 1):
                    dve.wait_ge(scattered[p], 32 * half)
                make_rows(srow[p], j, srow_made)

            def combine(n, j, p, half):
                dve.wait_ge(gathered[p], 32 * (half + 1))
                V.scalar_tensor_tensor(out=row(j), in0=yg[p][:, 0, :], scalar=sm[:, 10, bass.ds(j, 1)], in1=row(j),
                                       op0=ALU.mult, op1=ALU.add).then_inc(comb_a, 1)
                dve.wait_ge(comb_a, n + 1)
                V.scalar_tensor_tensor(out=row(j), in0=yg[p][:, 1, :], scalar=sm[:, 11, bass.ds(j, 1)], in1=row(j),
                                       op0=ALU.mult, op1=ALU.add).then_inc(comb_b, 1)

            def add_shared(j, p):
                V.scalar_tensor_tensor(out=row(j), in0=pb[1 + 5 * p][:, 0:D], scalar=gates[:, 1:2], in1=row(j),
                                       op0=ALU.mult, op1=ALU.add).then_inc(y_added, 1)

            shared_rows(R1, 0, 0)
            shared_rows(R1 + 1, 1, 1)
            split_low(R1, 0)

            def body(r, p, sect, prev, nxt, k):
                for j, (u, first, last) in enumerate(steps(r, sect)):
                    q = p if sect == "E" else j
                    dve.wait_ge(h3_mm, u + 1)
                    dve.wait_ge(sil_ready, u + 1)
                    if not (known(u) and u < 2):
                        dve.wait_ge(y_mm, u - 1)
                    V.tensor_tensor(hid[q], sil[q], pb[3 + 2 * q][:, :], ALU.mult).then_inc(hid_ready, 1)
                    if last and nxt is not None:
                        split_low(r + 1, 1 - p)
                    dve.wait_ge(hid_ready, u + 1)
                    V.tensor_tensor(hlo[q], hid[q], words_high(hid[q]), ALU.subtract).then_inc(hlo_ready, 1)
                    if first and prev in ("1", "2"):
                        dve.wait_ge(y_mm, u)
                        add_shared(r - 1 - R1 if prev == "1" else r - 1 - R2 + HALF, 1 - p)
                    if sect == "1" and j == 0:
                        scatter_rows(2 * r - 2 * R1, 0, r - R1)
                        scatter_rows(2 * r - (2 * R1 - 1), 1, r - R1)
                    if last and sect == "1" and not (known(r) and r + 2 >= RE):
                        shared_rows(r + 2, p, r + 2 - R1)
                    if sect == "E" and known(r) and r + 2 >= R2:
                        shared_rows(r + 2, p, r + 2 - R2 + HALF)
                    if last and sect == "2" and not (known(r) and r + 2 >= RTOT):
                        shared_rows(r + 2, p, r + 2 - R2 + HALF)
                if sect == "2":
                    m = r - R2
                    if known(r) and r == R2:
                        combine(0, 0, 0, 0)
                    else:
                        combine(2 * m - 1, m, 1, m - 1)
                        dve.wait_ge(y_added, m + HALF)
                        combine(2 * m, m + HALF - 1, 0, m)

            moe_loop(dve, body)
            dve.wait_ge(y_mm, UTOT)
            add_shared(B - 1, 1)
            dve.wait_ge(y_added, B)
            combine(B - 1, B - 1, 1, HALF - 1)


def kernel(**inputs):
    import numpy as np
    import concourse.bacc as bacc
    from concourse.bass_utils import run_bass_kernel_spmd

    a = {k: np.asarray(v) for k, v in inputs.items()}
    con = np.ascontiguousarray

    def chunked(w):
        k, n = w.shape[-2:]
        w = w.reshape(*w.shape[:-2], k // P, P, n)
        return con(np.moveaxis(w, -2, -3)).reshape(*w.shape[:-3], P, (k // P) * n)

    def transposed(w):
        return np.swapaxes(w, -1, -2)

    aw = [chunked(transposed(a[f"L0_xattn_{k}_w"])) for k in "qkvo"]
    w1, w3, w2 = (np.concatenate([a[f"L0_ffn_s{k}"], a[f"L0_ffn_{k}"]]) for k in ("w1", "w3", "w2"))
    wall = np.stack([chunked(transposed(w)) for w in (w1, w3, w2)], axis=1).reshape(NCHUNK, P, CHUNK)
    fside = a["fside_1x16xSxS2_0"][0]

    def by_row(w):
        w = w.transpose(1, 0, 2).reshape(S, 2, CHUNK)
        return con(w.transpose(1, 0, 2))

    mask = a["mask_BxS2_bk0"]
    arrays = {
        "x": con(a["x"]),
        "ctxT": con(a["ctx_1024"].reshape(B * S, D).T),
        "bias_q": by_row(fside),
        "bias_t": by_row(transposed(fside)),
        "mask": con(mask),
        "maskT": con(mask.T),
        "g_att": con(a["g_xattn"]),
        "g_ffn": con(a["g_ffn"]),
        "attw": con(np.stack([np.concatenate(aw[0:2], axis=1), np.concatenate(aw[2:4], axis=1)])),
        "qkb": con(np.stack([a["L0_xattn_q_b"], a["L0_xattn_k_b"]]).reshape(2 * C, P).T),
        "vb": con(a["L0_xattn_v_b"]),
        "ob": con(a["L0_xattn_o_b"]),
        "rw": con(a["L0_ffn_router_w"].T),
        "eb": con(a["L0_ffn_expert_bias"]),
        "wall": con(wall),
    }
    nc = bacc.Bacc("TRN2", target_bir_lowering=False, num_devices=1)
    args = {k: nc.dram_tensor(k, v.shape, mybir.dt.from_np(v.dtype), kind="ExternalInput").ap()
            for k, v in arrays.items()}
    args["out"] = nc.dram_tensor("out", (B, S, D), F32, kind="ExternalOutput").ap()
    build(nc, **args)
    return run_bass_kernel_spmd(nc, [arrays], core_ids=[0]).results[0]["out"]
```

```python
from contextlib import ExitStack

import concourse.bass as bass
from concourse import mybir

ALU = mybir.AluOpType
ACT = mybir.ActivationFunctionType
AX = mybir.AxisListType
F32 = mybir.dt.float32
F16 = mybir.dt.float16
BF16 = mybir.dt.bfloat16
I32 = mybir.dt.int32
U8 = mybir.dt.uint8

P = 128
B, S, D = 32, 128, 256
NH, HD = 16, 16
E, NSH, HID = 8, 2, 512
C = D // P
KC = HID // P
NPAIR = B // 2
QUAD = 4
NQ = NH // QUAD
SLOT_TILES = 72
HALF = B // 2
CHUNK = 1024
NCHUNK = 3 * (NSH + E)
PRE_CHUNKS = 0
ATT_CHUNKS = NPAIR
EPS = 1e-5
FRONT = 6
ZERO_DMAS = NPAIR - 4
ZERO_ROWS = SLOT_TILES // ZERO_DMAS
LATE_CHUNKS = NCHUNK - NPAIR
CONSTS = 9
PICK_STEP, EXP_STEP, RANK_STEP, ROUTE_STEPS = 14, 15, 43, 54
MASK_Q, MASK_K = 60000.0, -60000.0
MAX_CLAMP = 60000.0
ROW_MASK, ROW_MAX = 64, 96


def build(nc, x, ctxT, bias_q, bias_t, mask, maskT, g_att, g_ffn, attw, qkb, vb, ob,
          rw, eb, wall, out):
    es = ExitStack()
    with es:
        def sb(name, shape, dt):
            return es.enter_context(nc.sbuf_tensor(name, shape, dt))

        def sem(name):
            return es.enter_context(nc.semaphore(name))

        xs = sb("xs", [P, B, D], F32)
        stage = sb("stage", [P, 2, CHUNK], F32)
        ident = sb("ident", [P, P], F32)
        ident16 = sb("ident16", [P, P], F16)
        stats = sb("stats", [P, B, 6], F32)
        ln_tmp = sb("ln_tmp", [P, 2, B], F32)
        zeros = sb("zeros", [P, D], F32)
        mean = sb("mean", [P, B], F32)
        rstd = sb("rstd", [P, B], F32)
        var_eps = sb("var_eps", [P, B], F32)
        std = sb("std", [P, B], F32)
        nmr = sb("nmr", [P, B], F32)
        gates = sb("gates", [P, 2], F32)
        graw = sb("graw", [P, 2], F32)
        rw_f = sb("rw_f", [P, C, E], F32)
        rwh = sb("rwh", [P, C, E], F16)
        rwl = sb("rwl", [P, C, E], F16)
        ebr = sb("ebr", [P, E], F32)

        WBYTES = NCHUNK * CHUNK * 4
        ATT_AT = (PRE_CHUNKS + ATT_CHUNKS) * CHUNK * 4
        ARENA = 162 * 1024
        arena = sb("arena", [P, ARENA // 2], F16)
        cursor = [0]

        def carve(shape, dt, size):
            n = size
            for k in shape:
                n *= k
            a = arena[:, cursor[0] // 2:(cursor[0] + n) // 2]
            cursor[0] += -(-n // 32) * 32
            assert cursor[0] <= ARENA, cursor[0]
            if dt != F16:
                a = a.bitcast(dt)
            if len(shape) > 1:
                names = "abcd"[:len(shape)]
                a = a.rearrange(f"p ({' '.join(names)}) -> p {' '.join(names)}",
                                **{m: k for m, k in zip(names, shape)})
            return a

        wparts = arena[:, 0:WBYTES // 2]

        cursor[0] = ATT_AT
        bq = carve([NH, S], F16, 2)
        bth = carve([NH, S], F16, 2)
        btl = carve([NH, S], F16, 2)
        QS = [carve([NH, 2 * S], F16, 2) for _ in range(2)]
        KS = [carve([NH, 2 * S], F16, 2) for _ in range(2)]
        prob_all = carve([4 * QUAD, S], F32, 4)
        prob = [prob_all[:, QUAD * k:QUAD * k + QUAD, :] for k in range(4)]
        prob_lo = [carve([QUAD, S], F16, 2) for _ in range(4)]
        xn = carve([2, D], F32, 4)
        xnh = carve([C, 2, S], F16, 2)
        xnl = carve([C, 2, S], F16, 2)
        cf = [carve([C, 2, S], F32, 4) for _ in range(2)]
        ch = carve([C, 2, S], F16, 2)
        cl = carve([C, 2, S], F16, 2)
        qp = carve([2, C, 2 * S], F16, 2)
        kp = carve([2, C, 2 * S], F16, 2)
        v32 = carve([2, D], F32, 4)
        vh = [carve([2, NH, HD + 1], F16, 2) for _ in range(2)]
        vl = [carve([2, NH, HD + 1], F16, 2) for _ in range(2)]
        mx = carve([2, NH], F32, 4)
        mclamp = carve([2, NH], F32, 4)
        mrow = carve([2, S], F16, 2)
        den = carve([2, NH], F32, 4)
        rden = carve([2, NH], F32, 4)
        on = carve([2, D], F32, 4)
        onh = carve([2 * C, S], F16, 2)
        onl = carve([2 * C, S], F16, 2)
        awh = carve([4, C, D], F16, 2)
        awl = carve([4, C, D], F16, 2)
        qkbias = carve([4], F32, 4)
        vbr = carve([D], F32, 4)
        obr = carve([D], F32, 4)
        nmask = carve([B], F32, 4)
        mraw = carve([B], U8, 1)
        mrow_raw = carve([S], U8, 1)
        mrow16 = carve([S], F16, 2)

        cursor[0] = WBYTES
        rows = [carve([D], F32, 4) for _ in range(2)]
        xh = [carve([C, P], F16, 2) for _ in range(2)]
        xl = [carve([C, P], F16, 2) for _ in range(2)]
        sil = [carve([HID], F32, 4) for _ in range(2)]
        hid = [carve([HID], F32, 4) for _ in range(2)]
        hlo = [carve([HID], F16, 2) for _ in range(2)]
        ysb = [carve([D], F32, 4) for _ in range(2)]
        srow = [carve([D], F32, 4) for _ in range(2)]
        yg = [carve([2, D], F32, 4) for _ in range(2)]
        rt = carve([12, B, E], F32, 4)
        pick = carve([B, E], F16, 2)
        tri = carve([P], F16, 2)
        ones = carve([P], F16, 2)
        iota_e = carve([E], F32, 4)
        iota_t = carve([SLOT_TILES], F32, 4)
        sm = carve([12, B], F32, 4)
        cnt = carve([8, E], F32, 4)
        cnt_i = carve([E], I32, 4)
        slots = carve([2, B], I32, 4)
        slot_idx = [carve([2], I32, 4) for _ in range(2)]
        te_f = carve([SLOT_TILES, E], F32, 4)
        te_s = carve([SLOT_TILES], F32, 4)
        te = carve([SLOT_TILES], I32, 4)

        pb = [es.enter_context(nc.psum_tensor(f"bank{i}", [P, 512], F32)) for i in range(8)]
        psT, psQ, psK, psC = pb[0], pb[1], pb[2], pb[3]
        psR = pb[6]

        q_scr = nc.dram_tensor("q_scr", (2, 2, D, 2 * S), F16).ap()
        k_scr = nc.dram_tensor("k_scr", (2, 2, D, 2 * S), F16).ap()
        m_scr = nc.dram_tensor("m_scr", (B, S), F16).ap()
        xslots = nc.dram_tensor("xslots", (SLOT_TILES * P, D), F32).ap()
        yslots = nc.dram_tensor("yslots", (SLOT_TILES * P, D), F32).ap()
        ysv = yslots.rearrange("(t p) d -> t p d", p=P)

        x_in = [sem(f"x_in{q}") for q in range(4)]
        const_in = sem("const_in")
        const_rows = sem("const_rows")
        idents = sem("idents")
        stage_in = [sem("stage_in0"), sem("stage_in1")]
        stage_hi = sem("stage_hi")
        stage_lo = sem("stage_lo")
        setup_dve = sem("setup_dve")
        setup_act = sem("setup_act")
        mask_out = sem("mask_out")
        zero_out = sem("zero_out")
        zeroed = sem("zeroed")
        stats_done = sem("stats_done")
        ln_step = sem("ln_step")
        ln_var = sem("ln_var")
        ln_std = sem("ln_std")
        ln_ready = sem("ln_ready")

        ctx_in = [sem("ctx_in0"), sem("ctx_in1")]
        xn_ready = sem("xn_ready")
        xt_mm = sem("xt_mm")
        xh_ready = sem("xh_ready")
        xl_ready = sem("xl_ready")
        ch_ready = sem("ch_ready")
        cl_ready = sem("cl_ready")
        q_mm = sem("q_mm")
        k_mm = sem("k_mm")
        v_mm = sem("v_mm")
        qh_ready = sem("qh_ready")
        ql_ready = sem("ql_ready")
        kh_ready = sem("kh_ready")
        kl_ready = sem("kl_ready")
        v32_ready = sem("v32_ready")
        vh_ready = sem("vh_ready")
        vl_ready = sem("vl_ready")
        vmask_ready = sem("vmask_ready")
        q_out = sem("q_out")
        k_out = sem("k_out")
        qs_in = [sem("qs_in0"), sem("qs_in1")]
        ks_in = [sem("ks_in0"), sem("ks_in1")]
        s_mm = sem("s_mm")
        mx_ready = sem("mx_ready")
        mclamp_ready = sem("mclamp_ready")
        m_mm = sem("m_mm")
        mrow_ready = sem("mrow_ready")
        m_in = [sem("m_in0"), sem("m_in1")]
        st_mm = sem("st_mm")
        prob_ready = sem("prob_ready")
        prob_lo_ready = sem("prob_lo_ready")
        pv_mm = sem("pv_mm")
        den_ready = sem("den_ready")
        rden_ready = sem("rden_ready")
        on_ready = sem("on_ready")
        ot_mm = sem("ot_mm")
        onh_ready = sem("onh_ready")
        onl_ready = sem("onl_ready")
        o_mm = sem("o_mm")
        xb_ready = sem("xb_ready")
        x1_ready = sem("x1_ready")

        block = es.enter_context(nc.Block())

        def words_high(a):
            return a.bitcast(BF16).rearrange("p (n two) -> p n two", two=2)[:, :, 1]

        def flat(a):
            return a.rearrange("p a b -> p (a b)")

        bq_f, bth_f, btl_f = flat(bq), flat(bth), flat(btl)
        awh_f = awh.rearrange("p a b c -> p (a b c)")
        awl_f = awl.rearrange("p a b c -> p (a b c)")

        def front_parts(k):
            if k < 2:
                return awh_f[:, bass.ts(k, CHUNK)], awl_f[:, bass.ts(k, CHUNK)]
            if k < 4:
                return bq_f[:, bass.ts(k - 2, CHUNK)], None
            return bth_f[:, bass.ts(k - 4, CHUNK)], btl_f[:, bass.ts(k - 4, CHUNK)]

        def weight_parts(w):
            return (wparts[:, bass.ds(w * (2 * CHUNK), CHUNK)],
                    wparts[:, bass.ds(w * (2 * CHUNK) + CHUNK, CHUNK)])

        def lows(n):
            return (n if n <= 2 else 2 if n <= 4 else n - 2) if isinstance(n, int) else n - 2

        def act_high(act, k, slot, dst):
            act.wait_ge(stage_in[slot], k)
            nc.scalar.activation(dst, stage[:, slot, :], ACT.Copy).then_inc(stage_hi, 1)

        def pool_low(pool, n, slot, hi, lo):
            pool.wait_ge(stage_hi, n)
            nc.gpsimd.tensor_tensor(lo, stage[:, slot, :], hi, ALU.subtract).then_inc(stage_lo, 1)


        def pair_loop(eng, body):
            body(0, 0, 0)
            body(1, 1, 0)
            with eng.Fori(1, NPAIR // 2 - 1) as k:
                body(2 * k, 0, k)
                body(2 * k + 1, 1, k)
            body(NPAIR - 2, 0, NPAIR // 2 - 1)
            body(NPAIR - 1, 1, NPAIR // 2 - 1)

        def known(i):
            return isinstance(i, int)

        def before(i, n):
            return i >= n if known(i) else True

        def upto(i, n):
            return i <= n if known(i) else True

        R1, RE, R2 = B, B + HALF, B + HALF + SLOT_TILES
        RTOT = R2 + (B - HALF)
        U1, UE, U2 = 0, 2 * HALF, 2 * HALF + SLOT_TILES
        UTOT = U2 + 2 * (B - HALF)

        route_const = sem("route_const")
        rows_made = sem("rows_made")
        rows_in = [sem("rows_in0"), sem("rows_in1")]
        tr_mm = sem("tr_mm")
        th_ready = sem("th_ready")
        tl_ready = sem("tl_ready")
        router_mm = sem("router_mm")
        logit_ready = sem("logit_ready")
        route = sem("route")
        rank_mm = sem("rank_mm")
        exp_ready = sem("exp_ready")
        idx_ready = sem("idx_ready")
        dve_passed = sem("dve_passed")
        pool_passed = sem("pool_passed")
        pe_passed = sem("pe_passed")
        sp_passed = sem("sp_passed")
        srow_made = sem("srow_made")
        scattered = [sem("scattered0"), sem("scattered1")]
        h1_mm = sem("h1_mm")
        h3_mm = sem("h3_mm")
        sil_ready = sem("sil_ready")
        hid_ready = sem("hid_ready")
        hlo_ready = sem("hlo_ready")
        y_mm = sem("y_mm")
        y_added = sem("y_added")
        y_copied = sem("y_copied")
        y_out = [sem("y_out0"), sem("y_out1")]
        gathered = [sem("gathered0"), sem("gathered1")]
        comb_a = sem("comb_a")
        comb_b = sem("comb_b")
        res_out = sem("res_out")
        router_rows = sem("router_rows")

        LN_GROUPS = ((0, 8), (8, B - 8))

        def section(r):
            return "R" if r < R1 else "1" if r < RE else "E" if r < R2 else "2"

        def last_unit(r, sect=None):
            sect = sect or section(r)
            return {"1": 2 * (r - R1) + 1, "E": r - RE + UE, "2": 2 * (r - R2) + 1 + U2}[sect]

        def steps(r, sect):
            if sect == "E":
                return [(r - RE + UE, 1, 1)]
            u = 2 * (r - R1) if sect == "1" else 2 * (r - R2) + U2
            return [(u, 1, 0), (u + 1, 0, 1)]

        def moe_loop(eng, body):
            for a, b, sect, prev, nxt in ((R1, RE, "1", None, "E"), (RE, R2, "E", "1", "2"),
                                          (R2, RTOT, "2", "E", None)):
                n = (b - a) // 2
                body(a, 0, sect, prev, sect, 0)
                body(a + 1, 1, sect, sect, sect, 0)
                with eng.Fori(1, n - 1) as k:
                    body(2 * k + a, 0, sect, sect, sect, k)
                    body(2 * k + (a + 1), 1, sect, sect, sect, k)
                body(b - 2, 0, sect, sect, sect, n - 1)
                body(b - 1, 1, sect, sect, nxt, n - 1)

        @block.sync
        def _(sp):
            def wait_stage_slot(n):
                sp.wait_ge(stage_hi, n - 1)
                sp.sem_inc(sp_passed, 1)
                sp.wait_ge(stage_lo, lows(n - 1))

            def load_stage(slot, src):
                sp.dma_start(stage[:, slot, :], src).then_inc(stage_in[slot], 16)

            xv = x.rearrange("b s d -> s b d")

            def load_x(q):
                sp.dma_start(xs[:, 8 * q:8 * q + 8, :], xv[:, 8 * q:8 * q + 8, :]).then_inc(x_in[q], 16)

            cv = ctxT.rearrange("(c p) t -> p c t", p=P)

            def load_ctx(i, p):
                sp.dma_start(cf[p].rearrange("p c b t -> p c (b t)"),
                             cv[:, :, bass.ds(i * (2 * S), 2 * S)]).then_inc(ctx_in[p], 16)

            def front_src(k):
                if k < 2:
                    return attw[k]
                return (bias_q if k < 4 else bias_t)[k % 2]

            load_x(0)
            load_stage(0, front_src(0))
            load_stage(1, front_src(1))
            load_ctx(0, 0)
            load_ctx(1, 1)
            sp.wait_ge(setup_dve, 1)
            sp.dma_start(m_scr, mrow16[0:B, :]).then_inc(mask_out, 16)
            for k in range(2, FRONT):
                wait_stage_slot(k)
                load_stage(k % 2, front_src(k))
                if k < 5:
                    load_x(k - 1)
            sp.wait_ge(mask_out, 16)

            def parts_out(i, p):
                for scr, parts, ready, sent in ((q_scr, qp, ql_ready, q_out), (k_scr, kp, kl_ready, k_out)):
                    sp.wait_ge(ready, 2 * i + 2)
                    sp.dma_start(scr[p].rearrange("s (c p) t -> p s c t", p=P), parts).then_inc(sent, 16)

            def stack(i, p):
                if before(i, 2):
                    sp.wait_ge(st_mm, 8 * i - 8)
                for scr, dst, sent, arrived, order in ((q_scr, QS[p], q_out, qs_in[p], (0, 0, 1)),
                                                       (k_scr, KS[p], k_out, ks_in[p], (0, 1, 0))):
                    sp.wait_ge(sent, 16 * i + 16)
                    for j, part in enumerate(order):
                        sp.dma_start(dst[HD * j:HD * j + HD],
                                     scr[p, part].rearrange("(h d) t -> d h t", d=HD)).then_inc(arrived, 16)
                row = m_scr[bass.ds(2 * i, 2), :].rearrange("b t -> (b t)").partition_broadcast(NH)
                sp.dma_start(KS[p][ROW_MASK:ROW_MASK + 1], row.unsqueeze(0)).then_inc(ks_in[p], 16)

            def max_row(i, p, b):
                sp.wait_ge(mrow_ready, 2 * i + b + 1)
                sp.dma_start(QS[p][ROW_MAX:ROW_MAX + 1, :, b * S:b * S + S], mrow[0:NH, b, :]).then_inc(m_in[b], 16)

            sp.wait_ge(zeroed, 5)
            sp.wait_ge(const_rows, 2)
            parts_out(0, 0)
            stack(0, 0)

            def body(i, p, k):
                if upto(i, NPAIR - 3):
                    sp.wait_ge(ch_ready, i + 1)
                    sp.wait_ge(cl_ready, i + 1)
                    load_ctx(i + 2, p)
                max_row(i, p, 0)
                if upto(i, NPAIR - 2):
                    parts_out(i + 1, 1 - p)
                max_row(i, p, 1)
                if upto(i, NPAIR - 2):
                    stack(i + 1, 1 - p)
                wait_stage_slot(FRONT + PRE_CHUNKS + i)
                load_stage(p, wall[bass.ds(i + PRE_CHUNKS, 1)].rearrange("a p n -> (a p) n"))

            pair_loop(sp, body)

            for w in range(PRE_CHUNKS + ATT_CHUNKS, NCHUNK):
                wait_stage_slot(FRONT + w)
                load_stage(w % 2, wall[w])

            for s in range(2):
                sp.wait_ge(scattered[s], 16 * B)
            xsv = xslots.rearrange("(t p) d -> t p d", p=P)

            def load_rows(t, p):
                sp.wait_ge(tr_mm, t + RE - 1)
                sp.dma_start(rows[p], xsv[bass.ds(t, 1)].rearrange("a p d -> (a p) d")).then_inc(rows_in[p], 16)

            with sp.Fori(0, SLOT_TILES // 2) as k:
                load_rows(2 * k, 0)
                load_rows(2 * k + 1, 1)

            def store_out(n, j):
                sp.wait_ge(comb_b, n + 1)
                sp.dma_start(out[bass.ds(j, 1)].rearrange("a s d -> (a s) d"), xs[:, bass.ds(j, 1), :].rearrange("p a d -> p (a d)")).then_inc(res_out, 16)

            store_out(0, 0)
            with sp.Fori(1, HALF) as k:
                store_out(2 * k - 1, k)
                store_out(2 * k, k + HALF - 1)
            store_out(B - 1, B - 1)
            sp.wait_ge(res_out, 16 * B)

        @block.gpsimd
        def _(pool):
            nc.gpsimd.memset(ident[:, :], 0.0).then_inc(idents, 1)
            nc.gpsimd.memset(ident16[:, :], 0.0).then_inc(idents, 1)
            pool.wait_ge(idents, 2)
            nc.gpsimd.affine_select(out=ident[:, :], in_=ident[:, :], compare_op=ALU.not_equal, fill=1.0,
                                    base=0, pattern=[[-1, P]], channel_multiplier=1).then_inc(idents, 1)
            nc.gpsimd.affine_select(out=ident16[:, :], in_=ident16[:, :], compare_op=ALU.not_equal, fill=1.0,
                                    base=0, pattern=[[-1, P]], channel_multiplier=1).then_inc(idents, 1)
            for t in KS:
                nc.gpsimd.memset(flat(t), 1.0).then_inc(const_rows, 1)
            for t in vl:
                nc.gpsimd.memset(t.rearrange("p b h e -> p (b h e)"), 0.0).then_inc(const_rows, 1)
            def context_low(i, p):
                pool.wait_ge(ch_ready, i + 1)
                if before(i, 1):
                    pool.wait_ge(v_mm, i)
                nc.gpsimd.tensor_tensor(cl.rearrange("p c b t -> p (c b t)"), cf[p].rearrange("p c b t -> p (c b t)"),
                                        ch.rearrange("p c b t -> p (c b t)"), ALU.subtract).then_inc(cl_ready, 1)

            for k in range(FRONT + PRE_CHUNKS):
                hi, lo = front_parts(k) if k < FRONT else weight_parts(k - FRONT)
                if lo is not None:
                    pool_low(pool, k + 1, k % 2, hi, lo)
                if k == 1:
                    context_low(0, 0)

            def mask_columns(i, p):
                if before(i, 2):
                    pool.wait_ge(pv_mm, 8 * i - 8)
                for b in range(2):
                    nc.gpsimd.tensor_copy(vh[p][:, b, :, HD], nmask[:, bass.ds(2 * i + b, 1)].to_broadcast([P, NH])).then_inc(vmask_ready, 1)

            def add_output_bias(i):
                pool.wait_ge(xn_ready, 2 * i + 2)
                for b in range(2):
                    xb = xs[:, bass.ds(2 * i + b, 1), :].rearrange("p a d -> p (a d)")
                    nc.gpsimd.tensor_tensor(xb, xb, obr, ALU.add).then_inc(xb_ready, 1)

            pool.wait_ge(setup_dve, 6)
            zv = xslots.rearrange("(n p r) d -> n p r d", p=P, r=ZERO_ROWS)
            pool.wait_ge(zeroed, 1)

            def zero_slots(n):
                pool.dma_start(zv[bass.ds(n, 1)].rearrange("n p r d -> (n p) r d"),
                               zeros[:, :].unsqueeze(1).to_broadcast([P, ZERO_ROWS, D])).then_inc(zero_out, 16)

            mask_columns(0, 0)

            def body(i, p, k):
                if upto(i, NPAIR - 2):
                    context_low(i + 1, 1 - p)
                add_output_bias(i)
                if upto(i, NPAIR - 2):
                    mask_columns(i + 1, 1 - p)
                hi, lo = weight_parts(i + PRE_CHUNKS)
                pool_low(pool, FRONT + PRE_CHUNKS + i + 1, p, hi, lo)
                if not known(i):
                    if p == 0:
                        zero_slots(2 * k - 2)
                    else:
                        zero_slots(2 * k - 1)

            pair_loop(pool, body)

            pool.wait_ge(x1_ready, B)
            nc.gpsimd.memset(tri, 1.0).then_inc(route_const, 1)
            nc.gpsimd.memset(ones, 1.0).then_inc(route_const, 1)
            nc.gpsimd.iota(iota_e, [[1, E]], base=0, channel_multiplier=0,
                           allow_small_or_imprecise_dtypes=True).then_inc(route_const, 1)
            nc.gpsimd.iota(iota_t, [[1, SLOT_TILES]], base=0, channel_multiplier=0,
                           allow_small_or_imprecise_dtypes=True).then_inc(route_const, 1)
            pool.wait_ge(route_const, 4)
            nc.gpsimd.affine_select(out=tri, in_=tri, compare_op=ALU.is_gt, fill=0.0, base=0,
                                    pattern=[[1, P]], channel_multiplier=-1).then_inc(route_const, 1)
            pool.wait_ge(route, ROUTE_STEPS)
            pool.wait_ge(zero_out, 16 * ZERO_DMAS)

            def indices(n, j, p, users, used):
                if used is not None:
                    pool.wait_ge(users[p], used)
                nc.gpsimd.tensor_copy(slot_idx[p], slots[:, :, bass.ds(j, 1)].rearrange("p s a -> p (s a)"))\
                    .then_inc(idx_ready, 1)
                pool.wait_ge(idx_ready, n + 1)
                pool.sem_inc(pool_passed, 1)

            def scatter(j, p, used):
                pool.wait_ge(srow_made, j + 1)
                indices(j, j, p, scattered, used)
                for s in range(2):
                    nc.gpsimd.indirect_dma_start(
                        xslots, bass.IndirectOffsetOnAxis(ap=slot_idx[p][:, s:s + 1], axis=0),
                        srow[p], None).then_inc(scattered[p], 16)

            def late_chunk(m, p):
                hi, lo = weight_parts(m + ATT_CHUNKS)
                pool_low(pool, m + (FRONT + ATT_CHUNKS + 1), p, hi, lo)

            late_chunk(0, 0)
            scatter(0, 0, None)
            scatter(1, 1, None)
            late_chunk(1, 1)
            scatter(2, 0, 32)
            scatter(3, 1, 32)
            with pool.Fori(1, LATE_CHUNKS // 2) as k:
                late_chunk(2 * k, 0)
                scatter(4 * k, 0, 64 * k)
                scatter(4 * k + 1, 1, 64 * k)
                late_chunk(2 * k + 1, 1)
                scatter(4 * k + 2, 0, 64 * k + 32)
                scatter(4 * k + 3, 1, 64 * k + 32)
            for j in range(2 * LATE_CHUNKS, B):
                scatter(j, j % 2, 32 * (j // 2))
            for s in range(2):
                pool.wait_ge(y_out[s], 16 * (SLOT_TILES // 2))

            def gather(n, j, p, half):
                if known(half) and half < 1:
                    indices(B + n, j, p, scattered, 16 * B)
                else:
                    pool.wait_ge(comb_b, n - 1)
                    indices(B + n, j, p, gathered, 32 * half)
                for s in range(2):
                    nc.gpsimd.indirect_dma_start(
                        yg[p][:, s, :], None, yslots,
                        bass.IndirectOffsetOnAxis(ap=slot_idx[p][:, s:s + 1], axis=0)).then_inc(gathered[p], 16)

            gather(0, 0, 0, 0)
            gather(1, 1, 1, 0)
            gather(2, HALF, 0, 1)
            with pool.Fori(2, HALF) as k:
                gather(2 * k - 1, k, 1, k - 1)
                gather(2 * k, k + HALF - 1, 0, k)
            gather(B - 1, B - 1, 1, HALF - 1)

        @block.scalar
        def _(act):
            for dst, src in ((graw[:, 0:1], g_att.partition_broadcast(P)), (graw[:, 1:2], g_ffn.partition_broadcast(P)),
                             (mrow_raw[0:B, :], mask), (qkbias, qkb), (mraw, maskT),
                             (vbr, vb.partition_broadcast(P)), (obr, ob.partition_broadcast(P)),
                             (rw_f[:, :, :], rw.rearrange("(c p) e -> p c e", p=P)), (ebr[:, :], eb.partition_broadcast(P))):
                act.dma_start(dst, src).then_inc(const_in, 16)
            act.wait_ge(const_in, 16 * CONSTS)
            nc.scalar.activation(gates[:, :], graw[:, :], ACT.Tanh).then_inc(setup_act, 1)
            nc.scalar.activation(rwh[:, :, :], rw_f[:, :, :], ACT.Copy).then_inc(setup_act, 1)
            def context_high(i, p, k):
                act.wait_ge(ctx_in[p], 16 * (k + 1))
                if before(i, 1):
                    act.wait_ge(v_mm, i)
                nc.scalar.activation(ch.rearrange("p c b t -> p (c b t)"), cf[p].rearrange("p c b t -> p (c b t)"),
                                     ACT.Copy).then_inc(ch_ready, 1)

            def xn_high(i):
                act.wait_ge(xt_mm, i + 1)
                if before(i, 1):
                    act.wait_ge(q_mm, i)
                nc.scalar.activation(xnh, psT[:, :].rearrange("p (b c t) -> p c b t", b=2, c=C),
                                     ACT.Copy).then_inc(xh_ready, 1)

            def qk_high(i):
                for ps, parts, col, mm, sent, ready in ((psQ, qp, 0, q_mm, q_out, qh_ready),
                                                        (psK, kp, 2, k_mm, k_out, kh_ready)):
                    act.wait_ge(mm, i + 1)
                    if before(i, 1):
                        act.wait_ge(sent, 16 * i)
                    for m in range(C):
                        nc.scalar.activation(parts[:, 0, m, :], ps[:, bass.ts(m, 2 * S)], ACT.Identity,
                                             bias=qkbias[:, col + m:col + m + 1]).then_inc(ready, 1)

            def v_high(i, p):
                act.wait_ge(v32_ready, i + 1)
                if before(i, 2):
                    act.wait_ge(pv_mm, 8 * i - 8)
                for b in range(2):
                    nc.scalar.activation(vh[p][:, b, :, 0:HD], v32[:, b, :].rearrange("p (h e) -> p h e", h=NH),
                                         ACT.Copy, scale=nmask[:, bass.ds(2 * i + b, 1)]).then_inc(vh_ready, 1)

            def max_row(i, b):
                act.wait_ge(m_mm, 2 * i + b + 1)
                if before(i, 1):
                    act.wait_ge(m_in[b], 16 * i)
                nc.scalar.activation(mrow[0:NH, b, :], psC[0:NH, 384:512], ACT.Copy, scale=-1.0).then_inc(mrow_ready, 1)

            def out_high(i):
                act.wait_ge(ot_mm, i + 1)
                if before(i, 1):
                    act.wait_ge(o_mm, i)
                nc.scalar.activation(flat(onh), psT[:, :], ACT.Copy).then_inc(onh_ready, 1)

            def take_roots(n, at, count):
                act.wait_ge(ln_var, n)
                nc.scalar.activation(std[:, at:at + count], var_eps[:, at:at + count], ACT.Sqrt).then_inc(ln_std, 1)

            def normalise(i, group):
                act.wait_ge(ln_ready, group)
                if before(i, 1):
                    act.wait_ge(xt_mm, i)
                for b in range(2):
                    nc.scalar.activation(xn[:, b, :], xs[:, bass.ds(2 * i + b, 1), :].rearrange("p a d -> p (a d)"),
                                         ACT.Identity, bias=nmr[:, bass.ds(2 * i + b, 1)],
                                         scale=rstd[:, bass.ds(2 * i + b, 1)]).then_inc(xn_ready, 1)

            for k in range(FRONT + PRE_CHUNKS):
                hi, lo = front_parts(k) if k < FRONT else weight_parts(k - FRONT)
                if k == 0:
                    act.wait_ge(setup_dve, 3)
                act_high(act, 16 * (k // 2 + 1), k % 2, hi)
                if k == 0:
                    take_roots(1, *LN_GROUPS[0])
                    normalise(0, 1)
                if k == 1:
                    context_high(0, 0, 0)
                    xn_high(0)
                    qk_high(0)
                    normalise(1, 1)
            v_high(0, 0)
            take_roots(2, *LN_GROUPS[1])
            context_high(1, 1, 0)

            def body(i, p, k):
                if before(i, 1):
                    out_high(i - 1)
                max_row(i, 0)
                if upto(i, NPAIR - 2):
                    xn_high(i + 1)
                if upto(i, NPAIR - 3):
                    normalise(i + 2, 2)
                if upto(i, NPAIR - 2):
                    qk_high(i + 1)
                max_row(i, 1)
                if upto(i, NPAIR - 2):
                    v_high(i + 1, 1 - p)
                for n in range(8):
                    act.wait_ge(st_mm, 8 * i + n + 1)
                    if before(i, 1) or n >= 4:
                        act.wait_ge(pv_mm, 8 * i + n - 3)
                    nc.scalar.activation(flat(prob[n % 4]), pb[6 + n % 2][:, :], ACT.Exp).then_inc(prob_ready, 1)
                if upto(i, NPAIR - 3):
                    context_high(i + 2, p, k + 1)
                act_high(act, 16 * ((FRONT + PRE_CHUNKS) // 2 + k + 1), p, weight_parts(i + PRE_CHUNKS)[0])

            pair_loop(act, body)
            out_high(NPAIR - 1)
            act.wait_ge(x1_ready, B)


            def split_high(r, p, sect=None):
                act.wait_ge(tr_mm, r + 1)
                if not (known(r) and r < 2):
                    if (sect or section(r - 2)) == "R":
                        act.wait_ge(router_mm, r - 1)
                    else:
                        act.wait_ge(h3_mm, last_unit(r - 2, sect) + 1)
                nc.scalar.activation(flat(xh[p]), pb[7 * p][:, 0:D], ACT.Copy).then_inc(th_ready, 1)

            def write_rows(r, p):
                if not (known(r) and r < 2):
                    act.wait_ge(tr_mm, r - 1)
                nc.scalar.activation(rows[p], xs[:, bass.ds(r, 1), :].rearrange("p a d -> p (a d)"), ACT.Identity,
                                     bias=nmr[:, bass.ds(r, 1)], scale=rstd[:, bass.ds(r, 1)]).then_inc(router_rows, 1)

            take_roots(3, 0, B)
            act.wait_ge(ln_ready, 3)
            write_rows(0, 0)
            write_rows(1, 1)
            split_high(0, 0)
            with act.Fori(1, B // 2) as k:
                write_rows(2 * k, 0)
                split_high(2 * k - 1, 1, "R")
                write_rows(2 * k + 1, 1)
                split_high(2 * k, 0, "R")
            split_high(B - 1, 1)
            act.wait_ge(route, EXP_STEP)
            nc.scalar.activation(sm[:, 5, :], sm[:, 4, :], ACT.Exp).then_inc(exp_ready, 1)
            split_high(R1, 0)

            def copy_y(t, p, k):
                act.wait_ge(y_mm, t + UE + 1)
                if not (known(k) and k < 1):
                    act.wait_ge(y_out[p], 16 * k)
                nc.scalar.activation(ysb[p], pb[1 + 5 * p][:, 0:D], ACT.Copy).then_inc(y_copied, 1)
                act.wait_ge(y_copied, t + 1)
                act.dma_start(ysv[bass.ds(t, 1)].rearrange("a p d -> (a p) d"), ysb[p]).then_inc(y_out[p], 16)

            def body(r, p, sect, prev, nxt, k):
                for u, first_unit, last in steps(r, sect):
                    q = p if sect == "E" else 1 - first_unit
                    act.wait_ge(h1_mm, u + 1)
                    if not (known(u) and u < 2):
                        act.wait_ge(hid_ready, u - 1)
                    nc.scalar.activation(sil[q], pb[2 + 2 * q][:, :], ACT.Silu).then_inc(sil_ready, 1)
                    if last and nxt is not None:
                        split_high(r + 1, 1 - p, None if known(r) else sect)
                    if sect == "1" and last and not (known(r) and r - R1 >= LATE_CHUNKS):
                        act_high(act, 16 * ((FRONT + ATT_CHUNKS) // 2 + 1) + 16 * k, p,
                                 weight_parts(r + (ATT_CHUNKS - R1))[0])
                    if first_unit and prev == "E":
                        copy_y(r - 1 - RE, 1 - p, (r - 1 - RE) // 2 if known(r) else k if p else k - 1)

            moe_loop(act, body)

        @block.tensor
        def _(pe):
            mm = nc.tensor.matmul

            def transpose_xn(i):
                pe.wait_ge(xn_ready, 2 * i + 2)
                if before(i, 1):
                    pe.wait_ge(xl_ready, i)
                if before(i, 2):
                    pe.wait_ge(onl_ready, i - 1)
                for b in range(2):
                    for c in range(C):
                        k = b * C + c
                        last = nc.tensor.transpose(psT[:, bass.ts(k, P)], xn[:, b, bass.ts(c, P)], ident[:, :])
                last.then_inc(xt_mm, 1)

            def project_qk(ps, j, act_h, act_l, done):
                for m in range(C):
                    for c in range(C):
                        for w, a in ((awh, act_h), (awh, act_l), (awl, act_h)):
                            last = mm(ps[:, bass.ts(m, 2 * S)], w[:, j, c, bass.ts(m, P)],
                                      a[:, c].rearrange("p b t -> p (b t)"),
                                      start=(c == 0 and w is awh and a is act_h),
                                      stop=(c == C - 1 and w is awl))
                last.then_inc(done, 1)

            def project(i):
                pe.wait_ge(xl_ready, i + 1)
                if before(i, 1):
                    pe.wait_ge(v32_ready, i)
                project_qk(psQ, 0, xnh, xnl, q_mm)
                pe.wait_ge(cl_ready, i + 1)
                if before(i, 3):
                    pe.wait_ge(x1_ready, 2 * i - 4)
                project_qk(psK, 1, ch, cl, k_mm)
                pe.wait_ge(ql_ready, 2 * i + 2)
                for b in range(2):
                    for c in range(C):
                        for a, w in ((ch, awh), (cl, awh), (ch, awl)):
                            last = mm(psQ[:, bass.ts(b, D)], a[:, c, b, :], w[:, 2, c, :],
                                      start=(c == 0 and a is ch and w is awh),
                                      stop=(c == C - 1 and w is awl))
                last.then_inc(v_mm, 1)

            def scores(i, p, b, half):
                for k in range(NQ):
                    n = 4 * b + k
                    bank = pb[4 + n % 2]
                    if n == 0:
                        pe.wait_ge(qs_in[p], 48 * (half + 1))
                        pe.wait_ge(ks_in[p], 64 * (half + 1))
                    if before(i, 1) or n >= 2:
                        pe.wait_ge(mx_ready, 8 * i + n - 1)
                    mm(bank[:, :], ident16[:, :], bq_f[:, bass.ts(k, 512)], start=True, stop=False,
                   skip_group_check=True)
                    for h in range(QUAD):
                        last = mm(bank[:, bass.ts(h, S)], QS[p][0:ROW_MAX, QUAD * k + h, bass.ts(b, S)],
                                  KS[p][0:ROW_MAX, QUAD * k + h, bass.ts(b, S)], start=False, stop=True,
                                  skip_group_check=True)
                    last.then_inc(s_mm, 1)

            def transpose_max(i, b):
                pe.wait_ge(mclamp_ready, 2 * i + b + 1)
                if b == 0 and before(i, 1):
                    pe.wait_ge(on_ready, 2 * i)
                if before(i, 1) or b:
                    pe.wait_ge(mrow_ready, 2 * i + b)
                nc.tensor.transpose(psC[0:NH, 384:512], mclamp[:, b, :], ident[:, :]).then_inc(m_mm, 1)

            def scores_t(i, p, n):
                b, k = n // 4, n % 4
                bank = pb[6 + n % 2]
                if k == 0:
                    pe.wait_ge(m_in[b], 16 * i + 16)
                if before(i, 1) or n >= 2:
                    pe.wait_ge(prob_ready, 8 * i + n - 1)
                mm(bank[:, :], ident16[:, :], bth_f[:, bass.ts(k, 512)], start=True, stop=False,
                   skip_group_check=True)
                mm(bank[:, :], ident16[:, :], btl_f[:, bass.ts(k, 512)], start=False, stop=False,
                   skip_group_check=True)
                for h in range(QUAD):
                    last = mm(bank[:, bass.ts(h, S)], KS[p][0:ROW_MAX + 1, QUAD * k + h, bass.ts(b, S)],
                              QS[p][0:ROW_MAX + 1, QUAD * k + h, bass.ts(b, S)], start=False, stop=True,
                              skip_group_check=True)
                last.then_inc(st_mm, 1)

            def values(i, p, n):
                b, k = n // 4, n % 4
                if n == 0:
                    pe.wait_ge(vl_ready, 2 * i + 2)
                    pe.wait_ge(vmask_ready, 2 * i + 2)
                    pe.wait_ge(mrow_ready, 2 * i + 2)
                if k == 0 and (before(i, 1) or b):
                    pe.wait_ge(on_ready, 2 * i + b)
                pe.wait_ge(prob_lo_ready, 8 * i + n + 1)
                hi = words_high(flat(prob[n % 4]))
                for h in range(QUAD):
                    hh = QUAD * k + h
                    o = psC[:, hh * (HD + 1):(hh + 1) * (HD + 1)]
                    mm(o, hi[:, bass.ts(h, S)], vh[p][:, b, hh, :], start=True, stop=False)
                    mm(o, hi[:, bass.ts(h, S)], vl[p][:, b, hh, :], start=False, stop=False)
                    last = mm(o, prob_lo[n % 4][:, h, :], vh[p][:, b, hh, :], start=False, stop=True)
                last.then_inc(pv_mm, 1)

            def transpose_out(i):
                pe.wait_ge(on_ready, 2 * i + 2)
                pe.wait_ge(xl_ready, min(i + 2, NPAIR) if known(i) else i + 2)
                for k in range(2 * C):
                    last = nc.tensor.transpose(psT[:, bass.ts(k, P)], on.rearrange("p b d -> p (b d)")[:, bass.ts(k, P)],
                                               ident[:, :])
                last.then_inc(ot_mm, 1)

            def project_out(i):
                pe.wait_ge(onl_ready, i + 1)
                pe.wait_ge(kl_ready, min(2 * i + 6, 2 * NPAIR) if known(i) else 2 * i + 6)
                for b in range(2):
                    for c in range(C):
                        for a, w in ((onh, awh), (onl, awh), (onh, awl)):
                            last = mm(psK[:, bass.ts(b, D)], a[:, b * C + c, :], w[:, 3, c, :],
                                      start=(c == 0 and a is onh and w is awh),
                                      stop=(c == C - 1 and w is awl))
                last.then_inc(o_mm, 1)

            pe.wait_ge(idents, 4)
            transpose_xn(0)
            pe.wait_ge(stage_hi, 2)
            pe.wait_ge(stage_lo, 2)
            project(0)
            pe.wait_ge(stage_hi, FRONT)
            pe.wait_ge(stage_lo, lows(FRONT))

            def body(i, p, k):
                scores(i, p, 0, k)
                if before(i, 1):
                    transpose_out(i - 1)
                scores(i, p, 1, k)
                transpose_max(i, 0)
                if upto(i, NPAIR - 2):
                    transpose_xn(i + 1)
                    project(i + 1)
                transpose_max(i, 1)
                if before(i, 1):
                    project_out(i - 1)
                for n in range(8):
                    scores_t(i, p, n)
                    if n >= 2:
                        values(i, p, n - 2)
                values(i, p, 6)
                values(i, p, 7)

            pair_loop(pe, body)
            transpose_out(NPAIR - 1)
            project_out(NPAIR - 1)
            pe.wait_ge(x1_ready, B)

            def transpose_rows(r, p, sect, half):
                if sect == "E":
                    pe.wait_ge(rows_in[p], 16 * (half + 1))
                elif sect == "R":
                    pe.wait_ge(router_rows, r + 1)
                else:
                    pe.wait_ge(rows_made, r + 1 - R1 if sect == "1" else r + 1 - R2 + HALF)
                if not (known(r) and r < 2):
                    pe.wait_ge(tl_ready, r - 1)
                for c in range(C):
                    last = nc.tensor.transpose(pb[7 * p][:, bass.ts(c, P)], rows[p][:, bass.ts(c, P)], ident[:, :])
                last.then_inc(tr_mm, 1)

            def router(r, p):
                pe.wait_ge(tl_ready, r + 1)
                if not (known(r) and r < 2):
                    pe.wait_ge(logit_ready, r - 1)
                for c in range(C):
                    for a, w in ((xh[p], rwh), (xl[p], rwh), (xh[p], rwl)):
                        last = mm(pb[2 + p][:, 0:E], a[:, c, :], w[:, c, :],
                                  start=(c == 0 and a is xh[p] and w is rwh), stop=(c == C - 1 and w is rwl))
                last.then_inc(router_mm, 1)

            transpose_rows(0, 0, "R", 0)
            transpose_rows(1, 1, "R", 0)
            router(0, 0)
            with pe.Fori(1, B // 2) as k:
                transpose_rows(2 * k, 0, "R", k)
                router(2 * k - 1, 1)
                transpose_rows(2 * k + 1, 1, "R", k)
                router(2 * k, 0)
            router(B - 1, 1)
            pe.wait_ge(route, PICK_STEP)
            pe.wait_ge(route_const, 5)
            pe.wait_ge(logit_ready, B)
            mm(psR[:, 0:B * E], tri, flat(pick), start=True, stop=True)
            mm(psR[:, B * E:], ones, flat(pick), start=True, stop=True).then_inc(rank_mm, 1)
            transpose_rows(R1, 0, "1", 0)

            def up(u, q, p, at):
                if not (known(u) and u < 2):
                    pe.wait_ge(hid_ready, u - 1)
                for j, done in ((0, h1_mm), (1, h3_mm)):
                    base = at + j * 2 * CHUNK
                    for m in range(KC):
                        for c in range(C):
                            hi = wparts[:, bass.ds(base + c * HID + m * P, P)]
                            lo = wparts[:, bass.ds(base + CHUNK + c * HID + m * P, P)]
                            o = pb[2 + 2 * q + j][:, bass.ts(m, P)]
                            mm(o, hi, xh[p][:, c, :], start=(c == 0), stop=False)
                            mm(o, hi, xl[p][:, c, :], start=False, stop=False)
                            last = mm(o, lo, xh[p][:, c, :], start=False, stop=(c == C - 1))
                    last.then_inc(done, 1)

            def down(u, q, p, at, first, last_unit):
                pe.wait_ge(hlo_ready, u + 1)
                o = pb[1 + 5 * p][:, 0:D]
                hi = words_high(hid[q])
                base = at + 2 * 2 * CHUNK
                for k in range(KC):
                    w_hi = wparts[:, bass.ds(base + k * D, D)]
                    w_lo = wparts[:, bass.ds(base + CHUNK + k * D, D)]
                    mm(o, hi[:, bass.ts(k, P)], w_hi, start=(first and k == 0), stop=False)
                    mm(o, hi[:, bass.ts(k, P)], w_lo, start=False, stop=False)
                    last = mm(o, hlo[q][:, bass.ts(k, P)], w_hi, start=False, stop=(last_unit and k == KC - 1))
                last.then_inc(y_mm, 1)

            def wait_y_bank(r, sect=None):
                sect = sect or section(r - 2)
                if sect == "R":
                    pe.wait_ge(route, RANK_STEP)
                elif sect == "E":
                    pe.wait_ge(y_copied, r - 1 - RE)
                else:
                    pe.wait_ge(y_added, r - 1 - R1 if sect == "1" else r - 1 - R2 + HALF)

            def experts_at(t, n):
                return nc.values_load_multi_w_load_instructions(
                    te[0:1, bass.ds(t, n)], engines=[mybir.EngineType.PE], min_val=3 * NSH * 2 * CHUNK,
                    max_val=3 * (NSH + E - 1) * 2 * CHUNK,
                    skip_runtime_bounds_check_because="DVE clamps the expert to E - 1 before it scales it")[1]

            shared2 = 3 * 2 * CHUNK
            at_of = {}

            def body(r, p, sect, prev, nxt, k):
                if sect == "E" and p == 0:
                    if known(k) and k < 1:
                        pe.wait_ge(route, ROUTE_STEPS)
                        pe.sem_inc(pe_passed, 1)
                        at_of[0], at_of[1] = experts_at(0, 2)
                    else:
                        at_of[-1], at_of[0], at_of[1] = experts_at(2 * k - 1, 3)
                for j, (u, first, last) in enumerate(steps(r, sect)):
                    q = p if sect == "E" else j
                    at = at_of[p] if sect == "E" else j * shared2
                    if first:
                        pe.wait_ge(tl_ready, r + 1)
                    if sect == "E":
                        if known(r) and r == RE:
                            pe.wait_ge(stage_hi, FRONT + NCHUNK)
                            pe.wait_ge(stage_lo, lows(FRONT + NCHUNK))
                            pe.wait_ge(y_added, HALF - 1)
                        if known(r) and r == RE + 1:
                            pe.wait_ge(y_added, HALF)
                    up(u, q, p, at)
                    if last and nxt is not None:
                        transpose_rows(r + 1, 1 - p, nxt, 0 if nxt != sect else k + p)
                    if j == 1:
                        wait_y_bank(r, None if known(r) else sect)
                        down(u - 1, 1 - q, p, 0, True, False)
                    elif prev == "E":
                        wait_y_bank(r - 1, None if known(r) else sect)
                        before_at = at_of[0] if p else at_of[-1] if sect == "E" else at_of[1]
                        down(u - 1, 1 - q, 1 - p, before_at, True, True)
                    elif prev is not None:
                        down(u - 1, 1 - q, 1 - p, shared2, False, True)

            moe_loop(pe, body)
            down(UTOT - 1, 1, 1, shared2, False, True)

        @block.vector
        def _(dve):
            V = nc.vector
            V.memset(zeros[:, :], 0.0).then_inc(zeroed, 1)
            for p in range(2):
                V.memset(flat(QS[p]).bitcast(F32), 0.0).then_inc(zeroed, 1)
                dve.wait_ge(zeroed, 2 * p + 2)
                V.memset(flat(QS[p])[ROW_MASK:ROW_MASK + 1, :], MASK_Q).then_inc(zeroed, 1)
            dve.wait_ge(const_in, 16 * CONSTS)
            V.tensor_scalar(mrow16[0:B, :], mrow_raw[0:B, :], MASK_K, None, ALU.mult).then_inc(setup_dve, 1)
            dve.wait_ge(stage_in[0], 16)
            V.tensor_scalar(stage[:, 0, 0:C * D], stage[:, 0, 0:C * D], HD ** -0.5, None, ALU.mult).then_inc(setup_dve, 1)
            V.tensor_scalar(qkbias[:, 0:C], qkbias[:, 0:C], HD ** -0.5, None, ALU.mult).then_inc(setup_dve, 1)

            ln_count = [0]

            def ln_link(*steps):
                for ins in steps:
                    ins.then_inc(ln_step, 1)
                ln_count[0] += len(steps)
                dve.wait_ge(ln_step, ln_count[0])

            def ln_variances(at, count):
                a = slice(at, at + count)
                mu, d, m2 = mean[:, a], ln_tmp[:, 0, a], ln_tmp[:, 1, a]
                ln_link(V.tensor_tensor(mu, stats[:, a, 1], stats[:, a, 4], ALU.add),
                        V.tensor_tensor(d, stats[:, a, 1], stats[:, a, 4], ALU.subtract),
                        V.tensor_tensor(m2, stats[:, a, 2], stats[:, a, 5], ALU.add))
                ln_link(V.tensor_scalar(mu, mu, 0.5, None, ALU.mult), V.tensor_tensor(d, d, d, ALU.mult))
                ln_link(V.scalar_tensor_tensor(out=m2, in0=d, scalar=D / 4, in1=m2, op0=ALU.mult, op1=ALU.add))
                V.tensor_scalar(var_eps[:, a], m2, 1.0 / D, EPS, ALU.mult, ALU.add).then_inc(ln_var, 1)

            def ln_scales(n, at, count):
                a = slice(at, at + count)
                dve.wait_ge(ln_std, n)
                ln_link(V.reciprocal(rstd[:, a], std[:, a]))
                V.scalar_tensor_tensor(out=nmr[:, a], in0=mean[:, a], scalar=-1.0, in1=rstd[:, a],
                                       op0=ALU.mult, op1=ALU.mult).then_inc(ln_ready, 1)

            def x_stats(q):
                dve.wait_ge(x_in[q], 16)
                with dve.Fori(8 * q, 8 * q + 8) as j:
                    V.bn_stats(stats[:, bass.ds(j, 1), :].rearrange("p a s -> p (a s)"),
                               xs[:, bass.ds(j, 1), :].rearrange("p a d -> p (a d)")).then_inc(stats_done, 1)

            x_stats(0)
            dve.wait_ge(stats_done, 8)
            ln_variances(*LN_GROUPS[0])
            V.tensor_scalar(nmask, mraw, -1.0, 1.0, ALU.mult, ALU.add).then_inc(setup_dve, 1)
            dve.wait_ge(setup_act, 2)
            V.tensor_scalar(obr, obr, gates[:, 0:1], None, ALU.mult).then_inc(setup_dve, 1)
            V.tensor_tensor(rwl[:, :, :], rw_f[:, :, :], rwh[:, :, :], ALU.subtract).then_inc(setup_dve, 1)
            ln_scales(1, *LN_GROUPS[0])

            def xn_low(i):
                dve.wait_ge(xh_ready, i + 1)
                V.tensor_tensor(xnl, psT[:, :].rearrange("p (b c t) -> p c b t", b=2, c=C), xnh,
                                ALU.subtract).then_inc(xl_ready, 1)

            def qk_low(i):
                for ps, parts, col, high, ready in ((psQ, qp, 0, qh_ready, ql_ready), (psK, kp, 2, kh_ready, kl_ready)):
                    dve.wait_ge(high, 2 * i + 2)
                    for m in range(C):
                        V.scalar_tensor_tensor(out=parts[:, 1, m, :], in0=ps[:, bass.ts(m, 2 * S)],
                                               scalar=qkbias[:, col + m:col + m + 1], in1=parts[:, 0, m, :],
                                               op0=ALU.add, op1=ALU.subtract).then_inc(ready, 1)

            def v_parts(i, p):
                dve.wait_ge(v_mm, i + 1)
                if before(i, 1):
                    dve.wait_ge(vh_ready, 2 * i)
                    dve.wait_ge(vl_ready, 2 * i)
                V.tensor_tensor(v32, psQ[:, :].rearrange("p (b d) -> p b d", b=2),
                                vbr.unsqueeze(1).to_broadcast([P, 2, D]), ALU.add).then_inc(v32_ready, 1)
                dve.wait_ge(v32_ready, i + 1)
                for b in range(2):
                    dve.wait_ge(vh_ready, 2 * i + b + 1)
                    V.scalar_tensor_tensor(out=vl[p][:, b, :, 0:HD], in0=v32[:, b, :].rearrange("p (h e) -> p h e", h=NH),
                                           scalar=nmask[:, bass.ds(2 * i + b, 1)], in1=vh[p][:, b, :, 0:HD],
                                           op0=ALU.mult, op1=ALU.subtract).then_inc(vl_ready, 1)

            def maxima(i, b):
                for k in range(NQ):
                    n = 4 * b + k
                    dve.wait_ge(s_mm, 8 * i + n + 1)
                    V.tensor_reduce(mx[:, b, bass.ts(k, QUAD)], pb[4 + n % 2][:, :].rearrange("p (h t) -> p h t", h=QUAD),
                                    AX.X, ALU.max).then_inc(mx_ready, 1)
                dve.wait_ge(mx_ready, 8 * i + 4 * b + 4)
                if before(i, 1):
                    dve.wait_ge(m_mm, 2 * i + b - 1)
                V.tensor_scalar(mclamp[:, b, :], mx[:, b, :], -MAX_CLAMP, MAX_CLAMP, ALU.max, ALU.min)\
                    .then_inc(mclamp_ready, 1)

            def prob_low(i, n):
                dve.wait_ge(prob_ready, 8 * i + n + 1)
                V.tensor_tensor(flat(prob_lo[n % 4]), flat(prob[n % 4]), words_high(flat(prob[n % 4])),
                                ALU.subtract).then_inc(prob_lo_ready, 1)

            def normalise_heads(i, b):
                dve.wait_ge(pv_mm, 8 * i + 4 * b + 4)
                o = psC[:, 0:NH * (HD + 1)].rearrange("p (h e) -> p h e", h=NH)
                V.tensor_scalar(den[:, b, :], o[:, :, HD], 1e-6, None, ALU.max).then_inc(den_ready, 1)
                dve.wait_ge(den_ready, 2 * i + b + 1)
                V.reciprocal(rden[:, b, :], den[:, b, :]).then_inc(rden_ready, 1)
                dve.wait_ge(rden_ready, 2 * i + b + 1)
                if before(i, 1):
                    dve.wait_ge(ot_mm, i)
                V.tensor_tensor(on[:, b, :].rearrange("p (h e) -> p h e", h=NH), o[:, :, 0:HD],
                                rden[:, b, :].unsqueeze(2).to_broadcast([P, NH, HD]), ALU.mult).then_inc(on_ready, 1)

            def out_low(i):
                dve.wait_ge(onh_ready, i + 1)
                V.tensor_tensor(flat(onl), psT[:, :], flat(onh), ALU.subtract).then_inc(onl_ready, 1)

            def residual(i):
                dve.wait_ge(o_mm, i + 1)
                dve.wait_ge(xb_ready, 2 * i + 2)
                for b in range(2):
                    xb = xs[:, bass.ds(2 * i + b, 1), :].rearrange("p a d -> p (a d)")
                    V.scalar_tensor_tensor(out=xb, in0=psK[:, bass.ts(b, D)], scalar=gates[:, 0:1], in1=xb,
                                           op0=ALU.mult, op1=ALU.add).then_inc(x1_ready, 1)
                for b in range(2):
                    dve.wait_ge(x1_ready, 2 * i + b + 1)
                    V.bn_stats(stats[:, bass.ds(2 * i + b, 1), :].rearrange("p a s -> p (a s)"),
                               xs[:, bass.ds(2 * i + b, 1), :].rearrange("p a d -> p (a d)")).then_inc(stats_done, 1)

            xn_low(0)
            qk_low(0)
            v_parts(0, 0)
            for q in range(1, 4):
                x_stats(q)
            dve.wait_ge(stats_done, B)
            ln_variances(*LN_GROUPS[1])
            ln_scales(2, *LN_GROUPS[1])

            def body(i, p, k):
                maxima(i, 0)
                if before(i, 1):
                    out_low(i - 1)
                maxima(i, 1)
                if upto(i, NPAIR - 2):
                    xn_low(i + 1)
                    qk_low(i + 1)
                    v_parts(i + 1, 1 - p)
                if before(i, 1):
                    residual(i - 1)
                for n in range(4):
                    prob_low(i, n)
                prob_low(i, 4)
                normalise_heads(i, 0)
                for n in range(5, 8):
                    prob_low(i, n)
                normalise_heads(i, 1)

            pair_loop(dve, body)
            out_low(NPAIR - 1)
            residual(NPAIR - 1)
            dve.wait_ge(x1_ready, B)

            def row(j):
                return xs[:, bass.ds(j, 1), :].rearrange("p a d -> p (a d)")

            def make_rows(dst, j, made):
                V.tensor_scalar(dst, row(j), mean[:, bass.ds(j, 1)], rstd[:, bass.ds(j, 1)],
                                ALU.subtract, ALU.mult).then_inc(made, 1)

            def split_low(r, p):
                dve.wait_ge(th_ready, r + 1)
                V.tensor_tensor(flat(xl[p]), pb[7 * p][:, 0:D], flat(xh[p]), ALU.subtract).then_inc(tl_ready, 1)

            lg = rt[:, 0]

            def logits(r, p):
                dve.wait_ge(router_mm, r + 1)
                V.tensor_tensor(lg[:, bass.ds(r, 1), :].rearrange("p a e -> p (a e)"), pb[2 + p][:, 0:E], ebr[:, :],
                                ALU.add).then_inc(logit_ready, 1)

            def shared_rows(r, p, j):
                dve.wait_ge(tr_mm, r - 1)
                make_rows(rows[p], j, rows_made)

            dve.wait_ge(stats_done, 2 * B)
            ln_variances(0, B)
            ln_scales(3, 0, B)
            with dve.Fori(0, B // 2) as k:
                for p in range(2):
                    split_low(2 * k + p, p)
                    logits(2 * k + p, p)
            dve.wait_ge(ln_ready, 3)
            shared_rows(R1, 0, 0)
            dve.wait_ge(logit_ready, B)
            dve.wait_ge(route_const, 5)

            step = [0]

            def link(ins):
                step[0] += 1
                ins.then_inc(route, 1)
                dve.wait_ge(route, step[0])
                return step[0]

            ie = iota_e.unsqueeze(1).to_broadcast([P, B, E])

            def over_e(a):
                return a.unsqueeze(2).to_broadcast([P, B, E])

            src = lg
            for k in range(2):
                best, sel = sm[:, 2 * k], sm[:, 2 * k + 1]
                ge, hot = rt[:, 1], rt[:, 2 + k]
                link(V.tensor_reduce(best, src, AX.X, ALU.max))
                link(V.tensor_tensor(ge, src, over_e(best), ALU.is_ge))
                link(V.scalar_tensor_tensor(out=ge, in0=ge, scalar=-float(E), in1=ie, op0=ALU.mult, op1=ALU.add))
                link(V.tensor_reduce(sel, ge, AX.X, ALU.min))
                link(V.tensor_scalar(sel, sel, float(E), None, ALU.add))
                link(V.tensor_tensor(hot, ie, over_e(sel), ALU.is_equal))
                if k == 0:
                    link(V.scalar_tensor_tensor(out=rt[:, 4], in0=hot, scalar=-3.0e38, in1=lg, op0=ALU.mult, op1=ALU.add))
                    src = rt[:, 4]
            assert link(V.tensor_tensor(pick, rt[:, 2], rt[:, 3], ALU.add)) == PICK_STEP
            assert link(V.tensor_tensor(sm[:, 4], sm[:, 2], sm[:, 0], ALU.subtract)) == EXP_STEP
            dve.wait_ge(rank_mm, 1)
            a, bb = rt[:, 5], rt[:, 6]
            tot = rt[:, 7]
            link(V.tensor_copy(flat(tot), psR[:, B * E:]))
            link(V.tensor_copy(flat(a), psR[:, B * E:]))
            sh = 1
            while sh < B:
                V.tensor_copy(bb[:, 0:sh, :], a[:, 0:sh, :]).then_inc(route, 1)
                step[0] += 1
                link(V.tensor_tensor(bb[:, sh:, :], a[:, sh:, :], a[:, 0:B - sh, :], ALU.add))
                a, bb = bb, a
                sh *= 2
            link(V.tensor_scalar(cnt[:, 0], a[:, B - 1, :], float(P - 1), None, ALU.add))
            link(V.tensor_tensor(a, a, tot, ALU.subtract))
            link(V.tensor_copy(cnt_i, cnt[:, 0]))
            link(V.tensor_scalar(cnt_i, cnt_i, 7, None, ALU.logical_shift_right))
            link(V.tensor_copy(cnt[:, 1], cnt_i))
            ca, cb = cnt[:, 1], cnt[:, 2]
            link(V.tensor_copy(cnt[:, 3], cnt[:, 1]))
            ca = cnt[:, 3]
            sh = 1
            while sh < E:
                V.tensor_copy(cb[:, 0:sh], ca[:, 0:sh]).then_inc(route, 1)
                step[0] += 1
                link(V.tensor_tensor(cb[:, sh:], ca[:, sh:], ca[:, 0:E - sh], ALU.add))
                ca, cb = cb, ca
                sh *= 2
            link(V.tensor_tensor(cnt[:, 4], ca, cnt[:, 1], ALU.subtract))
            link(V.tensor_scalar(cnt[:, 5], cnt[:, 4], float(P), None, ALU.mult))
            link(V.tensor_tensor(a, a, cnt[:, 5].unsqueeze(1).to_broadcast([P, B, E]), ALU.add))
            link(V.tensor_tensor(flat(a), flat(a), psR[:, 0:B * E], ALU.add))
            for k in range(2):
                link(V.tensor_tensor(rt[:, 8], rt[:, 2 + k], a, ALU.mult))
                link(V.tensor_reduce(sm[:, 6 + k], rt[:, 8], AX.X, ALU.add))
                link(V.tensor_copy(slots[:, k, :], sm[:, 6 + k]))
            link(V.tensor_tensor(te_f, iota_t.unsqueeze(2).to_broadcast([P, SLOT_TILES, E]),
                                 ca.unsqueeze(1).to_broadcast([P, SLOT_TILES, E]), ALU.is_ge))
            link(V.tensor_reduce(te_s, te_f, AX.X, ALU.add))
            link(V.tensor_scalar(te_s, te_s, float(E - 1), float(NSH), ALU.min, ALU.add))
            link(V.tensor_scalar(te_s, te_s, float(3 * 2 * CHUNK), None, ALU.mult))
            assert link(V.tensor_copy(te, te_s)) == ROUTE_STEPS
            dve.wait_ge(exp_ready, 1)
            link(V.tensor_scalar(sm[:, 8], sm[:, 5], 1.0, None, ALU.add))
            link(V.reciprocal(sm[:, 9], sm[:, 8]))
            link(V.tensor_scalar(sm[:, 10], sm[:, 9], gates[:, 1:2], None, ALU.mult))
            link(V.tensor_tensor(sm[:, 11], sm[:, 10], sm[:, 5], ALU.mult))

            def scatter_rows(j, p, half):
                if not (known(half) and half < 1):
                    dve.wait_ge(scattered[p], 32 * half)
                make_rows(srow[p], j, srow_made)

            def combine(n, j, p, half):
                dve.wait_ge(gathered[p], 32 * (half + 1))
                V.scalar_tensor_tensor(out=row(j), in0=yg[p][:, 0, :], scalar=sm[:, 10, bass.ds(j, 1)], in1=row(j),
                                       op0=ALU.mult, op1=ALU.add).then_inc(comb_a, 1)
                dve.wait_ge(comb_a, n + 1)
                V.scalar_tensor_tensor(out=row(j), in0=yg[p][:, 1, :], scalar=sm[:, 11, bass.ds(j, 1)], in1=row(j),
                                       op0=ALU.mult, op1=ALU.add).then_inc(comb_b, 1)

            def add_shared(j, p):
                V.scalar_tensor_tensor(out=row(j), in0=pb[1 + 5 * p][:, 0:D], scalar=gates[:, 1:2], in1=row(j),
                                       op0=ALU.mult, op1=ALU.add).then_inc(y_added, 1)

            shared_rows(R1 + 1, 1, 1)
            split_low(R1, 0)

            def body(r, p, sect, prev, nxt, k):
                for j, (u, first, last) in enumerate(steps(r, sect)):
                    q = p if sect == "E" else j
                    dve.wait_ge(h3_mm, u + 1)
                    dve.wait_ge(sil_ready, u + 1)
                    if not (known(u) and u < 2):
                        dve.wait_ge(y_mm, u - 1)
                    V.tensor_tensor(hid[q], sil[q], pb[3 + 2 * q][:, :], ALU.mult).then_inc(hid_ready, 1)
                    if last and nxt is not None:
                        split_low(r + 1, 1 - p)
                    dve.wait_ge(hid_ready, u + 1)
                    V.tensor_tensor(hlo[q], hid[q], words_high(hid[q]), ALU.subtract).then_inc(hlo_ready, 1)
                    if first and prev in ("1", "2"):
                        dve.wait_ge(y_mm, u)
                        add_shared(r - 1 - R1 if prev == "1" else r - 1 - R2 + HALF, 1 - p)
                    if sect == "1" and j == 0:
                        scatter_rows(2 * r - 2 * R1, 0, r - R1)
                        scatter_rows(2 * r - (2 * R1 - 1), 1, r - R1)
                    if last and sect == "1" and not (known(r) and r + 2 >= RE):
                        shared_rows(r + 2, p, r + 2 - R1)
                    if sect == "E" and known(r) and r + 2 >= R2:
                        shared_rows(r + 2, p, r + 2 - R2 + HALF)
                    if last and sect == "2" and not (known(r) and r + 2 >= RTOT):
                        shared_rows(r + 2, p, r + 2 - R2 + HALF)
                if sect == "2":
                    m = r - R2
                    if known(r) and r == R2:
                        combine(0, 0, 0, 0)
                    else:
                        combine(2 * m - 1, m, 1, m - 1)
                        dve.wait_ge(y_added, m + HALF)
                        combine(2 * m, m + HALF - 1, 0, m)

            moe_loop(dve, body)
            dve.wait_ge(y_mm, UTOT)
            add_shared(B - 1, 1)
            dve.wait_ge(y_added, B)
            combine(B - 1, B - 1, 1, HALF - 1)


def kernel(**inputs):
    import numpy as np
    import concourse.bacc as bacc
    from concourse.bass_utils import run_bass_kernel_spmd

    a = {k: np.asarray(v) for k, v in inputs.items()}
    con = np.ascontiguousarray

    def chunked(w):
        k, n = w.shape[-2:]
        w = w.reshape(*w.shape[:-2], k // P, P, n)
        return con(np.moveaxis(w, -2, -3)).reshape(*w.shape[:-3], P, (k // P) * n)

    def transposed(w):
        return np.swapaxes(w, -1, -2)

    aw = [chunked(transposed(a[f"L0_xattn_{k}_w"])) for k in "qkvo"]
    w1, w3, w2 = (np.concatenate([a[f"L0_ffn_s{k}"], a[f"L0_ffn_{k}"]]) for k in ("w1", "w3", "w2"))
    wall = np.stack([chunked(transposed(w)) for w in (w1, w3, w2)], axis=1).reshape(NCHUNK, P, CHUNK)
    fside = a["fside_1x16xSxS2_0"][0]

    def by_row(w):
        w = w.transpose(1, 0, 2).reshape(S, 2, CHUNK)
        return con(w.transpose(1, 0, 2))

    mask = a["mask_BxS2_bk0"]
    arrays = {
        "x": con(a["x"]),
        "ctxT": con(a["ctx_1024"].reshape(B * S, D).T),
        "bias_q": by_row(fside),
        "bias_t": by_row(transposed(fside)),
        "mask": con(mask),
        "maskT": con(mask.T),
        "g_att": con(a["g_xattn"]),
        "g_ffn": con(a["g_ffn"]),
        "attw": con(np.stack([np.concatenate(aw[0:2], axis=1), np.concatenate(aw[2:4], axis=1)])),
        "qkb": con(np.stack([a["L0_xattn_q_b"], a["L0_xattn_k_b"]]).reshape(2 * C, P).T),
        "vb": con(a["L0_xattn_v_b"]),
        "ob": con(a["L0_xattn_o_b"]),
        "rw": con(a["L0_ffn_router_w"].T),
        "eb": con(a["L0_ffn_expert_bias"]),
        "wall": con(wall),
    }
    nc = bacc.Bacc("TRN2", target_bir_lowering=False, num_devices=1)
    args = {k: nc.dram_tensor(k, v.shape, mybir.dt.from_np(v.dtype), kind="ExternalInput").ap()
            for k, v in arrays.items()}
    args["out"] = nc.dram_tensor("out", (B, S, D), F32, kind="ExternalOutput").ap()
    build(nc, **args)
    return run_bass_kernel_spmd(nc, [arrays], core_ids=[0]).results[0]["out"]
```

```python
from contextlib import ExitStack

import concourse.bass as bass
from concourse import mybir
import numpy as np

ALU = mybir.AluOpType
ACT = mybir.ActivationFunctionType
AX = mybir.AxisListType
F32 = mybir.dt.float32
F16 = mybir.dt.float16
BF16 = mybir.dt.bfloat16
I32 = mybir.dt.int32
U8 = mybir.dt.uint8

P = 128
B, S, D = 32, 128, 256
NH, HD = 16, 16
E, NSH, HID = 8, 2, 512
C = D // P
KC = HID // P
NPAIR = B // 2
QUAD = 4
NQ = NH // QUAD
W = 2 * P
SLOT_TILES = 39
SLOT_SPACE = 40
HALF = NPAIR // 2
CHUNK = 1024
NCHUNK = 3 * (NSH + E)
ATT_CHUNKS = NPAIR
EPS = 1e-5
FRONT = 6
ZERO_ROWS = SLOT_SPACE * W // (P * NPAIR)
LATE_CHUNKS = NCHUNK - ATT_CHUNKS
CONSTS = 8
PICK_STEP, EXP_STEP, RANK_STEP, SLOT_STEP, ROUTE_STEPS = 14, 15, 43, 49, 54
MASK_Q, MASK_K = 60000.0, -60000.0
MAX_CLAMP = 60000.0
ROW_MASK, ROW_MAX = 64, 96
MASK_Q_TWICE = float(np.array([MASK_Q, MASK_Q], np.float16).view(np.float32)[0])


def build(nc, x, ctxT, bias_q, bias_t, mask, g_att, g_ffn, attw, qkb, vb, ob,
          rw, eb, wall, out):
    es = ExitStack()
    with es:
        def sb(name, shape, dt):
            return es.enter_context(nc.sbuf_tensor(name, shape, dt))

        def sem(name):
            return es.enter_context(nc.semaphore(name))

        xs = sb("xs", [P, B, D], F32)
        stage = sb("stage", [P, 2, CHUNK], F32)
        ident = sb("ident", [P, P], F32)
        ident16 = sb("ident16", [P, P], F16)
        stats = sb("stats", [P, B, 6], F32)
        ln_tmp = sb("ln_tmp", [P, 2, B], F32)
        zeros = sb("zeros", [P, D], F32)
        mean = sb("mean", [P, B], F32)
        rstd = sb("rstd", [P, B], F32)
        var_eps = sb("var_eps", [P, B], F32)
        std = sb("std", [P, B], F32)
        nmr = sb("nmr", [P, B], F32)
        gates = sb("gates", [P, 2], F32)
        graw = sb("graw", [P, 2], F32)
        rw_f = sb("rw_f", [P, C, E], F32)
        rwh = sb("rwh", [P, C, E], F16)
        rwl = sb("rwl", [P, C, E], F16)
        ebr = sb("ebr", [P, E], F32)

        WBYTES = NCHUNK * CHUNK * 4
        ATT_AT = ATT_CHUNKS * CHUNK * 4
        ARENA = 162 * 1024
        arena = sb("arena", [P, ARENA // 2], F16)
        cursor = [0]

        def carve(shape, dt, size):
            n = size
            for k in shape:
                n *= k
            a = arena[:, cursor[0] // 2:(cursor[0] + n) // 2]
            cursor[0] += -(-n // 32) * 32
            assert cursor[0] <= ARENA, cursor[0]
            if dt != F16:
                a = a.bitcast(dt)
            if len(shape) > 1:
                names = "abcd"[:len(shape)]
                a = a.rearrange(f"p ({' '.join(names)}) -> p {' '.join(names)}",
                                **{m: k for m, k in zip(names, shape)})
            return a

        wparts = arena[:, 0:WBYTES // 2]

        cursor[0] = ATT_AT
        bq = carve([NH, S], F16, 2)
        bth = carve([NH, S], F16, 2)
        btl = carve([NH, S], F16, 2)
        QS = [carve([NH, 2 * S], F16, 2) for _ in range(2)]
        KS = [carve([NH, 2 * S], F16, 2) for _ in range(2)]
        prob_all = carve([4 * QUAD, S], F32, 4)
        prob = [prob_all[:, QUAD * k:QUAD * k + QUAD, :] for k in range(4)]
        prob_lo = [carve([QUAD, S], F16, 2) for _ in range(4)]
        xn = carve([2, D], F32, 4)
        xnh = carve([C, 2, S], F16, 2)
        xnl = carve([C, 2, S], F16, 2)
        cf = [carve([C, 2, S], F32, 4) for _ in range(2)]
        ch = carve([C, 2, S], F16, 2)
        cl = carve([C, 2, S], F16, 2)
        qp = carve([2, C, 2 * S], F16, 2)
        kp = carve([2, C, 2 * S], F16, 2)
        vbh = carve([D], F16, 2)
        vbl = carve([D], F16, 2)
        mean_of = carve([S], F16, 2)
        vh = [carve([2, NH, HD + 1], F16, 2) for _ in range(2)]
        vl = [carve([2, NH, HD + 1], F16, 2) for _ in range(2)]
        mx = carve([2, NH], F32, 4)
        mclamp = carve([2, NH], F32, 4)
        mrow = carve([2, S], F16, 2)
        den = carve([2, NH], F32, 4)
        rden = carve([2, NH], F32, 4)
        on = carve([2, D], F32, 4)
        onh = carve([2 * C, S], F16, 2)
        onl = carve([2 * C, S], F16, 2)
        awh = carve([4, C, D], F16, 2)
        awl = carve([4, C, D], F16, 2)
        qkbias = carve([4], F32, 4)
        vbr = carve([D], F32, 4)
        obr = carve([D], F32, 4)
        mrow_raw = carve([S], U8, 1)
        mrow16 = carve([S], F16, 2)

        cursor[0] = WBYTES
        rows = [carve([2, D], F32, 4) for _ in range(2)]
        xh = [carve([C, W], F16, 2) for _ in range(2)]
        xl = [carve([C, W], F16, 2) for _ in range(2)]
        sil = [carve([HID], F32, 4) for _ in range(2)]
        hid = [carve([HID], F32, 4) for _ in range(2)]
        hlo = [carve([HID], F16, 2) for _ in range(2)]
        ysb = [carve([2, D], F32, 4) for _ in range(2)]
        srow = [carve([D], F32, 4) for _ in range(4)]
        rt = carve([9, B, E], F32, 4)
        yg_all = rt[:, 0:8].rearrange("p a b e -> p (a b e)").rearrange("p (n s d) -> p n s d", n=4, s=2)
        yg = [yg_all[:, n] for n in range(4)]
        pick = carve([B, E], F16, 2)
        tri = carve([P], F16, 2)
        ones = carve([P], F16, 2)
        iota_e = carve([E], F32, 4)
        iota_t = carve([SLOT_SPACE], F32, 4)
        sm = carve([12, B], F32, 4)
        cnt = carve([8, E], F32, 4)
        cnt_i = carve([E], I32, 4)
        slots = carve([2, B], I32, 4)
        slot_idx = [carve([2], I32, 4) for _ in range(4)]
        te_f = carve([SLOT_SPACE, E], F32, 4)
        te_s = carve([SLOT_SPACE], F32, 4)
        te = carve([SLOT_SPACE], I32, 4)

        pb = [es.enter_context(nc.psum_tensor(f"bank{i}", [P, 512], F32)) for i in range(8)]
        psT, psQ, psK, psC = pb[0], pb[1], pb[2], pb[3]
        psR = pb[6]

        q_scr = nc.dram_tensor("q_scr", (2, 2, D, 2 * S), F16).ap()
        k_scr = nc.dram_tensor("k_scr", (2, 2, D, 2 * S), F16).ap()
        m_scr = nc.dram_tensor("m_scr", (B, S), F16).ap()
        xslots = nc.dram_tensor("xslots", (SLOT_SPACE * W, D), F32).ap()
        yslots = nc.dram_tensor("yslots", (SLOT_TILES * W, D), F32).ap()
        xsv, ysv = (a.rearrange("(t w p) d -> t p w d", w=2, p=P) for a in (xslots, yslots))

        x_in = [sem(f"x_in{q}") for q in range(4)]
        const_in = sem("const_in")
        const_rows = sem("const_rows")
        idents = sem("idents")
        stage_in = [sem("stage_in0"), sem("stage_in1")]
        stage_hi = sem("stage_hi")
        stage_lo = sem("stage_lo")
        setup_dve = sem("setup_dve")
        setup_act = sem("setup_act")
        q_scaled = sem("q_scaled")
        mask_out = sem("mask_out")
        zero_out = sem("zero_out")
        zeroed = sem("zeroed")
        stats_done = sem("stats_done")
        ln_step = sem("ln_step")
        ln_var = sem("ln_var")
        ln_std = sem("ln_std")
        ln_ready = sem("ln_ready")

        ctx_in = [sem("ctx_in0"), sem("ctx_in1")]
        xn_ready = sem("xn_ready")
        xt_mm = sem("xt_mm")
        xh_ready = sem("xh_ready")
        xl_ready = sem("xl_ready")
        ch_ready = sem("ch_ready")
        cl_ready = sem("cl_ready")
        q_mm = sem("q_mm")
        k_mm = sem("k_mm")
        v_mm = sem("v_mm")
        qh_ready = sem("qh_ready")
        ql_ready = sem("ql_ready")
        kh_ready = sem("kh_ready")
        kl_ready = sem("kl_ready")
        vh_ready = sem("vh_ready")
        vl_ready = sem("vl_ready")
        q_out = sem("q_out")
        k_out = sem("k_out")
        qs_in = [sem("qs_in0"), sem("qs_in1")]
        ks_in = [sem("ks_in0"), sem("ks_in1")]
        s_mm = sem("s_mm")
        mx_ready = sem("mx_ready")
        mclamp_ready = sem("mclamp_ready")
        m_mm = sem("m_mm")
        mrow_ready = sem("mrow_ready")
        m_in = [sem("m_in0"), sem("m_in1")]
        st_mm = sem("st_mm")
        prob_ready = sem("prob_ready")
        prob_lo_ready = sem("prob_lo_ready")
        prob_lo_pool = sem("prob_lo_pool")
        pv_mm = sem("pv_mm")
        den_ready = sem("den_ready")
        rden_ready = sem("rden_ready")
        on_ready = sem("on_ready")
        ot_mm = sem("ot_mm")
        onh_ready = sem("onh_ready")
        onl_ready = sem("onl_ready")
        o_mm = sem("o_mm")
        xb_ready = sem("xb_ready")
        x1_ready = sem("x1_ready")

        block = es.enter_context(nc.Block())

        def words_high(a):
            return a.bitcast(BF16).rearrange("p (n two) -> p n two", two=2)[:, :, 1]

        def flat(a):
            return a.rearrange("p a b -> p (a b)")

        bq_f, bth_f, btl_f = flat(bq), flat(bth), flat(btl)
        awh_f = awh.rearrange("p a b c -> p (a b c)")
        awl_f = awl.rearrange("p a b c -> p (a b c)")

        def front_parts(k):
            if k < 2:
                return awh_f[:, bass.ts(k, CHUNK)], awl_f[:, bass.ts(k, CHUNK)]
            if k < 4:
                return bq_f[:, bass.ts(k - 2, CHUNK)], None
            return bth_f[:, bass.ts(k - 4, CHUNK)], btl_f[:, bass.ts(k - 4, CHUNK)]

        def weight_parts(w):
            return (wparts[:, bass.ds(w * (2 * CHUNK), CHUNK)],
                    wparts[:, bass.ds(w * (2 * CHUNK) + CHUNK, CHUNK)])

        def lows(n):
            return (n if n <= 2 else 2 if n <= 4 else n - 2) if isinstance(n, int) else n - 2

        def act_high(act, k, slot, dst):
            act.wait_ge(stage_in[slot], k)
            nc.scalar.activation(dst, stage[:, slot, :], ACT.Copy).then_inc(stage_hi, 1)

        def pool_low(pool, n, slot, hi, lo):
            pool.wait_ge(stage_hi, n)
            nc.gpsimd.tensor_tensor(lo, stage[:, slot, :], hi, ALU.subtract).then_inc(stage_lo, 1)


        def pair_loop(eng, body):
            body(0, 0, 0)
            body(1, 1, 0)
            with eng.Fori(1, NPAIR // 2 - 1) as k:
                body(2 * k, 0, k)
                body(2 * k + 1, 1, k)
            body(NPAIR - 2, 0, NPAIR // 2 - 1)
            body(NPAIR - 1, 1, NPAIR // 2 - 1)

        def known(i):
            return isinstance(i, int)

        def before(i, n):
            return i >= n if known(i) else True

        def upto(i, n):
            return i <= n if known(i) else True

        R1, RE, R2 = NPAIR, NPAIR + HALF, NPAIR + HALF + SLOT_TILES
        RTOT = R2 + (NPAIR - HALF)
        UE, U2 = 4 * HALF, 4 * HALF + 2 * SLOT_TILES
        UTOT = U2 + 4 * (NPAIR - HALF)

        route_const = sem("route_const")
        rows_made = sem("rows_made")
        rows_in = [sem("rows_in0"), sem("rows_in1")]
        tr_mm = sem("tr_mm")
        th_ready = sem("th_ready")
        tl_ready = sem("tl_ready")
        router_mm = sem("router_mm")
        logit_ready = sem("logit_ready")
        route = sem("route")
        rank_mm = sem("rank_mm")
        exp_ready = sem("exp_ready")
        idx_ready = sem("idx_ready")
        pool_passed = sem("pool_passed")
        pe_passed = sem("pe_passed")
        sp_passed = sem("sp_passed")
        srow_made = sem("srow_made")
        scattered = [sem(f"scattered{n}") for n in range(4)]
        h1_mm = sem("h1_mm")
        h3_mm = sem("h3_mm")
        sil_ready = sem("sil_ready")
        hid_ready = sem("hid_ready")
        hlo_ready = sem("hlo_ready")
        y_mm = sem("y_mm")
        y_added = sem("y_added")
        y_copied = sem("y_copied")
        y_out = [sem("y_out0"), sem("y_out1")]
        gathered = [sem(f"gathered{n}") for n in range(4)]
        comb_a = sem("comb_a")
        comb_b = sem("comb_b")
        res_out = sem("res_out")
        router_rows = sem("router_rows")
        router_rows2 = sem("router_rows2")

        LN_GROUPS = ((0, 8), (8, B - 8))

        def section(r):
            return "R" if r < R1 else "1" if r < RE else "E" if r < R2 else "2"

        def last_unit(r, sect=None):
            sect = sect or section(r)
            return {"1": 4 * (r - R1) + 3, "E": 2 * (r - RE) + UE + 1, "2": 4 * (r - R2) + U2 + 3}[sect]

        def steps(r, sect):
            if sect == "E":
                return [(2 * (r - RE) + UE + j, j, j == 1) for j in range(2)]
            u = 4 * (r - R1) if sect == "1" else 4 * (r - R2) + U2
            return [(u + j, j, j == 3) for j in range(4)]

        def moe_loop(eng, body):
            for a, b, sect, prev, nxt in ((R1, RE, "1", None, "E"), (RE, R2, "E", "1", "2"),
                                          (R2, RTOT, "2", "E", None)):
                n, p = (b - a) // 2, a % 2
                body(a, p, sect, prev, sect, 0)
                body(a + 1, 1 - p, sect, sect, sect, 0)
                with eng.Fori(1, n - 1) as k:
                    body(2 * k + a, p, sect, sect, sect, k)
                    body(2 * k + (a + 1), 1 - p, sect, sect, sect, k)
                for r in range(a + 2 * n - 2, b):
                    body(r, r % 2, sect, sect, sect if r < b - 1 else nxt, (r - a) // 2)

        @block.sync
        def _(sp):
            def wait_stage_slot(n):
                sp.wait_ge(stage_hi, n - 1)
                sp.sem_inc(sp_passed, 1)
                sp.wait_ge(stage_lo, lows(n - 1))

            def load_stage(slot, src):
                sp.dma_start(stage[:, slot, :], src).then_inc(stage_in[slot], 16)

            xv = x.rearrange("b s d -> s b d")

            def load_x(q):
                sp.dma_start(xs[:, 8 * q:8 * q + 8, :], xv[:, 8 * q:8 * q + 8, :]).then_inc(x_in[q], 16)

            cv = ctxT.rearrange("(c p) t -> p c t", p=P)

            def load_ctx(i, p):
                sp.dma_start(cf[p].rearrange("p c b t -> p c (b t)"),
                             cv[:, :, bass.ds(i * (2 * S), 2 * S)]).then_inc(ctx_in[p], 16)

            def front_src(k):
                if k < 2:
                    return attw[k]
                return (bias_q if k < 4 else bias_t)[k % 2]

            load_x(0)
            load_stage(0, front_src(0))
            load_stage(1, front_src(1))
            load_ctx(0, 0)
            load_ctx(1, 1)
            sp.wait_ge(setup_dve, 1)
            sp.dma_start(m_scr, mrow16[0:B, :]).then_inc(mask_out, 16)

            def parts_out(i, p):
                for scr, parts, ready, sent in ((k_scr, kp, kl_ready, k_out), (q_scr, qp, ql_ready, q_out)):
                    sp.wait_ge(ready, 2 * i + 2)
                    sp.dma_start(scr[p].rearrange("s (c p) t -> p s c t", p=P), parts).then_inc(sent, 16)

            def stack(i, p):
                if before(i, 2):
                    sp.wait_ge(st_mm, 8 * i - 8)
                for scr, dst, sent, arrived, order in ((k_scr, KS[p], k_out, ks_in[p], (0, 1, 0)),
                                                       (q_scr, QS[p], q_out, qs_in[p], (0, 0, 1))):
                    sp.wait_ge(sent, 16 * i + 16)
                    for j, part in enumerate(order):
                        sp.dma_start(dst[HD * j:HD * j + HD],
                                     scr[p, part].rearrange("(h d) t -> d h t", d=HD)).then_inc(arrived, 16)
                row = m_scr[bass.ds(2 * i, 2), :].rearrange("b t -> (b t)").partition_broadcast(NH)
                sp.dma_start(KS[p][ROW_MASK:ROW_MASK + 1], row.unsqueeze(0)).then_inc(ks_in[p], 16)

            def max_row(i, p, b):
                sp.wait_ge(mrow_ready, 2 * i + b + 1)
                sp.dma_start(QS[p][ROW_MAX:ROW_MAX + 1, :, b * S:b * S + S], mrow[0:NH, b, :]).then_inc(m_in[b], 16)

            for k in (2, 3):
                wait_stage_slot(k)
                load_stage(k % 2, front_src(k))
                load_x(k - 1)
            load_x(3)
            parts_out(0, 0)
            wait_stage_slot(4)
            load_stage(0, front_src(4))
            sp.wait_ge(zeroed, 5)
            sp.wait_ge(const_rows, 2)
            sp.wait_ge(mask_out, 16)
            stack(0, 0)
            wait_stage_slot(5)
            load_stage(1, front_src(5))
            max_row(0, 0, 0)

            def body(i, p, k):
                if upto(i, NPAIR - 3):
                    sp.wait_ge(ch_ready, i + 1)
                    sp.wait_ge(cl_ready, i + 1)
                    load_ctx(i + 2, p)
                if upto(i, NPAIR - 2):
                    parts_out(i + 1, 1 - p)
                    stack(i + 1, 1 - p)
                max_row(i, p, 1)
                wait_stage_slot(FRONT + i)
                load_stage(p, wall[bass.ds(i, 1)].rearrange("a p n -> (a p) n"))
                if upto(i, NPAIR - 2):
                    max_row(i + 1, 1 - p, 0)

            pair_loop(sp, body)

            for w in range(ATT_CHUNKS, NCHUNK):
                wait_stage_slot(FRONT + w)
                load_stage(w % 2, wall[w])

            for s in range(4):
                sp.wait_ge(scattered[s], 8 * B)

            def load_rows(t, p):
                sp.wait_ge(tr_mm, t + RE - 1)
                sp.dma_start(rows[p], xsv[bass.ds(t, 1)].rearrange("a p w d -> (a p) w d")).then_inc(rows_in[p], 16)

            with sp.Fori(0, SLOT_TILES // 2) as k:
                load_rows(2 * k, 0)
                load_rows(2 * k + 1, 1)
            load_rows(SLOT_TILES - 1, 0)

            def store_out(n, j):
                sp.wait_ge(comb_b, n + 1)
                sp.dma_start(out[bass.ds(j, 1)].rearrange("a s d -> (a s) d"), xs[:, bass.ds(j, 1), :].rearrange("p a d -> p (a d)")).then_inc(res_out, 16)

            store_out(0, 0)
            store_out(1, 1)
            with sp.Fori(1, HALF) as m:
                for n in range(4):
                    store_out(4 * m - 2 + n, 2 * m + (n if n < 2 else n - 4 + B // 2))
            store_out(B - 2, B - 2)
            store_out(B - 1, B - 1)
            sp.wait_ge(res_out, 16 * B)

        @block.gpsimd
        def _(pool):
            nc.gpsimd.memset(ident[:, :], 0.0).then_inc(idents, 1)
            nc.gpsimd.memset(ident16[:, :], 0.0).then_inc(idents, 1)
            pool.wait_ge(idents, 2)
            nc.gpsimd.affine_select(out=ident[:, :], in_=ident[:, :], compare_op=ALU.not_equal, fill=1.0,
                                    base=0, pattern=[[-1, P]], channel_multiplier=1).then_inc(idents, 1)
            nc.gpsimd.affine_select(out=ident16[:, :], in_=ident16[:, :], compare_op=ALU.not_equal, fill=1.0,
                                    base=0, pattern=[[-1, P]], channel_multiplier=1).then_inc(idents, 1)
            for t in KS:
                nc.gpsimd.memset(flat(t), 1.0).then_inc(const_rows, 1)
            for t, value in zip(vh + vl, (1.0, 1.0, 0.0, 0.0)):
                nc.gpsimd.memset(t.rearrange("p b h e -> p (b h e)"), value).then_inc(const_rows, 1)
            nc.gpsimd.memset(mean_of, 1.0 / P).then_inc(const_rows, 1)
            def context_low(i, p):
                pool.wait_ge(ch_ready, i + 1)
                if before(i, 1):
                    pool.wait_ge(v_mm, i)
                nc.gpsimd.tensor_tensor(cl.rearrange("p c b t -> p (c b t)"), cf[p].rearrange("p c b t -> p (c b t)"),
                                        ch.rearrange("p c b t -> p (c b t)"), ALU.subtract).then_inc(cl_ready, 1)

            for k in range(FRONT):
                hi, lo = front_parts(k)
                if lo is not None:
                    pool_low(pool, k + 1, k % 2, hi, lo)
                if k == 1:
                    context_low(0, 0)
                if k == 3:
                    context_low(1, 1)

            def add_output_bias(i):
                pool.wait_ge(xn_ready, 2 * i + 2)
                for b in range(2):
                    xb = xs[:, bass.ds(2 * i + b, 1), :].rearrange("p a d -> p (a d)")
                    nc.gpsimd.tensor_tensor(xb, xb, obr, ALU.add).then_inc(xb_ready, 1)

            pool.wait_ge(setup_dve, 5)
            zv = xslots.rearrange("(n p r) d -> n p r d", p=P, r=ZERO_ROWS)
            pool.wait_ge(zeroed, 1)

            def prob_low(i, n):
                pool.wait_ge(prob_ready, 8 * i + n + 1)
                nc.gpsimd.tensor_tensor(flat(prob_lo[n % 4]), flat(prob[n % 4]), words_high(flat(prob[n % 4])),
                                        ALU.subtract).then_inc(prob_lo_pool, 1)

            add_output_bias(0)

            def body(i, p, k):
                if upto(i, NPAIR - 2):
                    add_output_bias(i + 1)
                prob_low(i, 1)
                prob_low(i, 3)
                prob_low(i, 5)
                if upto(i, NPAIR - 3):
                    context_low(i + 2, p)
                prob_low(i, 7)
                hi, lo = weight_parts(i)
                pool_low(pool, FRONT + i + 1, p, hi, lo)
                pool.dma_start(zv[bass.ds(i, 1)].rearrange("n p r d -> (n p) r d"),
                               zeros[:, :].unsqueeze(1).to_broadcast([P, ZERO_ROWS, D])).then_inc(zero_out, 16)

            pair_loop(pool, body)

            pool.wait_ge(x1_ready, B)
            nc.gpsimd.memset(tri, 1.0).then_inc(route_const, 1)
            nc.gpsimd.memset(ones, 1.0).then_inc(route_const, 1)
            nc.gpsimd.iota(iota_e, [[1, E]], base=0, channel_multiplier=0,
                           allow_small_or_imprecise_dtypes=True).then_inc(route_const, 1)
            nc.gpsimd.iota(iota_t, [[1, SLOT_SPACE]], base=0, channel_multiplier=0,
                           allow_small_or_imprecise_dtypes=True).then_inc(route_const, 1)
            pool.wait_ge(route_const, 4)
            nc.gpsimd.affine_select(out=tri, in_=tri, compare_op=ALU.is_gt, fill=0.0, base=0,
                                    pattern=[[1, P]], channel_multiplier=-1).then_inc(route_const, 1)
            pool.wait_ge(route, SLOT_STEP)
            pool.wait_ge(zero_out, 16 * NPAIR)

            def indices(n, j, p, users, used):
                if used is not None:
                    pool.wait_ge(users[p], used)
                nc.gpsimd.tensor_copy(slot_idx[p], slots[:, :, bass.ds(j, 1)].rearrange("p s a -> p (s a)"))\
                    .then_inc(idx_ready, 1)
                pool.wait_ge(idx_ready, n + 1)
                pool.sem_inc(pool_passed, 1)

            def scatter(j, p, used):
                pool.wait_ge(srow_made, j + 1)
                indices(j, j, p, scattered, used)
                for s in range(2):
                    nc.gpsimd.indirect_dma_start(
                        xslots, bass.IndirectOffsetOnAxis(ap=slot_idx[p][:, s:s + 1], axis=0),
                        srow[p], None).then_inc(scattered[p], 16)

            def late_chunk(m, p):
                hi, lo = weight_parts(m + ATT_CHUNKS)
                pool_low(pool, m + (FRONT + ATT_CHUNKS + 1), p, hi, lo)

            def turn(k, used, chunks=True):
                for n in range(4):
                    scatter(4 * k + n, n, used)
                for n in range(2 if chunks else 0):
                    late_chunk(2 * k + n, n)

            turn(0, None)
            with pool.Fori(1, LATE_CHUNKS // 2) as k:
                turn(k, 32 * k)
            for k in range(LATE_CHUNKS // 2, B // 4):
                turn(k, 32 * k, False)
            for s in range(2):
                pool.wait_ge(y_out[s], 16 + 16 * ((SLOT_TILES + 1 - s) // 2))

            def gather(n, j, b, uses):
                if known(uses) and uses < 1:
                    indices(B + n, j, b, scattered, 8 * B)
                else:
                    pool.wait_ge(comb_b, n - 3)
                    indices(B + n, j, b, gathered, 32 * uses)
                for s in range(2):
                    nc.gpsimd.indirect_dma_start(
                        yg[b][:, s, :], None, yslots,
                        bass.IndirectOffsetOnAxis(ap=slot_idx[b][:, s:s + 1], axis=0)).then_inc(gathered[b], 16)

            def gather_turn(m):
                for n in range(4):
                    gather(4 * m - 2 + n, 2 * m + (n if n < 2 else n - 4 + B // 2), (n + 2) % 4, m - 1 + (n + 2) // 4)

            gather(0, 0, 0, 0)
            gather(1, 1, 1, 0)
            gather_turn(1)
            with pool.Fori(2, HALF) as m:
                gather_turn(m)
            gather(B - 2, B - 2, 2, B // 4 - 1)
            gather(B - 1, B - 1, 3, B // 4 - 1)

        @block.scalar
        def _(act):
            for dst, src in ((graw[:, 0:1], g_att.partition_broadcast(P)), (graw[:, 1:2], g_ffn.partition_broadcast(P)),
                             (mrow_raw[0:B, :], mask), (qkbias, qkb),
                             (vbr, vb.partition_broadcast(P)), (obr, ob.partition_broadcast(P)),
                             (rw_f[:, :, :], rw.rearrange("(c p) e -> p c e", p=P)), (ebr[:, :], eb.partition_broadcast(P))):
                act.dma_start(dst, src).then_inc(const_in, 16)
            def context_high(i, p, k):
                act.wait_ge(ctx_in[p], 16 * (k + 1))
                if before(i, 1):
                    act.wait_ge(v_mm, i)
                nc.scalar.activation(ch.rearrange("p c b t -> p (c b t)"), cf[p].rearrange("p c b t -> p (c b t)"),
                                     ACT.Copy).then_inc(ch_ready, 1)

            def xn_high(i):
                act.wait_ge(xt_mm, i + 1)
                if before(i, 1):
                    act.wait_ge(q_mm, i)
                nc.scalar.activation(xnh, psT[:, :].rearrange("p (b c t) -> p c b t", b=2, c=C),
                                     ACT.Copy).then_inc(xh_ready, 1)

            def proj_high(i, ps, parts, col, mm, sent, ready):
                act.wait_ge(mm, i + 1)
                if before(i, 1):
                    act.wait_ge(sent, 16 * i)
                for m in range(C):
                    nc.scalar.activation(parts[:, 0, m, :], ps[:, bass.ts(m, 2 * S)], ACT.Identity,
                                         bias=qkbias[:, col + m:col + m + 1]).then_inc(ready, 1)

            def qk_high(i):
                proj_high(i, psK, kp, 2, k_mm, k_out, kh_ready)
                proj_high(i, psQ, qp, 0, q_mm, q_out, qh_ready)

            def v_high(i, p):
                act.wait_ge(v_mm, i + 1)
                act.wait_ge(const_rows, 7)
                if before(i, 2):
                    act.wait_ge(pv_mm, 8 * i - 8)
                nc.scalar.activation(vh[p][:, :, :, 0:HD], psQ[:, :].rearrange("p (b h e) -> p b h e", b=2, h=NH),
                                     ACT.Copy).then_inc(vh_ready, 1)

            def max_row(i, b):
                act.wait_ge(m_mm, 2 * i + b + 1)
                if before(i, 1):
                    act.wait_ge(m_in[b], 16 * i)
                nc.scalar.activation(mrow[0:NH, b, :], psT[0:NH, 0:S], ACT.Copy, scale=-1.0).then_inc(mrow_ready, 1)

            def out_high(i):
                act.wait_ge(ot_mm, i + 1)
                if before(i, 1):
                    act.wait_ge(o_mm, i)
                nc.scalar.activation(flat(onh), psT[:, :], ACT.Copy).then_inc(onh_ready, 1)

            def take_roots(n, at, count):
                act.wait_ge(ln_var, n)
                nc.scalar.activation(std[:, at:at + count], var_eps[:, at:at + count], ACT.Sqrt).then_inc(ln_std, 1)

            def normalise(i, group):
                act.wait_ge(ln_ready, group)
                if before(i, 1):
                    act.wait_ge(xt_mm, i)
                for b in range(2):
                    nc.scalar.activation(xn[:, b, :], xs[:, bass.ds(2 * i + b, 1), :].rearrange("p a d -> p (a d)"),
                                         ACT.Identity, bias=nmr[:, bass.ds(2 * i + b, 1)],
                                         scale=rstd[:, bass.ds(2 * i + b, 1)]).then_inc(xn_ready, 1)

            for k in range(FRONT):
                hi, lo = front_parts(k)
                if k == 0:
                    take_roots(1, *LN_GROUPS[0])
                    act.wait_ge(q_scaled, 1)
                act_high(act, 16 * (k // 2 + 1), k % 2, hi)
                if k == 0:
                    normalise(0, 1)
                if k == 1:
                    act.wait_ge(const_in, 16 * CONSTS)
                    nc.scalar.activation(rwh[:, :, :], rw_f[:, :, :], ACT.Copy).then_inc(setup_act, 1)
                    context_high(0, 0, 0)
                    xn_high(0)
                    normalise(1, 1)
                    qk_high(0)
                if k == 3:
                    v_high(0, 0)
                    context_high(1, 1, 0)
                    xn_high(1)
                    take_roots(2, *LN_GROUPS[1])
                    qk_high(1)
            max_row(0, 0)
            nc.scalar.activation(gates[:, :], graw[:, :], ACT.Tanh).then_inc(setup_act, 1)

            def body(i, p, k):
                def exponentials(ns):
                    for n in ns:
                        act.wait_ge(st_mm, 8 * i + n + 1)
                        if before(i, 1) or n >= 4:
                            act.wait_ge(pv_mm, 8 * i + n - 3)
                        nc.scalar.activation(flat(prob[n % 4]), pb[6 + n % 2][:, :], ACT.Exp).then_inc(prob_ready, 1)

                exponentials((0, 1))
                if before(i, 1):
                    out_high(i - 1)
                exponentials((2, 3))
                max_row(i, 1)
                if upto(i, NPAIR - 3):
                    normalise(i + 2, 1 if not before(i, 2) else 2)
                if upto(i, NPAIR - 2):
                    v_high(i + 1, 1 - p)
                if upto(i, NPAIR - 3):
                    xn_high(i + 2)
                exponentials((4,))
                if upto(i, NPAIR - 3):
                    context_high(i + 2, p, k + 1)
                exponentials((5,))
                exponentials((6, 7))
                if upto(i, NPAIR - 2):
                    max_row(i + 1, 0)
                act_high(act, 16 * (FRONT // 2 + k + 1), p, weight_parts(i)[0])
                if upto(i, NPAIR - 3):
                    qk_high(i + 2)

            pair_loop(act, body)
            out_high(NPAIR - 1)
            act.wait_ge(x1_ready, B)


            def split_high(r, p, sect=None):
                act.wait_ge(tr_mm, r + 1)
                if not (known(r) and r < 2):
                    if (sect or section(r - 2)) == "R":
                        act.wait_ge(router_mm, r - 1)
                    else:
                        act.wait_ge(h3_mm, last_unit(r - 2, sect) + 1)
                nc.scalar.activation(flat(xh[p]), pb[7 * p][:, :], ACT.Copy).then_inc(th_ready, 1)

            def write_rows(r, p):
                if not (known(r) and r < 2):
                    act.wait_ge(tr_mm, r - 1)
                j = bass.ds(2 * r, 1)
                nc.scalar.activation(rows[p][:, 0, :], xs[:, j, :].rearrange("p a d -> p (a d)"), ACT.Identity,
                                     bias=nmr[:, j], scale=rstd[:, j]).then_inc(router_rows, 1)

            take_roots(3, 0, B)
            act.wait_ge(ln_ready, 3)
            write_rows(0, 0)
            write_rows(1, 1)
            split_high(0, 0)
            def rows_and_parts(k):
                write_rows(2 * k, 0)
                split_high(2 * k - 1, 1, "R")
                write_rows(2 * k + 1, 1)
                split_high(2 * k, 0, "R")

            rows_and_parts(1)
            with act.Fori(2, NPAIR // 2) as k:
                rows_and_parts(k)
            split_high(NPAIR - 1, 1)
            split_high(R1, 0)
            act.wait_ge(route, EXP_STEP)
            nc.scalar.activation(sm[:, 5, :], sm[:, 4, :], ACT.Exp).then_inc(exp_ready, 1)

            for n in range(2):
                act.sem_inc(y_out[n], 16)

            def copy_y(t, p, k):
                act.wait_ge(y_mm, 2 * t + (UE + 2))
                act.wait_ge(y_out[p], 16 * k + 16)
                nc.scalar.activation(flat(ysb[p]), pb[1 + 5 * p][:, :], ACT.Copy).then_inc(y_copied, 1)
                act.wait_ge(y_copied, t + 1)
                act.dma_start(ysv[bass.ds(t, 1)].rearrange("a p w d -> (a p) w d"), ysb[p]).then_inc(y_out[p], 16)

            def body(r, p, sect, prev, nxt, k):
                for u, j, last in steps(r, sect):
                    if last and nxt is not None:
                        split_high(r + 1, 1 - p, None if known(r) else sect)
                    act.wait_ge(h1_mm, u + 1)
                    if not (known(u) and u < 2):
                        act.wait_ge(hid_ready, u - 1)
                    nc.scalar.activation(sil[j % 2], pb[2 + 2 * (j % 2)][:, :], ACT.Silu).then_inc(sil_ready, 1)
                    if sect == "1" and j < 2 and not (known(r) and r - R1 >= LATE_CHUNKS // 2):
                        act_high(act, 16 * ((FRONT + ATT_CHUNKS) // 2 + p + 1) + 32 * k, j,
                                 weight_parts(2 * r + (ATT_CHUNKS - 2 * R1 + j))[0])
                    if j == 0 and prev == "E":
                        copy_y(r - 1 - RE, 1 - p, (r - 1 - RE) // 2 if known(r) else k if p else k - 1)

            moe_loop(act, body)

        @block.tensor
        def _(pe):
            mm = nc.tensor.matmul

            def transpose_xn(i):
                pe.wait_ge(xn_ready, 2 * i + 2)
                if before(i, 2):
                    pe.wait_ge(mrow_ready, 2 * i - 2)
                elif i == 1:
                    pe.wait_ge(xl_ready, 1)
                for b in range(2):
                    for c in range(C):
                        k = b * C + c
                        last = nc.tensor.transpose(psT[:, bass.ts(k, P)], xn[:, b, bass.ts(c, P)], ident[:, :])
                last.then_inc(xt_mm, 1)

            def project_qk(ps, j, act_h, act_l, done):
                for m in range(C):
                    for c in range(C):
                        for w, a in ((awh, act_h), (awh, act_l), (awl, act_h)):
                            last = mm(ps[:, bass.ts(m, 2 * S)], w[:, j, c, bass.ts(m, P)],
                                      a[:, c].rearrange("p b t -> p (b t)"),
                                      start=(c == 0 and w is awh and a is act_h),
                                      stop=(c == C - 1 and w is awl))
                last.then_inc(done, 1)

            def project_q(i):
                pe.wait_ge(xl_ready, i + 1)
                if before(i, 1):
                    pe.wait_ge(vl_ready, i)
                project_qk(psQ, 0, xnh, xnl, q_mm)

            def project_k(i):
                pe.wait_ge(cl_ready, i + 1)
                if before(i, 3):
                    pe.wait_ge(x1_ready, 2 * i - 4)
                project_qk(psK, 1, ch, cl, k_mm)

            def project_v(i):
                pe.wait_ge(ql_ready, 2 * i + 2)
                for b in range(2):
                    o = psQ[:, bass.ts(b, D)]
                    mm(o, mean_of, vbh, start=True, stop=False)
                    mm(o, mean_of, vbl, start=False, stop=False)
                    for c in range(C):
                        for a, w in ((ch, awh), (cl, awh), (ch, awl)):
                            last = mm(o, a[:, c, b, :], w[:, 2, c, :], start=False, stop=(c == C - 1 and w is awl))
                last.then_inc(v_mm, 1)

            def scores(i, p, b, k, half):
                n = 4 * b + k
                bank = pb[4 + n % 2]
                if n == 0:
                    pe.wait_ge(qs_in[p], 48 * (half + 1))
                    pe.wait_ge(ks_in[p], 64 * (half + 1))
                if before(i, 1) or n >= 2:
                    pe.wait_ge(mx_ready, 8 * i + n - 1)
                mm(bank[:, :], ident16[:, :], bq_f[:, bass.ts(k, 512)], start=True, stop=False,
                   skip_group_check=True)
                for h in range(QUAD):
                    last = mm(bank[:, bass.ts(h, S)], QS[p][0:ROW_MAX, QUAD * k + h, bass.ts(b, S)],
                              KS[p][0:ROW_MAX, QUAD * k + h, bass.ts(b, S)], start=False, stop=True,
                              skip_group_check=True)
                last.then_inc(s_mm, 1)

            def transpose_max(i, b):
                pe.wait_ge(mclamp_ready, 2 * i + b + 1)
                if b == 0:
                    pe.wait_ge(xl_ready, min(i + 2, NPAIR) if known(i) else i + 2)
                elif before(i, 1):
                    pe.wait_ge(onl_ready, i)
                if before(i, 1) or b:
                    pe.wait_ge(mrow_ready, 2 * i + b)
                nc.tensor.transpose(psT[0:NH, 0:S], mclamp[:, b, :], ident[:, :]).then_inc(m_mm, 1)

            def scores_t(i, p, n):
                b, k = n // 4, n % 4
                bank = pb[6 + n % 2]
                if k == 0:
                    pe.wait_ge(m_in[b], 16 * i + 16)
                if before(i, 1) or n >= 2:
                    pe.wait_ge(prob_ready, 8 * i + n - 1)
                mm(bank[:, :], ident16[:, :], bth_f[:, bass.ts(k, 512)], start=True, stop=False,
                   skip_group_check=True)
                mm(bank[:, :], ident16[:, :], btl_f[:, bass.ts(k, 512)], start=False, stop=False,
                   skip_group_check=True)
                for h in range(QUAD):
                    last = mm(bank[:, bass.ts(h, S)], KS[p][0:ROW_MAX + 1, QUAD * k + h, bass.ts(b, S)],
                              QS[p][0:ROW_MAX + 1, QUAD * k + h, bass.ts(b, S)], start=False, stop=True,
                              skip_group_check=True)
                last.then_inc(st_mm, 1)

            def values(i, p, n):
                b, k = n // 4, n % 4
                if n == 0:
                    pe.wait_ge(vl_ready, i + 1)
                if k == 0 and (before(i, 1) or b):
                    pe.wait_ge(on_ready, 2 * i + b)
                pe.wait_ge(prob_lo_pool if k % 2 else prob_lo_ready, 4 * i + 2 * b + k // 2 + 1)
                hi = words_high(flat(prob[n % 4]))
                for h in range(QUAD):
                    hh = QUAD * k + h
                    o = psC[:, hh * (HD + 1):(hh + 1) * (HD + 1)]
                    mm(o, hi[:, bass.ts(h, S)], vh[p][:, b, hh, :], start=True, stop=False)
                    mm(o, hi[:, bass.ts(h, S)], vl[p][:, b, hh, :], start=False, stop=False)
                    last = mm(o, prob_lo[n % 4][:, h, :], vh[p][:, b, hh, :], start=False, stop=True)
                last.then_inc(pv_mm, 1)

            def transpose_out(i):
                pe.wait_ge(on_ready, 2 * i + 2)
                pe.wait_ge(mrow_ready, min(2 * i + 3, 2 * NPAIR) if known(i) else 2 * i + 3)
                for k in range(2 * C):
                    last = nc.tensor.transpose(psT[:, bass.ts(k, P)], on.rearrange("p b d -> p (b d)")[:, bass.ts(k, P)],
                                               ident[:, :])
                last.then_inc(ot_mm, 1)

            def project_out(i):
                pe.wait_ge(onl_ready, i + 1)
                pe.wait_ge(kl_ready, min(2 * i + 6, 2 * NPAIR) if known(i) else 2 * i + 6)
                for b in range(2):
                    for c in range(C):
                        for a, w in ((onh, awh), (onl, awh), (onh, awl)):
                            last = mm(psK[:, bass.ts(b, D)], a[:, b * C + c, :], w[:, 3, c, :],
                                      start=(c == 0 and a is onh and w is awh),
                                      stop=(c == C - 1 and w is awl))
                last.then_inc(o_mm, 1)

            pe.wait_ge(idents, 4)
            transpose_xn(0)
            pe.wait_ge(stage_hi, 1)
            pe.wait_ge(stage_lo, 1)
            project_q(0)
            project_k(0)
            pe.wait_ge(stage_hi, 2)
            pe.wait_ge(stage_lo, 2)
            pe.wait_ge(setup_dve, 4)
            pe.wait_ge(const_rows, 7)
            project_v(0)
            transpose_xn(1)
            project_q(1)
            project_k(1)
            pe.wait_ge(stage_hi, 4)
            for k in range(NQ):
                scores(0, 0, 0, k, 0)
            transpose_max(0, 0)
            for k in range(2):
                scores(0, 0, 1, k, 0)
            pe.wait_ge(stage_hi, FRONT)
            pe.wait_ge(stage_lo, lows(FRONT))

            def body(i, p, k):
                scores_t(i, p, 0)
                scores(i, p, 1, 2, k)
                scores_t(i, p, 1)
                if before(i, 1):
                    transpose_out(i - 1)
                values(i, p, 0)
                scores(i, p, 1, 3, k)
                scores_t(i, p, 2)
                values(i, p, 1)
                scores_t(i, p, 3)
                values(i, p, 2)
                transpose_max(i, 1)
                if before(i, 1):
                    project_out(i - 1)
                values(i, p, 3)
                if upto(i, NPAIR - 2):
                    project_v(i + 1)
                if upto(i, NPAIR - 3):
                    transpose_xn(i + 2)
                more = upto(i, NPAIR - 2)

                def next_scores(quad):
                    if more:
                        scores(i + 1, 1 - p, 0, quad, k + p)

                next_scores(0)
                next_scores(1)
                scores_t(i, p, 4)
                next_scores(2)
                scores_t(i, p, 5)
                values(i, p, 4)
                next_scores(3)
                scores_t(i, p, 6)
                values(i, p, 5)
                scores_t(i, p, 7)
                values(i, p, 6)
                if more:
                    transpose_max(i + 1, 0)
                if upto(i, NPAIR - 3):
                    project_k(i + 2)
                if more:
                    scores(i + 1, 1 - p, 1, 0, k + p)
                values(i, p, 7)
                if more:
                    scores(i + 1, 1 - p, 1, 1, k + p)
                if upto(i, NPAIR - 3):
                    project_q(i + 2)

            pair_loop(pe, body)
            transpose_out(NPAIR - 1)
            project_out(NPAIR - 1)
            pe.wait_ge(x1_ready, B)

            def transpose_rows(r, p, sect, half):
                if sect == "E":
                    pe.wait_ge(rows_in[p], 16 * (half + 1))
                elif sect == "R":
                    pe.wait_ge(router_rows, r + 1)
                    pe.wait_ge(router_rows2, r + 1)
                else:
                    pe.wait_ge(rows_made, 2 * r + 2 * (1 - R1 if sect == "1" else 1 - R2 + HALF))
                if not (known(r) and r < 2):
                    pe.wait_ge(tl_ready, r - 1)
                for c in range(C):
                    for t in range(2):
                        last = nc.tensor.transpose(pb[7 * p][:, bass.ts(2 * c + t, P)], rows[p][:, t, bass.ts(c, P)],
                                                   ident[:, :])
                last.then_inc(tr_mm, 1)

            def router(r, p):
                pe.wait_ge(tl_ready, r + 1)
                if not (known(r) and r < 2):
                    pe.wait_ge(logit_ready, r - 1)
                for t in range(2):
                    for c in range(C):
                        for a, w in ((xh[p], rwh), (xl[p], rwh), (xh[p], rwl)):
                            last = mm(pb[2 + p][:, bass.ts(t, E)], a[:, c, bass.ts(t, P)], w[:, c, :],
                                      start=(c == 0 and a is xh[p] and w is rwh), stop=(c == C - 1 and w is rwl))
                last.then_inc(router_mm, 1)

            transpose_rows(0, 0, "R", 0)
            transpose_rows(1, 1, "R", 0)
            router(0, 0)
            def tiles_of_router(k):
                transpose_rows(2 * k, 0, "R", k)
                router(2 * k - 1, 1)
                transpose_rows(2 * k + 1, 1, "R", k)
                router(2 * k, 0)

            tiles_of_router(1)
            with pe.Fori(2, NPAIR // 2) as k:
                tiles_of_router(k)
            router(NPAIR - 1, 1)
            transpose_rows(R1, 0, "1", 0)

            def ranks():
                pe.wait_ge(route, PICK_STEP)
                pe.wait_ge(route_const, 5)
                mm(psR[:, 0:B * E], tri, flat(pick), start=True, stop=True)
                mm(psR[:, B * E:], ones, flat(pick), start=True, stop=True).then_inc(rank_mm, 1)

            def up(u, q, p, at, g):
                if not (known(u) and u < 2):
                    pe.wait_ge(hid_ready, u - 1)
                for j, done in ((0, h1_mm), (1, h3_mm)):
                    for m in range(2):
                        for c in range(C):
                            col = j * 2 * CHUNK + c * HID + (2 * g + m) * P
                            hi = wparts[:, bass.ds(at + col, P)]
                            lo = wparts[:, bass.ds(at + (col + CHUNK), P)]
                            o = pb[2 + 2 * q + j][:, bass.ts(m, W)]
                            mm(o, hi, xh[p][:, c, :], start=(c == 0), stop=False)
                            mm(o, hi, xl[p][:, c, :], start=False, stop=False)
                            last = mm(o, lo, xh[p][:, c, :], start=False, stop=(c == C - 1))
                    last.then_inc(done, 1)

            def down(u, q, p, at, g, first, last_unit):
                pe.wait_ge(hlo_ready, u + 1)
                hi = words_high(hid[q])
                for t in range(2):
                    o = pb[1 + 5 * p][:, bass.ts(t, D)]
                    for m in range(2):
                        col = 2 * 2 * CHUNK + (2 * g + m) * D
                        w_hi = wparts[:, bass.ds(at + col, D)]
                        w_lo = wparts[:, bass.ds(at + (col + CHUNK), D)]
                        rows_of = bass.ts(2 * m + t, P)
                        mm(o, hi[:, rows_of], w_hi, start=(first and t == 0 and m == 0), stop=False,
                           skip_group_check=True)
                        mm(o, hi[:, rows_of], w_lo, start=False, stop=False, skip_group_check=True)
                        last = mm(o, hlo[q][:, rows_of], w_hi, start=False, stop=(last_unit and m == 1),
                                  skip_group_check=True)
                last.then_inc(y_mm, 1)

            def wait_y_bank(r, sect=None):
                sect = sect or section(r - 2)
                if sect == "R":
                    if r == R1 + 1:
                        pe.wait_ge(route, RANK_STEP)
                elif sect == "E":
                    pe.wait_ge(y_copied, r - 1 - RE)
                else:
                    pe.wait_ge(y_added, r - 1 - R1 if sect == "1" else r - 1 - R2 + HALF)

            def experts_at(t, n):
                return nc.values_load_multi_w_load_instructions(
                    te[0:1, bass.ds(t, n)], engines=[mybir.EngineType.PE], min_val=3 * NSH * 2 * CHUNK,
                    max_val=3 * (NSH + E - 1) * 2 * CHUNK,
                    skip_runtime_bounds_check_because="DVE clamps the expert to E - 1 before it scales it")[1]

            shared2 = 3 * 2 * CHUNK
            at_of = {}

            def body(r, p, sect, prev, nxt, k):
                if sect == "E" and p == 0:
                    if known(k) and k < 1:
                        pe.wait_ge(route, ROUTE_STEPS)
                        pe.sem_inc(pe_passed, 1)
                        at_of[0], at_of[1] = experts_at(0, 2)
                    else:
                        at_of[-1], at_of[0], at_of[1] = experts_at(2 * k - 1, 3)
                for u, j, last in steps(r, sect):
                    at = at_of[p] if sect == "E" else j // 2 * shared2
                    if j == 0:
                        pe.wait_ge(tl_ready, r + 1)
                        if known(r) and r == R1:
                            pe.wait_ge(logit_ready, NPAIR)
                        if known(r) and r == RE:
                            pe.wait_ge(stage_hi, FRONT + NCHUNK)
                            pe.wait_ge(stage_lo, lows(FRONT + NCHUNK))
                    if last and nxt is not None:
                        transpose_rows(r + 1, 1 - p, nxt, 0 if nxt != sect else k + p)
                    up(u, j % 2, p, at, j % 2)
                    if known(u) and u == 0:
                        ranks()
                    if j == 1:
                        wait_y_bank(r, None if known(r) else sect)
                    if j:
                        down(u - 1, (j - 1) % 2, p, at_of[p] if sect == "E" else (j - 1) // 2 * shared2,
                             (j - 1) % 2, j == 1, False)
                    elif prev == "E":
                        at = at_of[0] if p else at_of[-1] if sect == "E" else at_of[1]
                        down(u - 1, 1, 1 - p, at, 1, False, True)
                    elif prev is not None:
                        down(u - 1, 1, 1 - p, shared2, 1, False, True)

            moe_loop(pe, body)
            down(UTOT - 1, 1, (RTOT - 1) % 2, shared2, 1, False, True)

        @block.vector
        def _(dve):
            V = nc.vector
            V.memset(zeros[:, :], 0.0).then_inc(zeroed, 1)
            def clear_stack(p):
                V.memset(flat(QS[p]).bitcast(F32), 0.0).then_inc(zeroed, 1)
                dve.wait_ge(zeroed, 2 * p + 2)
                V.memset(flat(QS[p])[ROW_MASK:ROW_MASK + 1, :].bitcast(F32), MASK_Q_TWICE).then_inc(zeroed, 1)

            clear_stack(0)
            ln_count = [0]

            def ln_link(*steps):
                for ins in steps:
                    ins.then_inc(ln_step, 1)
                ln_count[0] += len(steps)
                dve.wait_ge(ln_step, ln_count[0])

            def ln_variances(at, count):
                a = slice(at, at + count)
                mu, d, m2 = mean[:, a], ln_tmp[:, 0, a], ln_tmp[:, 1, a]
                ln_link(V.tensor_tensor(mu, stats[:, a, 1], stats[:, a, 4], ALU.add),
                        V.tensor_tensor(d, stats[:, a, 1], stats[:, a, 4], ALU.subtract),
                        V.tensor_tensor(m2, stats[:, a, 2], stats[:, a, 5], ALU.add))
                ln_link(V.tensor_scalar(mu, mu, 0.5, None, ALU.mult), V.tensor_tensor(d, d, d, ALU.mult))
                ln_link(V.scalar_tensor_tensor(out=m2, in0=d, scalar=D / 4, in1=m2, op0=ALU.mult, op1=ALU.add))
                V.tensor_scalar(var_eps[:, a], m2, 1.0 / D, EPS, ALU.mult, ALU.add).then_inc(ln_var, 1)

            def ln_scales(n, at, count):
                a = slice(at, at + count)
                dve.wait_ge(ln_std, n)
                ln_link(V.reciprocal(rstd[:, a], std[:, a]))
                V.scalar_tensor_tensor(out=nmr[:, a], in0=mean[:, a], scalar=-1.0, in1=rstd[:, a],
                                       op0=ALU.mult, op1=ALU.mult).then_inc(ln_ready, 1)

            def x_stats(q):
                dve.wait_ge(x_in[q], 16)
                for j in range(8 * q, 8 * q + 8):
                    V.bn_stats(stats[:, j, :], xs[:, j, :]).then_inc(stats_done, 1)

            x_stats(0)
            dve.wait_ge(stats_done, 8)
            ln_variances(*LN_GROUPS[0])
            dve.wait_ge(stage_in[0], 16)
            V.tensor_scalar(stage[:, 0, 0:C * D], stage[:, 0, 0:C * D], HD ** -0.5, None, ALU.mult).then_inc(q_scaled, 1)
            ln_scales(1, *LN_GROUPS[0])
            dve.wait_ge(const_in, 16 * CONSTS)
            V.tensor_scalar(mrow16[0:B, :], mrow_raw[0:B, :], MASK_K, None, ALU.mult).then_inc(setup_dve, 1)
            V.tensor_scalar(qkbias[:, 0:C], qkbias[:, 0:C], HD ** -0.5, None, ALU.mult).then_inc(setup_dve, 1)
            V.tensor_copy(vbh, vbr).then_inc(setup_dve, 1)
            dve.wait_ge(setup_dve, 3)
            V.tensor_tensor(vbl, vbr, vbh, ALU.subtract).then_inc(setup_dve, 1)

            def xn_low(i):
                dve.wait_ge(xh_ready, i + 1)
                V.tensor_tensor(xnl, psT[:, :].rearrange("p (b c t) -> p c b t", b=2, c=C), xnh,
                                ALU.subtract).then_inc(xl_ready, 1)

            def proj_low(i, ps, parts, col, high, ready):
                dve.wait_ge(high, 2 * i + 2)
                for m in range(C):
                    V.scalar_tensor_tensor(out=parts[:, 1, m, :], in0=ps[:, bass.ts(m, 2 * S)],
                                           scalar=qkbias[:, col + m:col + m + 1], in1=parts[:, 0, m, :],
                                           op0=ALU.add, op1=ALU.subtract).then_inc(ready, 1)

            def q_low(i):
                proj_low(i, psQ, qp, 0, qh_ready, ql_ready)

            def k_low(i):
                proj_low(i, psK, kp, 2, kh_ready, kl_ready)

            def v_low(i, p):
                dve.wait_ge(vh_ready, i + 1)
                V.tensor_tensor(vl[p][:, :, :, 0:HD], psQ[:, :].rearrange("p (b h e) -> p b h e", b=2, h=NH),
                                vh[p][:, :, :, 0:HD], ALU.subtract).then_inc(vl_ready, 1)

            def maxima(i, b, k):
                n = 4 * b + k
                dve.wait_ge(s_mm, 8 * i + n + 1)
                V.tensor_reduce(mx[:, b, bass.ts(k, QUAD)], pb[4 + n % 2][:, :].rearrange("p (h t) -> p h t", h=QUAD),
                                AX.X, ALU.max).then_inc(mx_ready, 1)

            def clamp(i, b):
                dve.wait_ge(mx_ready, 8 * i + 4 * b + 4)
                if before(i, 1):
                    dve.wait_ge(m_mm, 2 * i + b - 1)
                V.tensor_scalar(mclamp[:, b, :], mx[:, b, :], -MAX_CLAMP, MAX_CLAMP, ALU.max, ALU.min)\
                    .then_inc(mclamp_ready, 1)

            def prob_low(i, n):
                dve.wait_ge(prob_ready, 8 * i + n + 1)
                V.tensor_tensor(flat(prob_lo[n % 4]), flat(prob[n % 4]), words_high(flat(prob[n % 4])),
                                ALU.subtract).then_inc(prob_lo_ready, 1)

            def normalise_heads(i, b):
                dve.wait_ge(pv_mm, 8 * i + 4 * b + 4)
                o = psC[:, 0:NH * (HD + 1)].rearrange("p (h e) -> p h e", h=NH)
                V.tensor_scalar(den[:, b, :], o[:, :, HD], 1e-6, None, ALU.max).then_inc(den_ready, 1)
                dve.wait_ge(den_ready, 2 * i + b + 1)
                V.reciprocal(rden[:, b, :], den[:, b, :]).then_inc(rden_ready, 1)
                dve.wait_ge(rden_ready, 2 * i + b + 1)
                if before(i, 1):
                    dve.wait_ge(ot_mm, i)
                V.tensor_tensor(on[:, b, :].rearrange("p (h e) -> p h e", h=NH), o[:, :, 0:HD],
                                rden[:, b, :].unsqueeze(2).to_broadcast([P, NH, HD]), ALU.mult).then_inc(on_ready, 1)

            def out_low(i):
                dve.wait_ge(onh_ready, i + 1)
                V.tensor_tensor(flat(onl), psT[:, :], flat(onh), ALU.subtract).then_inc(onl_ready, 1)

            def residual(i):
                dve.wait_ge(o_mm, i + 1)
                dve.wait_ge(xb_ready, 2 * i + 2)
                for b in range(2):
                    xb = xs[:, bass.ds(2 * i + b, 1), :].rearrange("p a d -> p (a d)")
                    V.scalar_tensor_tensor(out=xb, in0=psK[:, bass.ts(b, D)], scalar=gates[:, 0:1], in1=xb,
                                           op0=ALU.mult, op1=ALU.add).then_inc(x1_ready, 1)

            def x1_stats(i):
                for b in range(2):
                    dve.wait_ge(x1_ready, 2 * i + b + 1)
                    V.bn_stats(stats[:, bass.ds(2 * i + b, 1), :].rearrange("p a s -> p (a s)"),
                               xs[:, bass.ds(2 * i + b, 1), :].rearrange("p a d -> p (a d)")).then_inc(stats_done, 1)

            xn_low(0)
            clear_stack(1)
            q_low(0)
            k_low(0)
            x_stats(1)
            v_low(0, 0)
            xn_low(1)
            x_stats(2)
            x_stats(3)
            dve.wait_ge(stats_done, B)
            ln_variances(*LN_GROUPS[1])
            k_low(1)
            q_low(1)
            for k in range(NQ):
                maxima(0, 0, k)
            clamp(0, 0)
            for k in range(2):
                maxima(0, 1, k)
            ln_scales(2, *LN_GROUPS[1])
            dve.wait_ge(setup_act, 2)
            V.tensor_scalar(obr, obr, gates[:, 0:1], None, ALU.mult).then_inc(setup_dve, 1)
            V.tensor_tensor(rwl[:, :, :], rw_f[:, :, :], rwh[:, :, :], ALU.subtract).then_inc(setup_dve, 1)

            def body(i, p, k):
                if before(i, 1) and upto(i, NPAIR - 2):
                    q_low(i + 1)
                prob_low(i, 0)
                maxima(i, 1, 2)
                maxima(i, 1, 3)
                clamp(i, 1)
                if before(i, 1):
                    out_low(i - 1)
                prob_low(i, 2)
                if before(i, 1):
                    residual(i - 1)
                normalise_heads(i, 0)
                more = upto(i, NPAIR - 2)
                if more:
                    v_low(i + 1, 1 - p)
                    maxima(i + 1, 0, 0)
                    maxima(i + 1, 0, 1)
                prob_low(i, 4)
                if more:
                    maxima(i + 1, 0, 2)
                if upto(i, NPAIR - 3):
                    xn_low(i + 2)
                if more:
                    maxima(i + 1, 0, 3)
                    clamp(i + 1, 0)
                prob_low(i, 6)
                if before(i, 1):
                    x1_stats(i - 1)
                if more:
                    maxima(i + 1, 1, 0)
                normalise_heads(i, 1)
                if upto(i, NPAIR - 3):
                    k_low(i + 2)
                if more:
                    maxima(i + 1, 1, 1)

            pair_loop(dve, body)
            out_low(NPAIR - 1)
            residual(NPAIR - 1)
            x1_stats(NPAIR - 1)
            dve.wait_ge(x1_ready, B)

            def row(j):
                return xs[:, bass.ds(j, 1), :].rearrange("p a d -> p (a d)")

            def make_rows(dst, j, made):
                V.tensor_scalar(dst, row(j), mean[:, bass.ds(j, 1)], rstd[:, bass.ds(j, 1)],
                                ALU.subtract, ALU.mult).then_inc(made, 1)

            def split_low(r, p):
                dve.wait_ge(th_ready, r + 1)
                V.tensor_tensor(flat(xl[p]), pb[7 * p][:, :], flat(xh[p]), ALU.subtract).then_inc(tl_ready, 1)

            lg = rt[:, 0]

            def hidden(u, q):
                dve.wait_ge(h3_mm, u + 1)
                dve.wait_ge(sil_ready, u + 1)
                if not (known(u) and u < 2):
                    dve.wait_ge(y_mm, u - 1)
                V.tensor_tensor(hid[q], sil[q], pb[3 + 2 * q][:, :], ALU.mult).then_inc(hid_ready, 1)
                dve.wait_ge(hid_ready, u + 1)
                V.tensor_tensor(hlo[q], hid[q], words_high(hid[q]), ALU.subtract).then_inc(hlo_ready, 1)

            def logits(r, p):
                dve.wait_ge(router_mm, r + 1)
                V.tensor_tensor(lg[:, bass.ds(2 * r, 2), :], pb[2 + p][:, 0:2 * E].rearrange("p (t e) -> p t e", t=2),
                                ebr[:, :].unsqueeze(1).to_broadcast([P, 2, E]), ALU.add).then_inc(logit_ready, 1)

            def shared_rows(r, p, n):
                dve.wait_ge(tr_mm, r - 1)
                for t in range(2):
                    make_rows(rows[p][:, t, :], 2 * n + t, rows_made)

            dve.wait_ge(stats_done, 2 * B)
            ln_variances(0, B)
            ln_scales(3, 0, B)

            def router_rows_of(r, p):
                if not (known(r) and r < 2):
                    dve.wait_ge(tr_mm, r - 1)
                make_rows(rows[p][:, 1, :], 2 * r + 1, router_rows2)

            dve.wait_ge(ln_step, ln_count[0])
            dve.wait_ge(ln_ready, 3)
            router_rows_of(0, 0)
            router_rows_of(1, 1)
            with dve.Fori(0, NPAIR // 2 - 1) as k:
                for p in range(2):
                    split_low(2 * k + p, p)
                    router_rows_of(2 * k + (2 + p), p)
                    logits(2 * k + p, p)
            for p in range(2):
                split_low(NPAIR - 2 + p, p)
                logits(NPAIR - 2 + p, p)
            shared_rows(R1, 0, 0)
            split_low(R1, 0)
            shared_rows(R1 + 1, 1, 1)
            dve.wait_ge(logit_ready, NPAIR)
            dve.wait_ge(route_const, 5)

            step = [0]

            def link(ins):
                step[0] += 1
                ins.then_inc(route, 1)
                dve.wait_ge(route, step[0])
                return step[0]

            ie = iota_e.unsqueeze(1).to_broadcast([P, B, E])

            def over_e(a):
                return a.unsqueeze(2).to_broadcast([P, B, E])

            src = lg
            for k in range(2):
                best, sel = sm[:, 2 * k], sm[:, 2 * k + 1]
                ge, hot = rt[:, 1], rt[:, 2 + k]
                link(V.tensor_reduce(best, src, AX.X, ALU.max))
                link(V.tensor_tensor(ge, src, over_e(best), ALU.is_ge))
                link(V.scalar_tensor_tensor(out=ge, in0=ge, scalar=-float(E), in1=ie, op0=ALU.mult, op1=ALU.add))
                link(V.tensor_reduce(sel, ge, AX.X, ALU.min))
                link(V.tensor_scalar(sel, sel, float(E), None, ALU.add))
                link(V.tensor_tensor(hot, ie, over_e(sel), ALU.is_equal))
                if k == 0:
                    link(V.scalar_tensor_tensor(out=rt[:, 4], in0=hot, scalar=-3.0e38, in1=lg, op0=ALU.mult, op1=ALU.add))
                    src = rt[:, 4]
            assert link(V.tensor_tensor(pick, rt[:, 2], rt[:, 3], ALU.add)) == PICK_STEP
            assert link(V.tensor_tensor(sm[:, 4], sm[:, 2], sm[:, 0], ALU.subtract)) == EXP_STEP
            dve.wait_ge(rank_mm, 1)
            a, bb = rt[:, 5], rt[:, 6]
            tot = rt[:, 7]
            link(V.tensor_copy(flat(tot), psR[:, B * E:]))
            link(V.tensor_copy(flat(a), psR[:, B * E:]))
            sh = 1
            while sh < B:
                V.tensor_copy(bb[:, 0:sh, :], a[:, 0:sh, :]).then_inc(route, 1)
                step[0] += 1
                link(V.tensor_tensor(bb[:, sh:, :], a[:, sh:, :], a[:, 0:B - sh, :], ALU.add))
                a, bb = bb, a
                sh *= 2
            hidden(0, 0)
            hidden(1, 1)
            link(V.tensor_scalar(cnt[:, 0], a[:, B - 1, :], float(W - 1), None, ALU.add))
            link(V.tensor_tensor(a, a, tot, ALU.subtract))
            link(V.tensor_copy(cnt_i, cnt[:, 0]))
            link(V.tensor_scalar(cnt_i, cnt_i, W.bit_length() - 1, None, ALU.logical_shift_right))
            link(V.tensor_copy(cnt[:, 1], cnt_i))
            ca, cb = cnt[:, 1], cnt[:, 2]
            link(V.tensor_copy(cnt[:, 3], cnt[:, 1]))
            ca = cnt[:, 3]
            sh = 1
            while sh < E:
                V.tensor_copy(cb[:, 0:sh], ca[:, 0:sh]).then_inc(route, 1)
                step[0] += 1
                link(V.tensor_tensor(cb[:, sh:], ca[:, sh:], ca[:, 0:E - sh], ALU.add))
                ca, cb = cb, ca
                sh *= 2
            link(V.tensor_tensor(cnt[:, 4], ca, cnt[:, 1], ALU.subtract))
            link(V.tensor_scalar(cnt[:, 5], cnt[:, 4], float(W), None, ALU.mult))
            link(V.tensor_tensor(a, a, cnt[:, 5].unsqueeze(1).to_broadcast([P, B, E]), ALU.add))
            link(V.tensor_tensor(flat(a), flat(a), psR[:, 0:B * E], ALU.add))
            for k in range(2):
                link(V.tensor_tensor(rt[:, 8], rt[:, 2 + k], a, ALU.mult))
                link(V.tensor_reduce(sm[:, 6 + k], rt[:, 8], AX.X, ALU.add))
                link(V.tensor_copy(slots[:, k, :], sm[:, 6 + k]))
            assert step[0] == SLOT_STEP

            def tiles_and_gates():
                link(V.tensor_tensor(te_f, iota_t.unsqueeze(2).to_broadcast([P, SLOT_SPACE, E]),
                                     ca.unsqueeze(1).to_broadcast([P, SLOT_SPACE, E]), ALU.is_ge))
                link(V.tensor_reduce(te_s, te_f, AX.X, ALU.add))
                link(V.tensor_scalar(te_s, te_s, float(E - 1), float(NSH), ALU.min, ALU.add))
                link(V.tensor_scalar(te_s, te_s, float(3 * 2 * CHUNK), None, ALU.mult))
                assert link(V.tensor_copy(te, te_s)) == ROUTE_STEPS
                dve.wait_ge(exp_ready, 1)
                link(V.tensor_scalar(sm[:, 8], sm[:, 5], 1.0, None, ALU.add))
                link(V.reciprocal(sm[:, 9], sm[:, 8]))
                link(V.tensor_scalar(sm[:, 10], sm[:, 9], gates[:, 1:2], None, ALU.mult))
                link(V.tensor_tensor(sm[:, 11], sm[:, 10], sm[:, 5], ALU.mult))

            def scatter_rows(j, n, used):
                if used is not None:
                    dve.wait_ge(scattered[n], used)
                make_rows(srow[n], j, srow_made)

            def combine(n, j, p, uses):
                dve.wait_ge(gathered[p], 32 * (uses + 1))
                V.scalar_tensor_tensor(out=row(j), in0=yg[p][:, 0, :], scalar=sm[:, 10, bass.ds(j, 1)], in1=row(j),
                                       op0=ALU.mult, op1=ALU.add).then_inc(comb_a, 1)
                dve.wait_ge(comb_a, n + 1)
                V.scalar_tensor_tensor(out=row(j), in0=yg[p][:, 1, :], scalar=sm[:, 11, bass.ds(j, 1)], in1=row(j),
                                       op0=ALU.mult, op1=ALU.add).then_inc(comb_b, 1)

            def add_shared(n, p):
                both = xs[:, bass.ds(2 * n, 2), :]
                V.scalar_tensor_tensor(out=both, in0=pb[1 + 5 * p][:, :].rearrange("p (t d) -> p t d", t=2),
                                       scalar=gates[:, 1:2], in1=both, op0=ALU.mult, op1=ALU.add).then_inc(y_added, 1)

            for n in range(4):
                scatter_rows(n, n, None)

            def body(r, p, sect, prev, nxt, k):
                for u, j, last in steps(r, sect):
                    if last and nxt is not None:
                        split_low(r + 1, 1 - p)
                    if not (known(u) and u < 2):
                        hidden(u, j % 2)
                    if j == 0 and prev in ("1", "2"):
                        dve.wait_ge(y_mm, u)
                        add_shared(r - 1 - R1 if prev == "1" else r - 1 - R2 + HALF, 1 - p)
                    if known(u) and u == 2:
                        tiles_and_gates()
                    if known(r) and r == R1:
                        for n in (2 * j - 4, 2 * j - 3):
                            if n >= 0:
                                scatter_rows(4 + n, n, 32)
                    elif sect == "1" and not (known(r) and r == RE - 1):
                        scatter_rows(4 * r - (4 * R1 - 4 - j), j, 64 * k + (32 * p + 32))
                    if last and sect == "1" and not (known(r) and r + 2 >= RE):
                        shared_rows(r + 2, p, r + 2 - R1)
                    if last and sect == "E" and known(r) and r + 2 >= R2:
                        shared_rows(r + 2, p, r + 2 - R2 + HALF)
                    if last and sect == "2" and not (known(r) and r + 2 >= RTOT):
                        shared_rows(r + 2, p, r + 2 - R2 + HALF)
                    if sect == "2" and known(r) and r == R2:
                        if last:
                            combine(0, 0, 0, 0)
                            combine(1, 1, 1, 0)
                    elif sect == "2":
                        odd = (p + R2) % 2
                        if j == 2:
                            dve.wait_ge(y_added, 2 * k + (odd + HALF))
                        combine(8 * k + (4 * odd - 2 + j), 4 * k + (2 * odd + (j if j < 2 else j - 4 + B // 2)),
                                (j + 2) % 4, 2 * k + (odd - 1 + (j + 2) // 4))

            moe_loop(dve, body)
            dve.wait_ge(y_mm, UTOT)
            add_shared(NPAIR - 1, (RTOT - 1) % 2)
            dve.wait_ge(y_added, NPAIR)
            combine(B - 2, B - 2, 2, B // 4 - 1)
            combine(B - 1, B - 1, 3, B // 4 - 1)


def kernel(**inputs):
    import concourse.bacc as bacc
    from concourse.bass_utils import run_bass_kernel_spmd

    a = {k: np.asarray(v) for k, v in inputs.items()}
    con = np.ascontiguousarray

    def chunked(w):
        k, n = w.shape[-2:]
        w = w.reshape(*w.shape[:-2], k // P, P, n)
        return con(np.moveaxis(w, -2, -3)).reshape(*w.shape[:-3], P, (k // P) * n)

    def transposed(w):
        return np.swapaxes(w, -1, -2)

    aw = [chunked(transposed(a[f"L0_xattn_{k}_w"])) for k in "qkvo"]
    w1, w3, w2 = (np.concatenate([a[f"L0_ffn_s{k}"], a[f"L0_ffn_{k}"]]) for k in ("w1", "w3", "w2"))
    wall = np.stack([chunked(transposed(w)) for w in (w1, w3, w2)], axis=1).reshape(NCHUNK, P, CHUNK)
    fside = a["fside_1x16xSxS2_0"][0]

    def by_row(w):
        w = w.transpose(1, 0, 2).reshape(S, 2, CHUNK)
        return con(w.transpose(1, 0, 2))

    arrays = {
        "x": con(a["x"]),
        "ctxT": con(a["ctx_1024"].reshape(B * S, D).T),
        "bias_q": by_row(fside),
        "bias_t": by_row(transposed(fside)),
        "mask": con(a["mask_BxS2_bk0"]),
        "g_att": con(a["g_xattn"]),
        "g_ffn": con(a["g_ffn"]),
        "attw": con(np.stack([np.concatenate(aw[0:2], axis=1), np.concatenate(aw[2:4], axis=1)])),
        "qkb": con(np.stack([a["L0_xattn_q_b"], a["L0_xattn_k_b"]]).reshape(2 * C, P).T),
        "vb": con(a["L0_xattn_v_b"]),
        "ob": con(a["L0_xattn_o_b"]),
        "rw": con(a["L0_ffn_router_w"].T),
        "eb": con(a["L0_ffn_expert_bias"]),
        "wall": con(wall),
    }
    nc = bacc.Bacc("TRN2", target_bir_lowering=False, num_devices=1)
    args = {k: nc.dram_tensor(k, v.shape, mybir.dt.from_np(v.dtype), kind="ExternalInput").ap()
            for k, v in arrays.items()}
    args["out"] = nc.dram_tensor("out", (B, S, D), F32, kind="ExternalOutput").ap()
    build(nc, **args)
    return run_bass_kernel_spmd(nc, [arrays], core_ids=[0]).results[0]["out"]
```
